# Optimizing a Trainium2 kernel written in Bass

```python
import numpy as np
import jax
import jax.numpy as jnp

def _softmax(x, axis=-1):
    return jax.nn.softmax(x, axis=axis)

def _gelu(x):
    return jax.nn.gelu(x, approximate=True)

def _silu(x):
    return jax.nn.silu(x)

def _sigmoid(x):
    return jax.nn.sigmoid(x)

def _layernorm(x, axis=-1, eps=1e-05):
    m = jnp.mean(x, axis=axis, keepdims=True)
    v = jnp.var(x, axis=axis, keepdims=True)
    return (x - m) / jnp.sqrt(v + eps)

def _scatter_add(tgt, idx, src, axis=0):
    return tgt.at[idx].add(src)

def _segment_sum(src, seg, n):
    return jax.ops.segment_sum(src, seg, n)
kernel_name = 'mk_gnn_resnorm_d2_gnn_r64_693cf9'

def setup_inputs(seed: int=0):
    np.random.seed(seed)
    _w = jnp.asarray

    def _rec_inputs():
        import jax
        import jax.numpy as jnp
        _gk = jax.random.key(seed)
        x = -0.000202 + 1 * jax.random.normal(jax.random.fold_in(_gk, 1), (100000, 64), jnp.float32)
        src = jax.random.randint(jax.random.fold_in(_gk, 2), (50000,), 0, 100000, jnp.int32)
        dst = jnp.minimum((100000 * jax.random.uniform(jax.random.fold_in(_gk, 3), (50000,)) ** 2.0).astype(jnp.int32), 99999)
        _o = jnp.argsort(dst, stable=True)
        src = src[_o]
        dst = dst[_o]
        edge_type_64 = jax.random.randint(jax.random.fold_in(_gk, 13), (50000,), 0, 64, jnp.int32)
        edge_weight1 = jax.random.uniform(jax.random.fold_in(_gk, 14), (50000, 1), jnp.float32, 0.0, 0.999998)
        return (x, src, dst, edge_type_64, edge_weight1)
    x, src, dst, edge_type_64, edge_weight1 = _rec_inputs()

    def _L0_gnn_setup():
        import jax, jax.numpy as jnp
        import numpy as np
        N = 100000
        E = 25000
        D_IN = 64
        D_H = 64
        EPS = 1e-05

        def _sage_conv(x, src, dst, Wl, bl, Wr, n_nodes):
            msg = x[src]
            agg = jax.ops.segment_sum(msg, dst, num_segments=n_nodes)
            deg = jax.ops.segment_sum(jnp.ones((src.shape[0], 1), x.dtype), dst, num_segments=n_nodes)
            agg = agg / jnp.maximum(deg, 1.0)
            return agg @ Wl.T + bl + x @ Wr.T

        def _layer_norm(h, g, b):
            mu = jnp.mean(h, axis=-1, keepdims=True)
            var = jnp.mean(jnp.square(h - mu), axis=-1, keepdims=True)
            return (h - mu) * jax.lax.rsqrt(var + EPS) * g + b
        key = jax.random.key(seed)
        ks = jax.random.split(key, 12)
        x = jax.random.normal(ks[0], (N, D_IN), dtype=jnp.float32)
        edge_index = jax.random.randint(ks[1], (2, E), 0, N, dtype=jnp.int32)
        s1 = 1.0 / np.sqrt(D_IN)
        s2 = 1.0 / np.sqrt(D_H)
        return {'x': x, 'edge_index': edge_index, 'W1l': jax.random.uniform(ks[2], (D_H, D_IN), jnp.float32, -s1, s1), 'b1l': jnp.zeros((D_H,), jnp.float32), 'W1r': jax.random.uniform(ks[3], (D_H, D_IN), jnp.float32, -s1, s1), 'g1': jnp.ones((D_H,), jnp.float32), 'beta1': jnp.zeros((D_H,), jnp.float32), 'W2l': jax.random.uniform(ks[4], (D_H, D_H), jnp.float32, -s2, s2), 'b2l': jnp.zeros((D_H,), jnp.float32), 'W2r': jax.random.uniform(ks[5], (D_H, D_H), jnp.float32, -s2, s2), 'g2': jnp.ones((D_H,), jnp.float32), 'beta2': jnp.zeros((D_H,), jnp.float32)}
    _L0_gnn_all = _L0_gnn_setup()
    _L0_gnn_in = {k: v for k, v in _L0_gnn_all.items() if k in ('W1l', 'b1l', 'W1r', 'g1', 'beta1', 'W2l', 'b2l', 'W2r', 'g2', 'beta2')}
    del _L0_gnn_all

    def _L1_gnn_setup():
        import jax, jax.numpy as jnp
        import numpy as np
        N_NODES = 50000
        N_EDGES = 25000
        IN_F = 64
        OUT_F = 64
        NUM_RELS = 64
        NUM_BASES = 64
        BN_EPS = 1e-05
        key = jax.random.key(seed)
        ks = jax.random.split(key, 12)
        node_feats = jax.random.normal(ks[0], (N_NODES, IN_F), dtype=jnp.float32)
        src = jax.random.randint(ks[1], (N_EDGES,), 0, N_NODES, dtype=jnp.int32)
        dst = jax.random.randint(ks[2], (N_EDGES,), 0, N_NODES, dtype=jnp.int32)
        etype = jax.random.randint(ks[3], (N_EDGES,), 0, NUM_RELS, dtype=jnp.int32)
        norm = jax.random.uniform(ks[4], (N_EDGES, 1), dtype=jnp.float32)
        basis = jax.random.normal(ks[5], (NUM_BASES, IN_F, OUT_F), dtype=jnp.float32) * (1.0 / np.sqrt(IN_F))
        comp = jax.random.normal(ks[6], (NUM_RELS, NUM_BASES), dtype=jnp.float32) * (1.0 / np.sqrt(NUM_BASES))
        bias = jnp.zeros((OUT_F,), dtype=jnp.float32)
        res_w = jax.random.normal(ks[7], (OUT_F, IN_F), dtype=jnp.float32) * (1.0 / np.sqrt(IN_F))
        res_b = jnp.zeros((OUT_F,), dtype=jnp.float32)
        gamma = jnp.ones((OUT_F,), dtype=jnp.float32)
        beta = jnp.zeros((OUT_F,), dtype=jnp.float32)
        return {'node_feats': node_feats, 'src': src, 'dst': dst, 'etype': etype, 'norm': norm, 'basis': basis, 'comp': comp, 'bias': bias, 'res_w': res_w, 'res_b': res_b, 'gamma': gamma, 'beta': beta}
    _L1_gnn_all = _L1_gnn_setup()
    _L1_gnn_in = {k: v for k, v in _L1_gnn_all.items() if k in ('basis', 'comp', 'bias', 'res_w', 'res_b', 'gamma', 'beta')}
    del _L1_gnn_all
    return {'x': x, 'src': src, 'dst': dst, 'edge_type_64': edge_type_64, 'edge_weight1': edge_weight1, 'L0_gnn_W1l': _L0_gnn_in['W1l'], 'L0_gnn_b1l': _L0_gnn_in['b1l'], 'L0_gnn_W1r': _L0_gnn_in['W1r'], 'L0_gnn_g1': _L0_gnn_in['g1'], 'L0_gnn_beta1': _L0_gnn_in['beta1'], 'L0_gnn_W2l': _L0_gnn_in['W2l'], 'L0_gnn_b2l': _L0_gnn_in['b2l'], 'L0_gnn_W2r': _L0_gnn_in['W2r'], 'L0_gnn_g2': _L0_gnn_in['g2'], 'L0_gnn_beta2': _L0_gnn_in['beta2'], 'L1_gnn_basis': _L1_gnn_in['basis'], 'L1_gnn_comp': _L1_gnn_in['comp'], 'L1_gnn_bias': _L1_gnn_in['bias'], 'L1_gnn_res_w': _L1_gnn_in['res_w'], 'L1_gnn_res_b': _L1_gnn_in['res_b'], 'L1_gnn_gamma': _L1_gnn_in['gamma'], 'L1_gnn_beta': _L1_gnn_in['beta']}

def reference(x, src, dst, edge_type_64, edge_weight1, L0_gnn_W1l, L0_gnn_b1l, L0_gnn_W1r, L0_gnn_g1, L0_gnn_beta1, L0_gnn_W2l, L0_gnn_b2l, L0_gnn_W2r, L0_gnn_g2, L0_gnn_beta2, L1_gnn_basis, L1_gnn_comp, L1_gnn_bias, L1_gnn_res_w, L1_gnn_res_b, L1_gnn_gamma, L1_gnn_beta):
    import jax
    import jax.numpy as jnp

    def _L0_gnn_ref(x, edge_index, W1l, b1l, W1r, g1, beta1, W2l, b2l, W2r, g2, beta2):
        import jax, jax.numpy as jnp
        import numpy as np
        N = 100000
        E = 25000
        D_IN = 64
        D_H = 64
        EPS = 1e-05

        def _sage_conv(x, src, dst, Wl, bl, Wr, n_nodes):
            msg = x[src]
            agg = jax.ops.segment_sum(msg, dst, num_segments=n_nodes)
            deg = jax.ops.segment_sum(jnp.ones((src.shape[0], 1), x.dtype), dst, num_segments=n_nodes)
            agg = agg / jnp.maximum(deg, 1.0)
            return agg @ Wl.T + bl + x @ Wr.T

        def _layer_norm(h, g, b):
            mu = jnp.mean(h, axis=-1, keepdims=True)
            var = jnp.mean(jnp.square(h - mu), axis=-1, keepdims=True)
            return (h - mu) * jax.lax.rsqrt(var + EPS) * g + b
        src, dst = (edge_index[0], edge_index[1])
        n = x.shape[0]
        h = _sage_conv(x, src, dst, W1l, b1l, W1r, n)
        h = jax.nn.relu(_layer_norm(h, g1, beta1))
        res = h
        h = _sage_conv(h, src, dst, W2l, b2l, W2r, n)
        h = jax.nn.relu(_layer_norm(h, g2, beta2))
        return h + res

    def _L1_gnn_ref(node_feats, src, dst, etype, norm, basis, comp, bias, res_w, res_b, gamma, beta):
        import jax, jax.numpy as jnp
        import numpy as np
        N_NODES = 50000
        N_EDGES = 25000
        IN_F = 64
        OUT_F = 64
        NUM_RELS = 64
        NUM_BASES = 64
        BN_EPS = 1e-05
        N = node_feats.shape[0]
        R = comp.shape[0]
        W = jnp.einsum('rb,bio->rio', comp, basis)
        msg = node_feats[src] * norm
        seg = etype.astype(jnp.int32) * N + dst
        s = jax.ops.segment_sum(msg, seg, num_segments=R * N)
        s = s.reshape(R, N, -1)
        h = jnp.einsum('rni,rio->no', s, W) + bias
        h = jax.nn.relu(h)
        res = jax.nn.relu(node_feats @ res_w.T + res_b)
        y = h + res
        mean = jnp.mean(y, axis=0)
        var = jnp.var(y, axis=0)
        return (y - mean) * jax.lax.rsqrt(var + BN_EPS) * gamma + beta
    edge_index = jnp.stack([src, dst])
    x = _layernorm(x + _L0_gnn_ref(x, edge_index, L0_gnn_W1l, L0_gnn_b1l, L0_gnn_W1r, L0_gnn_g1, L0_gnn_beta1, L0_gnn_W2l, L0_gnn_b2l, L0_gnn_W2r, L0_gnn_g2, L0_gnn_beta2), axis=-1)
    x = _layernorm(x + _L1_gnn_ref(x, src, dst, edge_type_64, edge_weight1, L1_gnn_basis, L1_gnn_comp, L1_gnn_bias, L1_gnn_res_w, L1_gnn_res_b, L1_gnn_gamma, L1_gnn_beta), axis=-1)
    return x

_drawn_inputs = setup_inputs


def setup_inputs(seed=0):
    import zlib

    import numpy as np

    out = dict(_drawn_inputs(seed))
    spreads = {'L0_gnn_b1l': (0.0, 0.1),
     'L0_gnn_g1': (1.0, 0.2),
     'L0_gnn_beta1': (0.0, 0.1),
     'L0_gnn_b2l': (0.0, 0.1),
     'L0_gnn_g2': (1.0, 0.2),
     'L0_gnn_beta2': (0.0, 0.1),
     'L1_gnn_bias': (0.0, 0.1),
     'L1_gnn_res_b': (0.0, 0.1),
     'L1_gnn_gamma': (1.0, 0.2),
     'L1_gnn_beta': (0.0, 0.1)}
    factors = {}
    for name, (base, spread) in spreads.items():
        noise = np.random.default_rng([zlib.crc32(name.encode()), seed]).standard_normal(out[name].shape)
        drawn = base * np.exp(spread * noise) if base else spread * noise
        out[name] = jnp.asarray(drawn.astype(out[name].dtype))
    for name, factor in factors.items():
        out[name] = (out[name] * factor).astype(out[name].dtype)
    return out
```

```python
import concourse.bass as bass
from concourse import mybir
from contextlib import ExitStack

N = 100000
E = 50000
D = 64
R = 64
B = 64
EPS = 1e-5
P = 128

TILES = -(-E // (8 * P)) * 8
LAST_TILE = E // P
LAST_ROWS = E - LAST_TILE * P
BLOCKS = 4
TB = TILES // BLOCKS
SUPERS = TILES // 8
RTILES = -(-(E // P + R) // 8) * 8
RSUPERS = RTILES // 8
RTB = RTILES // BLOCKS

J = 16
CH = P * J
CHUNKS = -(-N // CH)
PLAST = (N - (CHUNKS - 1) * CH) // J
assert PLAST * J == N - (CHUNKS - 1) * CH and CHUNKS == SUPERS and TILES % 8 == 0

TRASH = N
DUMP = N + 1
TROWS = 784 * P
assert TROWS >= DUMP + 2 * P
FILLS = 16

fp32 = mybir.dt.float32
bf16 = mybir.dt.bfloat16
i32 = mybir.dt.int32
ALU = mybir.AluOpType
ACT = mybir.ActivationFunctionType
AX = mybir.AxisListType
ds = bass.ds

VECS = ["b1", "g1", "be1", "b2", "g2", "be2", "bias", "res_b", "gamma", "beta"]


class Scope:

    def __init__(self, nc, tag):
        self.nc, self.tag, self.stack, self.sems = nc, tag, ExitStack(), []

    def sb(self, name, shape, dt=fp32):
        return self.stack.enter_context(self.nc.sbuf_tensor(f"{self.tag}_{name}", shape, dt))

    def ps(self, name, shape, dt=fp32):
        return self.stack.enter_context(self.nc.psum_tensor(f"{self.tag}_{name}", shape, dt))

    def sem(self, name):
        self.sems.append(self.nc.alloc_semaphore(f"{self.tag}_{name}"))
        return self.sems[-1]

    def block(self):
        return self.stack.enter_context(self.nc.Block())

    def __enter__(self):
        return self

    def __exit__(self, *error):
        self.stack.close()
        if self.sems:
            self.nc.clear_and_free_semaphores(self.sems)
            self.nc.all_engine_barrier()
        return False


def tile_rows(tensor, first, count, partitions=P, each=J):
    return tensor[ds(first, count), :].rearrange("(p j) d -> p (j d)", j=each)


def bc(ap, shape, axis):
    return ap.unsqueeze(axis).to_broadcast(shape)


class Chain:

    def __init__(self, eng, sem):
        self.eng, self.sem, self.n = eng, sem, 0

    def __call__(self, ins):
        self.n += 1
        ins.then_inc(self.sem, 1)
        self.eng.wait_ge(self.sem, self.n)


class Persistent:

    def __init__(self, s):
        self.ident = s.sb("ident", [P, P])
        self.onesf = s.sb("onesf", [P, P])
        self.onesb = s.sb("onesb", [P, P], bf16)
        self.before = s.sb("before", [P, 2, 2 * P])
        self.beforeb = s.sb("beforeb", [P, P], bf16)
        self.iota_rel = s.sb("iota_rel", [P, R])
        self.iota_tile = s.sb("iota_tile", [P, BLOCKS])
        self.dumpcol = s.sb("dumpcol", [P, 2])
        self.srcidx = s.sb("srcidx", [P, TILES], i32)
        self.dcol = s.sb("dcol", [P, TILES])
        self.ddump = s.sb("ddump", [P, TILES])
        self.tcol = s.sb("tcol", [P, TILES])
        self.rec = s.sb("rec", [P, TILES, 4])
        self.posidx = s.sb("posidx", [P, TILES], i32)
        self.wst1 = s.sb("wst1", [P, D])
        self.wst2 = s.sb("wst2", [P, D])
        self.wblk = s.sb("wblk", [P, 3, P])
        self.vecs = s.sb("vecs", [P, len(VECS), D])
        self.eps = s.sb("eps", [P, 1])
        self.inv = s.sb("inv", [P, CHUNKS * J])
        self.bnab = s.sb("bnab", [P, 2, D])
        self.srcidx2 = s.sb("srcidx2", [P, RTILES], i32)
        self.dcol2 = s.sb("dcol2", [P, RTILES])
        self.ddump2 = s.sb("ddump2", [P, RTILES])
        self.wcol2 = s.sb("wcol2", [P, RTILES])

    def vec(self, name):
        return self.vecs[:, VECS.index(name), :]


def setup_phase(nc, g, io, dr):
    s = Scope(nc, "su")
    with s:
        rows_i = s.sb("rows_i", [TB, 3, BLOCKS, P], i32)
        rows_f = s.sb("rows_f", [TB, 4, BLOCKS, P])
        wnat = s.sb("wnat", [D, 5, 2 * D])
        cent = s.sb("cent", [D, D])
        comp = s.sb("comp", [R, B])
        compT = s.sb("compT", [B, R])
        basis = s.sb("basis", [B, D * D])
        wrel = s.sb("wrel", [R, D * D])
        bsum = s.sb("bsum", [P, 2])
        recpad = s.sb("recpad", [P, RTILES, 4])
        ps_edge = [s.ps(f"ps_edge{a}", [P, TILES]) for a in range(4)]
        ps_w = s.ps("ps_w", [P, 5, D])
        ps_ct = s.ps("ps_ct", [B, R])
        ps_rel = [s.ps(f"ps_rel{a}", [R, 512]) for a in range(2)]

        rows_padded = s.sem("rows_padded")
        recpad_set = s.sem("recpad_set")
        edges_loaded = s.sem("edges_loaded")
        weights_loaded = s.sem("weights_loaded")
        vectors_loaded = s.sem("vectors_loaded")
        basis_loaded = s.sem("basis_loaded")
        pool_steps = s.sem("pool_steps")
        consts_made = s.sem("consts_made")
        centering_made = s.sem("centering_made")
        rows_converted = s.sem("rows_converted")
        columns_made = s.sem("columns_made")
        weights_turned = s.sem("weights_turned")
        comp_turned = s.sem("comp_turned")
        comp_copied = s.sem("comp_copied")
        rel_made = s.sem("rel_made")
        rel_copied = s.sem("rel_copied")
        dve_steps = s.sem("dve_steps")
        stored = s.sem("stored")
        block = s.block()

        @block.sync
        def _(sp):
            sp.wait_ge(rows_padded, 4)
            full = 3 * TB * P
            n_edge = 0
            for k, name in enumerate(["src", "dst", "edge_type_64", "edge_weight1"]):
                flat = io[name] if k < 3 else io[name].rearrange("e o -> (e o)")
                rows = rows_i[:, k] if k < 3 else rows_f[:, 3]
                sp.dma_start(rows[:, 0:3, :],
                             flat[0:full].rearrange("(b r p) -> r b p", b=3, p=P)).then_inc(edges_loaded, 16)
                rest = LAST_TILE - 3 * TB
                sp.dma_start(rows[0:rest, 3, :],
                             flat[full:full + rest * P].rearrange("(r p) -> r p", p=P)).then_inc(edges_loaded, 16)
                sp.dma_start(rows[rest:rest + 1, 3, 0:LAST_ROWS],
                             flat[full + rest * P:E].rearrange("(r p) -> r p", p=LAST_ROWS)).then_inc(edges_loaded, 16)
            for k, name in enumerate(["L0_gnn_W1l", "L0_gnn_W2l", "L0_gnn_W1r", "L0_gnn_W2r", "L1_gnn_res_w"]):
                for h in range(2):
                    sp.dma_start(wnat[:, k, h * D:(h + 1) * D], io[name][:, :]).then_inc(weights_loaded, 16)
            sp.dma_start(comp[:, :], io["L1_gnn_comp"][:, :]).then_inc(basis_loaded, 16)
            sp.dma_start(basis[:, :], io["L1_gnn_basis"].rearrange("b i o -> b (i o)")).then_inc(basis_loaded, 16)
            for k, name in enumerate(["L0_gnn_b1l", "L0_gnn_g1", "L0_gnn_beta1", "L0_gnn_b2l", "L0_gnn_g2",
                                      "L0_gnn_beta2", "L1_gnn_bias", "L1_gnn_res_b", "L1_gnn_gamma",
                                      "L1_gnn_beta"]):
                sp.dma_start(g.vecs[:, k, :],
                             io[name].unsqueeze(0).to_broadcast([P, D])).then_inc(vectors_loaded, 16)
            sp.wait_ge(recpad_set, 2)
            sp.dma_start(dr["recs"].rearrange("(p t) f -> p (t f)", p=P),
                         recpad[:, :, :].rearrange("p t f -> p (t f)")).then_inc(stored, 16)
            sp.wait_ge(rows_converted, 1)
            sp.dma_start(dr["dst1"].rearrange("(b r p) -> r b p", b=BLOCKS, p=P),
                         rows_f[:, 1]).then_inc(stored, 16)
            sp.wait_ge(rel_copied, 8)
            sp.dma_start(dr["wrel"].rearrange("(r i) o -> r (i o)", i=D), wrel[:, :]).then_inc(stored, 16)
            sp.wait_ge(stored, 48)

        @block.gpsimd
        def _(pool):
            step = Chain(pool, pool_steps)
            step(nc.gpsimd.memset(g.ident[:, :], 0.0))
            step(nc.gpsimd.affine_select(out=g.ident[:, :], in_=g.ident[:, :], compare_op=ALU.not_equal, fill=1.0,
                                         base=0, pattern=[[-1, P]], channel_multiplier=1))
            step(nc.gpsimd.memset(g.before[:, :, :], 1.0))
            for i in range(2):
                nc.gpsimd.affine_select(out=g.before[:, i, :], in_=g.before[:, i, :], compare_op=ALU.is_gt, fill=0.0,
                                        base=-P * i, pattern=[[1, 2 * P]], channel_multiplier=-1)
            nc.gpsimd.iota(g.iota_rel[:, :], [[1, R]], base=0, channel_multiplier=0,
                           allow_small_or_imprecise_dtypes=True)
            nc.gpsimd.iota(g.iota_tile[:, :], [[P, BLOCKS]], base=0, channel_multiplier=1,
                           allow_small_or_imprecise_dtypes=True)
            nc.gpsimd.iota(g.dumpcol[:, :], [[P, 2]], base=DUMP, channel_multiplier=1,
                           allow_small_or_imprecise_dtypes=True).then_inc(consts_made, 1)

        @block.tensor
        def _(pe):
            pe.wait_ge(consts_made, 1)
            pe.wait_ge(rows_converted, 1)
            for a in range(4):
                for b in range(BLOCKS):
                    last = nc.tensor.transpose(ps_edge[a][:, b * TB:(b + 1) * TB], rows_f[:, a, b, :],
                                               g.ident[0:TB, 0:TB])
            last.then_inc(columns_made, 1)
            pe.wait_ge(weights_loaded, 160)
            pe.wait_ge(centering_made, 1)
            for k in range(5):
                last = nc.tensor.matmul(ps_w[:, k, :], wnat[:, k, :], cent[:, :] if k < 4 else g.ident[0:D, 0:D],
                                        start=True, stop=True)
            last.then_inc(weights_turned, 1)
            pe.wait_ge(basis_loaded, 32)
            nc.tensor.transpose(ps_ct[:, :], comp[:, :], g.ident[0:R, 0:R]).then_inc(comp_turned, 1)
            pe.wait_ge(comp_copied, 1)
            for k in range(8):
                if k >= 2:
                    pe.wait_ge(rel_copied, k - 1)
                nc.tensor.matmul(ps_rel[k % 2][:, :], compT[:, :], basis[:, k * 512:(k + 1) * 512],
                                 start=True, stop=True).then_inc(rel_made, 1)

        @block.scalar
        def _(act):
            act.wait_ge(comp_turned, 1)
            nc.scalar.copy(compT[:, :], ps_ct[:, :]).then_inc(comp_copied, 1)
            for k in range(8):
                act.wait_ge(rel_made, k + 1)
                nc.scalar.copy(wrel[:, k * 512:(k + 1) * 512], ps_rel[k % 2][:, :]).then_inc(rel_copied, 1)

        @block.vector
        def _(dve):
            step = Chain(dve, dve_steps)
            for k, pad in enumerate([0, TRASH, R]):
                nc.vector.memset(rows_i[:, k, 3, :], pad).then_inc(rows_padded, 1)
            nc.vector.memset(rows_f[:, 3, 3, :], 0.0).then_inc(rows_padded, 1)
            nc.vector.memset(recpad[:, :, :], 0.0).then_inc(recpad_set, 1)
            dve.wait_ge(recpad_set, 1)
            nc.vector.memset(recpad[:, :, 1:2], float(TRASH)).then_inc(recpad_set, 1)
            nc.vector.memset(g.onesf[:, :], 1.0)
            nc.vector.memset(g.onesb[:, :], 1.0)
            nc.vector.memset(g.eps[:, :], EPS)
            step(nc.vector.memset(g.wblk[:, :, :], 0.0))
            step(nc.vector.memset(g.rec[:, :, 3:4], 0.0))
            dve.wait_ge(edges_loaded, 12 * 16)
            nc.vector.tensor_copy(rows_f[:, 0:3], rows_i[:, :]).then_inc(rows_converted, 1)
            dve.wait_ge(consts_made, 1)
            nc.vector.tensor_scalar(cent[:, :], g.ident[0:D, 0:D], -1.0 / D, None, ALU.add).then_inc(centering_made, 1)
            nc.vector.tensor_copy(g.beforeb[:, :], g.before[:, 0, 0:P])
            dve.wait_ge(vectors_loaded, 160)
            for j, name in enumerate(["b1", "b2"]):
                step(nc.vector.tensor_reduce(bsum[:, j:j + 1], g.vec(name), AX.X, ALU.add))
                step(nc.vector.tensor_scalar(bsum[:, j:j + 1], bsum[:, j:j + 1], -1.0 / D, None, ALU.mult))
                step(nc.vector.tensor_scalar(g.vec(name), g.vec(name), bsum[:, j:j + 1], None, ALU.add))
            dve.wait_ge(columns_made, 1)
            nc.vector.tensor_copy(g.srcidx[:, :], ps_edge[0][:, :])
            step(nc.vector.tensor_copy(g.dcol[:, :], ps_edge[1][:, :]))
            nc.vector.tensor_copy(g.tcol[:, :], ps_edge[2][:, :])
            for f, a in enumerate([0, 1, 3]):
                nc.vector.tensor_copy(g.rec[:, :, f], ps_edge[a][:, :])
            nc.vector.tensor_tensor(g.ddump[:, :].rearrange("p (g j) -> p g j", j=2),
                                    bc(g.dumpcol[:, :], [P, TILES // 2, 2], 1),
                                    g.dcol[:, :].rearrange("p (g j) -> p g j", j=2), ALU.subtract)
            dve.wait_ge(weights_turned, 1)
            nc.vector.tensor_copy(g.wst1[:, :], ps_w[:, 0, :])
            nc.vector.tensor_copy(g.wst2[:, :], ps_w[:, 1, :])
            for k in range(3):
                for h in range(2):
                    nc.vector.tensor_copy(g.wblk[h * D:(h + 1) * D, k, h * D:(h + 1) * D],
                                          ps_w[h * D:(h + 1) * D, 2 + k, :])


def sort_phase(nc, g, dr):
    s = Scope(nc, "so")
    with s:
        onehot = s.sb("onehot", [P, TILES, R], bf16)
        zero = s.sb("zero", [P, TROWS * (D + 1) // (P * FILLS)])
        bias = s.sb("bias", [P, TROWS // (P * FILLS), D])
        count = s.sb("count", [P, R])
        count_i = s.sb("count_i", [P, R], i32)
        tiles_i = s.sb("tiles_i", [P, R], i32)
        tiles_f = s.sb("tiles_f", [P, R])
        tend = s.sb("tend", [P, R])
        base = s.sb("base", [P, R])
        cmp = s.sb("cmp", [P, BLOCKS, R])
        ttype = s.sb("ttype", [P, BLOCKS])
        ttype_i = s.sb("ttype_i", [P, BLOCKS], i32)
        work = s.sb("work", [P, 8, R])
        pos = s.sb("pos", [P, TILES])
        pos_i = s.sb("pos_i", [P, TILES], i32)
        tile_i = s.sb("tile_i", [P, TILES], i32)
        slot_i = s.sb("slot_i", [P, TILES], i32)
        ps_count = s.ps("ps_count", [P, 8, R])
        ps_rank = [s.ps(f"ps_rank{a}", [P, 8, R]) for a in range(2)]
        ps_total = [s.ps(f"ps_total{a}", [P, R]) for a in range(2)]

        fills_set = s.sem("fills_set")
        filled = s.sem("filled")
        onehot_made = s.sem("onehot_made")
        counted = s.sem("counted")
        ranked = s.sem("ranked")
        rank_used = s.sem("rank_used")
        dve_steps = s.sem("dve_steps")
        loop_steps = s.sem("loop_steps")
        types_made = s.sem("types_made")
        block = s.block()

        @block.sync
        def _(sp):
            sp.wait_ge(fills_set, 2)
            views = [(dr["t1"], zero[:, :], D + 1), (dr["t2"], zero[:, :], D),
                     (dr["t3"], bias[:, :, :].rearrange("p n d -> p (n d)"), D)]
            for table, tile, width in views:
                each = TROWS * width // (P * FILLS)
                flat = table.rearrange("(p n) d -> p (n d)", p=P)
                for k in range(FILLS):
                    sp.dma_start(flat[:, k * each:(k + 1) * each], tile[:, 0:each]).then_inc(filled, 16)
            sp.wait_ge(types_made, 1)
            with nc.allow_non_contiguous_dma(reason="512 small words, once"):
                sp.dma_start(dr["ttype"].rearrange("(b p) -> p b", p=P), ttype_i[:, :]).then_inc(filled, 16)
            sp.wait_ge(filled, 16 * (3 * FILLS + 1))

        @block.tensor
        def _(pe):
            for q in range(4):
                pe.wait_ge(onehot_made, q + 1)
            for b in range(SUPERS):
                last = nc.tensor.matmul(ps_count[:, :, :], g.onesb[:, :], onehot[:, 8 * b:8 * b + 8, :],
                                        start=(b == 0), stop=(b == SUPERS - 1))
            last.then_inc(counted, 1)

            def rank(b, a, first):
                if not first:
                    pe.wait_ge(rank_used, b - 1)
                tiles = onehot[:, ds(8 * b, 8), :]
                nc.tensor.matmul(ps_rank[a][:, :, :], g.beforeb[:, :], tiles, start=True, stop=False)
                for k in range(1, 8):
                    nc.tensor.matmul(ps_rank[a][:, k:8, :], g.onesb[:, :], onehot[:, ds(8 * b, 8 - k), :],
                                     start=False, stop=(k == 7))
                for k in range(8):
                    last = nc.tensor.matmul(ps_total[a][:, :], g.onesb[:, :], onehot[:, ds(8 * b + k, 1), :],
                                            start=(k == 0), stop=(k == 7))
                last.then_inc(ranked, 1)

            rank(0, 0, True)
            rank(1, 1, True)
            with pe.Fori(1, SUPERS // 2) as h:
                rank(2 * h, 0, False)
                rank(2 * h + 1, 1, False)
            rank(SUPERS - 1, 0, False)

        @block.vector
        def _(dve):
            step = Chain(dve, dve_steps)
            nc.vector.memset(zero[:, :], 0.0).then_inc(fills_set, 1)
            nc.vector.tensor_copy(bias[:, :, :], bc(g.vec("bias"), [P, TROWS // (P * FILLS), D], 1)).then_inc(
                fills_set, 1)
            for q in range(4):
                t = slice(q * TB, (q + 1) * TB)
                nc.vector.tensor_tensor(onehot[:, t, :], bc(g.iota_rel[:, :], [P, TB, R], 1),
                                        bc(g.tcol[:, t], [P, TB, R], 2), ALU.is_equal).then_inc(onehot_made, 1)
            dve.wait_ge(counted, 1)
            step(nc.vector.tensor_reduce(count[:, :], ps_count[:, :, :].rearrange("p k r -> p r k"), AX.X, ALU.add))
            step(nc.vector.tensor_scalar(count_i[:, :], count[:, :], float(P - 1), None, ALU.add))
            step(nc.vector.tensor_scalar(tiles_i[:, :], count_i[:, :], 7, None, ALU.arith_shift_right))
            step(nc.vector.tensor_copy(tiles_f[:, :], tiles_i[:, :]))
            step(nc.vector.tensor_tensor_scan(tend[:, :], g.onesf[:, 0:R], tiles_f[:, :], 0.0, ALU.mult, ALU.add))
            step(nc.vector.tensor_tensor(base[:, :], tend[:, :], tiles_f[:, :], ALU.subtract))
            step(nc.vector.tensor_scalar(base[:, :], base[:, :], float(P), None, ALU.mult))
            step(nc.vector.tensor_tensor(cmp[:, :, :], bc(g.iota_tile[:, :], [P, BLOCKS, R], 2),
                                         bc(tend[:, :], [P, BLOCKS, R], 1), ALU.is_ge))
            step(nc.vector.tensor_reduce(ttype[:, :], cmp[:, :, :], AX.X, ALU.add))
            nc.vector.tensor_scalar(ttype_i[:, :], ttype[:, :], float(R - 1), None, ALU.min).then_inc(types_made, 1)

            def place(b, a, _):
                dve.wait_ge(ranked, b + 1)
                nc.vector.tensor_tensor(work[:, :, :], ps_rank[a][:, :, :], bc(base[:, :], [P, 8, R], 1),
                                        ALU.add).then_inc(loop_steps, 1)
                dve.wait_ge(loop_steps, 3 * b + 1)
                nc.vector.tensor_tensor(base[:, :], base[:, :], ps_total[a][:, :], ALU.add).then_inc(rank_used, 1)
                nc.vector.tensor_tensor(work[:, :, :], work[:, :, :], onehot[:, ds(8 * b, 8), :],
                                        ALU.mult).then_inc(loop_steps, 1)
                dve.wait_ge(loop_steps, 3 * b + 2)
                nc.vector.tensor_reduce(pos[:, ds(8 * b, 8)], work[:, :, :], AX.X, ALU.add).then_inc(loop_steps, 1)
                dve.wait_ge(loop_steps, 3 * b + 3)

            place(0, 0, True)
            place(1, 1, True)
            with dve.Fori(1, SUPERS // 2) as h:
                place(2 * h, 0, False)
                place(2 * h + 1, 1, False)
            place(SUPERS - 1, 0, False)
            step(nc.vector.tensor_copy(pos_i[:, :], pos[:, :]))
            step(nc.vector.tensor_scalar(tile_i[:, :], pos_i[:, :], 7, None, ALU.arith_shift_right))
            step(nc.vector.tensor_scalar(slot_i[:, :], pos_i[:, :], P - 1, None, ALU.bitwise_and))
            nc.vector.scalar_tensor_tensor(g.posidx[:, :], slot_i[:, :], float(RTILES), tile_i[:, :], ALU.mult,
                                           ALU.add)


def edge_phase(nc, g, tag, x, dst_rows, srcidx, dcol, ddump, table, width, wst, lin_out, wblk, lin_bias, supers,
               wcol=None, wrel=None, ttype=None):
    s = Scope(nc, tag)
    relation = wrel is not None
    degree = width > D
    with s:
        xg = s.sb("xg", [P, 4, 2, P])
        gidx = s.sb("gidx", [P, 4, 2], i32)
        sidx = s.sb("sidx", [P, 4, 2], i32)
        first = s.sb("first", [P, 4, 2])
        drow = s.sb("drow", [P, 4, 2 * P])
        same = s.sb("same", [P, 4, 2, 2 * P])
        dup = s.sb("dup", [P, 4, 2, 2 * P], bf16)
        zs = s.sb("zs", [P, 2, 2 * P])
        outs = s.sb("outs", [P, 4, 2, width])
        wslot = s.sb("wslot", [P, 4, D]) if relation else None
        xf = s.sb("xf", [P, J // 2, P])
        xt = s.sb("xt", [P, 2, 512])
        lf = s.sb("lf", [P, J * D])
        ps_z = [s.ps(f"ps_z{a}", [P, 2 * P]) for a in range(2)]
        ps_o = [s.ps(f"ps_o{a}", [P, 512]) for a in range(2)]
        ps_d = [s.ps(f"ps_d{a}", [P, 512]) for a in range(2)]
        ps_t = s.ps("ps_t", [P, 512])
        ps_l = s.ps("ps_l", [P, 512])

        drow_loaded = [s.sem(f"drow_loaded{q}") for q in range(4)]
        gathered = [s.sem(f"gathered{q}") for q in range(4)]
        w_loaded = [s.sem(f"w_loaded{q}") for q in range(4)] if relation else None
        scattered = s.sem("scattered")
        xg_zeroed = s.sem("xg_zeroed")
        gidx_ready = s.sem("gidx_ready")
        select_ready = s.sem("select_ready")
        dups_counted = s.sem("dups_counted")
        dups_read = s.sem("dups_read")
        sidx_ready = s.sem("sidx_ready")
        z_ready = s.sem("z_ready")
        z_copied = s.sem("z_copied")
        out_ready = s.sem("out_ready")
        out_copied = s.sem("out_copied")
        pool_tick = s.sem("pool_tick")
        xf_loaded = s.sem("xf_loaded")
        turned = s.sem("turned")
        turned_copied = s.sem("turned_copied")
        lin_ready = s.sem("lin_ready")
        lin_done = s.sem("lin_done")
        lin_stored = s.sem("lin_stored")
        block = s.block()
        last_super = supers - 1

        def over_supers(eng, body):
            cuts = sorted({0, 1, CHUNKS - 2, CHUNKS - 1, CHUNKS, CHUNKS + 1, last_super, supers})
            for a, b in zip(cuts, cuts[1:]):
                if b > supers:
                    break
                if b - a == 1:
                    body(a, a)
                else:
                    with eng.Fori(a, b) as c:
                        body(c, a)

        def parts(at):
            return 0 if not 0 <= at < CHUNKS else PLAST if at == CHUNKS - 1 else P

        def chunk(tensor, c, at):
            return tile_rows(tensor, c * CH, parts(at) * J)

        @block.sync
        def _(sp):
            sp.dma_start(xf[:, :, :].rearrange("p a b -> p (a b)"), chunk(x, 0, 0)).then_inc(xf_loaded, 16)

            def body(c, at):
                for q in range(4):
                    if relation:
                        rels = [sp.value_load(ttype[ds(8 * c + 2 * q + i, 1)].unsqueeze(0), min_val=0,
                                              max_val=R - 1) for i in range(2)]
                    if at > 0:
                        sp.wait_ge(select_ready, 4 * c + q - 3)
                    src = dst_rows[ds(1024 * c + 256 * q, 256)].unsqueeze(0).to_broadcast([P, 256])
                    sp.dma_start(drow[:, q, :], src).then_inc(drow_loaded[q], 16)
                    if relation:
                        if at > 0:
                            sp.wait_ge(out_ready, 4 * c + q - 3)
                        for i in range(2):
                            sp.dma_start(wslot[i * D:(i + 1) * D, q, :],
                                         wrel[ds(rels[i] * D, D), :]).then_inc(w_loaded[q], 16)
                if parts(at - 1):
                    sp.wait_ge(lin_done, 2 * c)
                    sp.dma_start(chunk(lin_out, c - 1, at - 1), lf[0:parts(at - 1), :]).then_inc(lin_stored, 16)
                if parts(at + 1):
                    sp.wait_ge(turned, 2 * c + 2)
                    n = parts(at + 1)
                    sp.dma_start(xf[0:n, :, :].rearrange("p a b -> p (a b)"),
                                 chunk(x, c + 1, at + 1)).then_inc(xf_loaded, 16)

            over_supers(sp, body)
            if parts(last_super):
                sp.wait_ge(lin_done, 2 * CHUNKS)
                sp.dma_start(chunk(lin_out, CHUNKS - 1, CHUNKS - 1), lf[0:PLAST, :]).then_inc(lin_stored, 16)
            sp.wait_ge(lin_stored, 16 * CHUNKS)

        @block.gpsimd
        def _(pool):
            def gather(c, q, used):
                grp = 4 * c + q
                pool.wait_ge(gidx_ready, grp + 1)
                if used:
                    pool.wait_ge(z_ready, grp - 3)
                else:
                    pool.wait_ge(xg_zeroed, 1)
                pool.sem_inc(pool_tick, 1)
                for i in range(2):
                    pool.indirect_dma_start(out=xg[:, q, i, i * D:(i + 1) * D], out_offset=None, in_=x[:, :],
                                            in_offset=bass.IndirectOffsetOnAxis(ap=gidx[:, q, i:i + 1], axis=0)
                                            ).then_inc(gathered[q], 16)

            gather(0, 0, False)
            gather(0, 1, False)

            def body(c, at):
                for q in range(4):
                    if q < 2:
                        gather(c, q + 2, at > 0)
                    elif at < last_super:
                        gather(c + 1, q - 2, True)
                    grp = 4 * c + q
                    pool.wait_ge(sidx_ready, grp + 1)
                    pool.wait_ge(out_copied, grp + 1)
                    if at > 0 or q > 0:
                        pool.wait_ge(scattered, 32 * grp)
                    pool.sem_inc(pool_tick, 1)
                    for j in range(2):
                        pool.indirect_dma_start(out=table[:, :],
                                                out_offset=bass.IndirectOffsetOnAxis(ap=sidx[:, q, j:j + 1], axis=0),
                                                in_=outs[:, q, j, :], in_offset=None,
                                                compute_op=ALU.add).then_inc(scattered, 16)

            over_supers(pool, body)
            pool.wait_ge(scattered, 32 * 4 * supers)

        @block.vector
        def _(dve):
            nc.vector.memset(xg[:, :, :, :], 0.0).then_inc(xg_zeroed, 1)

            def stage_gather(c, q, used):
                grp = 4 * c + q
                if used:
                    dve.wait_ge(gathered[q], 32 * c)
                nc.vector.tensor_copy(gidx[:, q, :], srcidx[:, ds(2 * grp, 2)]).then_inc(gidx_ready, 1)

            def select(c, q, used):
                grp = 4 * c + q
                dve.wait_ge(drow_loaded[q], 16 * (c + 1))
                if used:
                    dve.wait_ge(z_ready, grp - 3)
                for i in range(2):
                    col = ds(2 * grp + i, 1)
                    if wcol is None:
                        nc.vector.tensor_scalar(same[:, q, i, :], drow[:, q, :], dcol[:, col], None, ALU.is_equal)
                    else:
                        nc.vector.tensor_scalar(same[:, q, i, :], drow[:, q, :], dcol[:, col], wcol[:, col],
                                                ALU.is_equal, ALU.mult)
                for i in range(2):
                    col = ds(2 * grp + i, 1)
                    last = nc.vector.scalar_tensor_tensor(dup[:, q, i, :], drow[:, q, :], dcol[:, col],
                                                          g.before[:, i, :], ALU.is_equal, ALU.mult)
                last.then_inc(select_ready, 1)

            stage_gather(0, 0, False)
            stage_gather(0, 1, False)
            select(0, 0, False)

            def body(c, at):
                for q in range(4):
                    if q < 2:
                        stage_gather(c, q + 2, at > 0)
                    elif at < last_super:
                        stage_gather(c + 1, q - 2, True)
                    if q < 3:
                        select(c, q + 1, at > 0)
                    elif at < last_super:
                        select(c + 1, 0, True)
                    grp = 4 * c + q
                    cols = ds(2 * grp, 2)
                    dve.wait_ge(dups_counted, grp + 1)
                    nc.vector.scalar_tensor_tensor(first[:, q, :], ps_d[q % 2][:, 0:2], 1.0,
                                                   ddump[:, cols], ALU.min, ALU.mult).then_inc(dups_read, 1)
                    dve.wait_ge(dups_read, grp + 1)
                    if at > 0:
                        dve.wait_ge(scattered, 32 * (grp - 3))
                    nc.vector.tensor_tensor(sidx[:, q, :], first[:, q, :], dcol[:, cols],
                                            ALU.add).then_inc(sidx_ready, 1)
                    if parts(at) and q >= 2:
                        h, n = q - 2, parts(at)
                        dve.wait_ge(lin_ready, 2 * c + h + 1)
                        if at > 0:
                            dve.wait_ge(lin_stored, 16 * c)
                        nc.vector.tensor_tensor(
                            lf[0:n, h * 512:(h + 1) * 512].rearrange("p (j d) -> p j d", d=D),
                            ps_l[0:n, :].rearrange("p (j d) -> p j d", d=D),
                            bc(lin_bias[0:n, :], [n, 8, D], 1), ALU.add).then_inc(lin_done, 1)

            over_supers(dve, body)

        @block.tensor
        def _(pe):
            def body(c, at):
                for q in range(4):
                    grp, a = 4 * c + q, q % 2
                    ready = at > 0 or q >= 2
                    pe.wait_ge(select_ready, grp + 1)
                    if ready:
                        pe.wait_ge(dups_read, grp - 1)
                    for j in range(2):
                        for i in range(2):
                            last = nc.tensor.matmul(ps_d[a][:, j:j + 1],
                                                    dup[:, q, i, j * P:(j + 1) * P], g.onesb[:, 0:1],
                                                    start=(i == 0), stop=(i == 1))
                    last.then_inc(dups_counted, 1)
                    if ready:
                        pe.wait_ge(out_copied, grp - 1)
                    if degree:
                        for j in range(2):
                            for i in range(2):
                                nc.tensor.matmul(ps_o[a][:, j * width + D:j * width + D + 1],
                                                 same[:, q, i, j * P:(j + 1) * P], g.onesf[:, 0:1],
                                                 start=(i == 0), stop=(i == 1))
                    pe.wait_ge(gathered[q], 32 * (c + 1))
                    if ready:
                        pe.wait_ge(z_copied, grp - 1)
                    for i in range(2):
                        last = nc.tensor.matmul(ps_z[a][:, :], xg[:, q, i, :], same[:, q, i, :],
                                                start=(i == 0), stop=(i == 1))
                    last.then_inc(z_ready, 1)
                    n = parts(at)
                    if n and q < 2:
                        if q == 0:
                            pe.wait_ge(xf_loaded, 16 * (c + 1))
                        if at > 0 or q > 0:
                            pe.wait_ge(turned_copied, 2 * c + q)
                        for k in range(4):
                            last = nc.tensor.transpose(ps_t[:, k * n:(k + 1) * n], xf[0:n, 4 * q + k, :],
                                                       g.ident[0:n, 0:n])
                        last.then_inc(turned, 1)
                    if n and q >= 2:
                        h = q - 2
                        pe.wait_ge(turned_copied, 2 * c + h + 1)
                        if at > 0 or h > 0:
                            pe.wait_ge(lin_done, 2 * c + h)
                        for k in range(4):
                            last = nc.tensor.matmul(ps_l[0:n, k * P:(k + 1) * P], xt[:, h, k * n:(k + 1) * n],
                                                    wblk, start=True, stop=True)
                        last.then_inc(lin_ready, 1)
                    pe.wait_ge(z_copied, grp + 1)
                    if relation:
                        pe.wait_ge(w_loaded[q], 32 * (c + 1))
                    for j in range(2):
                        last = nc.tensor.matmul(ps_o[a][:, j * width:j * width + D], zs[:, a, j * P:(j + 1) * P],
                                                wslot[:, q, :] if relation else wst[:, :], start=True, stop=True)
                    last.then_inc(out_ready, 1)

            over_supers(pe, body)

        @block.scalar
        def _(act):
            def body(c, at):
                for q in range(4):
                    grp, a = 4 * c + q, q % 2
                    act.wait_ge(z_ready, grp + 1)
                    if at > 0 or q >= 2:
                        act.wait_ge(out_ready, grp - 1)
                    nc.scalar.copy(zs[:, a, :], ps_z[a][:, :]).then_inc(z_copied, 1)
                    n = parts(at)
                    if n and q < 2:
                        act.wait_ge(turned, 2 * c + q + 1)
                        if at > 0:
                            act.wait_ge(lin_ready, 2 * c + q - 1)
                        nc.scalar.copy(xt[:, q, 0:4 * n], ps_t[:, 0:4 * n]).then_inc(turned_copied, 1)
                    act.wait_ge(out_ready, grp + 1)
                    if at > 0:
                        act.wait_ge(scattered, 32 * (grp - 3))
                    nc.scalar.copy(outs[:, q, :, :].rearrange("p j w -> p (j w)"),
                                   ps_o[a][:, 0:2 * width]).then_inc(out_copied, 1)

            over_supers(act, body)


DEEP = 4
PEEL = 2 * DEEP


def over_chunks(eng, stages):
    deepest = max(lag for _, lag in stages)

    def step(s, j, fixed):
        for stage, lag in stages:
            if fixed and not 0 <= s - lag < CHUNKS:
                continue
            n = PLAST if fixed and s - lag == CHUNKS - 1 else P
            stage(s - lag, (j - lag) % DEEP, n, not fixed or s - lag >= DEEP)

    for t in range(PEEL):
        step(t, t % DEEP, True)
    with eng.Fori(PEEL // DEEP, (CHUNKS - 1) // DEEP) as k:
        for j in range(DEEP):
            step(DEEP * k + j, j, False)
    for t in range(CHUNKS - 1, CHUNKS + deepest):
        step(t, t % DEEP, True)


def wide(ap, n, row=D):
    return ap[0:n, :].rearrange("p (j d) -> p j d", d=row)


class RecordScatter:

    def __init__(self, nc, g, s, table, first_tile):
        self.nc, self.g, self.table, self.first_tile = nc, g, table, first_tile
        self.idx = s.sb("rec_idx", [P, DEEP, 4], i32)
        self.val = s.sb("rec_val", [P, DEEP, 4, 4])
        self.staged = s.sem("rec_staged")
        self.landed = [s.sem(f"rec_landed{j}") for j in range(DEEP)]
        self.tick = s.sem("rec_tick")
        self.lots = [0] * DEEP

    def tiles(self, c):
        return [k for k in range(4) if not isinstance(c, int) or self.first_tile + 4 * c + k <= LAST_TILE]

    def stage(self, eng):
        def run(c, j, n, old):
            if old:
                eng.wait_ge(self.landed[j], self.done(c, j))
            cols = ds(4 * c + self.first_tile, 4)
            self.nc.vector.tensor_copy(self.idx[:, j, :], self.g.posidx[:, cols])
            self.nc.vector.tensor_copy(self.val[:, j, :, :], self.g.rec[:, cols, :]).then_inc(self.staged, 1)
        return run

    def done(self, c, j):
        return 64 * ((c - j) // DEEP) if isinstance(c, int) else 16 * (c - j)

    def scatter(self, pool):
        def run(c, j, n, old):
            pool.wait_ge(self.staged, c + 1)
            pool.sem_inc(self.tick, 1)
            for k in self.tiles(c):
                rows = P
                if isinstance(c, int) and self.first_tile + 4 * c + k == LAST_TILE:
                    rows = LAST_ROWS
                pool.indirect_dma_start(out=self.table[:, :],
                                        out_offset=bass.IndirectOffsetOnAxis(ap=self.idx[0:rows, j, k:k + 1], axis=0),
                                        in_=self.val[0:rows, j, k, :], in_offset=None).then_inc(self.landed[j], 16)
        return run

    def wait_all(self, pool):
        for j in range(DEEP):
            chunks = [c for c in range(CHUNKS) if c % DEEP == j]
            pool.wait_ge(self.landed[j], 16 * sum(len(self.tiles(c)) for c in chunks))


def norm_phase1(nc, g, table, lin, h_out, recs):
    s = Scope(nc, "n1")
    with s:
        W = J * (D + 1)
        tin = s.sb("tin", [P, DEEP, W])
        rin = s.sb("rin", [P, DEEP, J * D])
        a = s.sb("a", [P, DEEP, J * D])
        sq = s.sb("sq", [P, DEEP, J * D])
        deg = s.sb("deg", [P, DEEP, J])
        var = s.sb("var", [P, DEEP, J])
        rec = RecordScatter(nc, g, s, recs, 0)
        loaded = [s.sem(f"loaded{j}") for j in range(DEEP)]
        stored = [s.sem(f"stored{j}") for j in range(DEEP)]
        d1, inverted, divided, summed = s.sem("deg_max"), s.sem("inverted"), s.sem("divided"), s.sem("summed")
        squared, reduced, rooted = s.sem("squared"), s.sem("reduced"), s.sem("rooted")
        rsigma, scaled, gained = s.sem("rsigma"), s.sem("scaled"), s.sem("gained")
        shifted, h_ready = s.sem("shifted"), s.sem("h_ready")
        tick = s.sem("tick")
        block = s.block()

        @block.sync
        def _(sp):
            def load(c, j, n, old):
                if old:
                    sp.wait_ge(summed, c - DEEP + 1)
                sp.dma_start(tin[0:n, j, :], tile_rows(table, c * CH, n * J)).then_inc(loaded[j], 16)
                sp.dma_start(rin[0:n, j, :], tile_rows(lin, c * CH, n * J)).then_inc(loaded[j], 16)

            def store(c, j, n, old):
                sp.wait_ge(h_ready, c + 1)
                sp.dma_start(tile_rows(h_out, c * CH, n * J), a[0:n, j, :]).then_inc(stored[j], 16)

            over_chunks(sp, [(load, 0), (store, 3)])
            for j in range(DEEP):
                sp.wait_ge(stored[j], 16 * len(range(j, CHUNKS, DEEP)))

        @block.vector
        def _(dve):
            def add_up(c, j, n, old):
                dve.wait_ge(loaded[j], full(c, j, 32))
                t3, a3 = wide(tin[:, j, :], n, D + 1), wide(a[:, j, :], n)
                inv = g.inv[0:n, ds(c * J, J)]
                nc.vector.tensor_scalar(deg[0:n, j, :], t3[:, :, D], 1.0, None, ALU.max).then_inc(d1, 1)
                dve.wait_ge(d1, c + 1)
                nc.vector.reciprocal(inv, deg[0:n, j, :]).then_inc(inverted, 1)
                dve.wait_ge(inverted, c + 1)
                if old:
                    dve.wait_ge(stored[j], full(c, j, 16) - 16)
                nc.vector.tensor_tensor(a3, t3[:, :, 0:D], bc(inv, [n, J, D], 2), ALU.mult).then_inc(divided, 1)
                dve.wait_ge(divided, c + 1)
                nc.vector.tensor_tensor(a[0:n, j, :], a[0:n, j, :], rin[0:n, j, :], ALU.add).then_inc(summed, 1)

            def variance(c, j, n, old):
                dve.wait_ge(squared, c + 1)
                nc.vector.tensor_reduce(var[0:n, j, :], wide(sq[:, j, :], n), AX.X, ALU.add).then_inc(reduced, 1)

            def scale(c, j, n, old):
                dve.wait_ge(rooted, c + 1)
                a3 = wide(a[:, j, :], n)
                nc.vector.reciprocal(var[0:n, j, :], var[0:n, j, :]).then_inc(rsigma, 1)
                dve.wait_ge(rsigma, c + 1)
                nc.vector.tensor_tensor(a3, a3, bc(var[0:n, j, :], [n, J, D], 2), ALU.mult).then_inc(scaled, 1)
                dve.wait_ge(scaled, c + 1)
                nc.vector.tensor_tensor(a3, a3, bc(g.vec("g1")[0:n, :], [n, J, D], 1), ALU.mult).then_inc(gained, 1)

            over_chunks(dve, [(rec.stage(dve), 0), (variance, 1), (add_up, 0), (scale, 1)])

        @block.scalar
        def _(act):
            def square(c, j, n, old):
                act.wait_ge(summed, c + 1)
                if old:
                    act.wait_ge(reduced, c - DEEP + 1)
                nc.scalar.activation(sq[0:n, j, :], a[0:n, j, :], ACT.Square).then_inc(squared, 1)

            def root(c, j, n, old):
                act.wait_ge(reduced, c + 1)
                nc.scalar.activation(var[0:n, j, :], var[0:n, j, :], ACT.Sqrt, bias=g.eps[0:n, :],
                                     scale=1.0 / D).then_inc(rooted, 1)

            def clip(c, j, n, old):
                act.wait_ge(shifted, c + 1)
                nc.scalar.activation(a[0:n, j, :], a[0:n, j, :], ACT.Relu).then_inc(h_ready, 1)

            over_chunks(act, [(root, 1), (square, 0), (clip, 2)])

        @block.gpsimd
        def _(pool):
            def shift(c, j, n, old):
                pool.wait_ge(gained, c + 1)
                a3 = wide(a[:, j, :], n)
                nc.gpsimd.tensor_tensor(a3, a3, bc(g.vec("be1")[0:n, :], [n, J, D], 1), ALU.add).then_inc(shifted, 1)

            over_chunks(pool, [(rec.scatter(pool), 0), (shift, 1)])
            rec.wait_all(pool)


def full(c, j, each):
    return each * ((c - j) // DEEP + 1) if isinstance(c, int) else each // DEEP * (c - j) + each


def norm_phase2(nc, g, table, lin, h1, x, x1_out, recs):
    s = Scope(nc, "n2")
    with s:
        W = J * D
        tin = s.sb("tin", [P, DEEP, W])
        rin = s.sb("rin", [P, DEEP, W])
        hin = s.sb("hin", [P, DEEP, W])
        xin = s.sb("xin", [P, DEEP, W])
        a = s.sb("a", [P, DEEP, W])
        sq = s.sb("sq", [P, 2, W])
        sq2 = s.sb("sq2", [P, 2, W])
        out = s.sb("out", [P, DEEP, W])
        var = s.sb("var", [P, DEEP, J])
        mean = s.sb("mean", [P, DEEP, J])
        var2 = s.sb("var2", [P, DEEP, J])
        rec = RecordScatter(nc, g, s, recs, 4 * CHUNKS)
        loaded = [s.sem(f"loaded{j}") for j in range(DEEP)]
        hx_loaded = [s.sem(f"hx_loaded{j}") for j in range(DEEP)]
        stored = [s.sem(f"stored{j}") for j in range(DEEP)]
        divided, summed, squared, reduced = s.sem("divided"), s.sem("summed"), s.sem("squared"), s.sem("reduced")
        rooted, rsigma, scaled = s.sem("rooted"), s.sem("rsigma"), s.sem("scaled")
        gained, shifted, residual = s.sem("gained"), s.sem("shifted"), s.sem("residual")
        joined, meaned, mean_neg, centred = s.sem("joined"), s.sem("meaned"), s.sem("mean_neg"), s.sem("centred")
        squared2, reduced2, rooted2 = s.sem("squared2"), s.sem("reduced2"), s.sem("rooted2")
        rsigma2, out_ready = s.sem("rsigma2"), s.sem("out_ready")
        block = s.block()

        @block.sync
        def _(sp):
            def load(c, j, n, old):
                if old:
                    sp.wait_ge(summed, c - DEEP + 1)
                sp.dma_start(tin[0:n, j, :], tile_rows(table, c * CH, n * J)).then_inc(loaded[j], 16)
                sp.dma_start(rin[0:n, j, :], tile_rows(lin, c * CH, n * J)).then_inc(loaded[j], 16)

            def load_hx(c, j, n, old):
                if old:
                    sp.wait_ge(joined, c - DEEP + 1)
                sp.dma_start(hin[0:n, j, :], tile_rows(h1, c * CH, n * J)).then_inc(hx_loaded[j], 16)
                sp.dma_start(xin[0:n, j, :], tile_rows(x, c * CH, n * J)).then_inc(hx_loaded[j], 16)

            def store(c, j, n, old):
                sp.wait_ge(out_ready, c + 1)
                sp.dma_start(tile_rows(x1_out, c * CH, n * J), out[0:n, j, :]).then_inc(stored[j], 16)

            over_chunks(sp, [(load, 0), (store, 5), (load_hx, 1)])
            for j in range(DEEP):
                sp.wait_ge(stored[j], 16 * len(range(j, CHUNKS, DEEP)))

        @block.vector
        def _(dve):
            def add_up(c, j, n, old):
                dve.wait_ge(loaded[j], full(c, j, 32))
                if old:
                    dve.wait_ge(out_ready, c - DEEP + 1)
                nc.vector.tensor_tensor(wide(a[:, j, :], n), wide(tin[:, j, :], n),
                                        bc(g.inv[0:n, ds(c * J, J)], [n, J, D], 2), ALU.mult).then_inc(divided, 1)
                dve.wait_ge(divided, c + 1)
                nc.vector.tensor_tensor(a[0:n, j, :], a[0:n, j, :], rin[0:n, j, :], ALU.add).then_inc(summed, 1)

            def variance(c, j, n, old):
                dve.wait_ge(squared, c + 1)
                nc.vector.tensor_reduce(var[0:n, j, :], wide(sq[:, j % 2, :], n), AX.X, ALU.add).then_inc(reduced, 1)

            def scale(c, j, n, old):
                dve.wait_ge(rooted, c + 1)
                a3 = wide(a[:, j, :], n)
                nc.vector.reciprocal(var[0:n, j, :], var[0:n, j, :]).then_inc(rsigma, 1)
                dve.wait_ge(rsigma, c + 1)
                nc.vector.tensor_tensor(a3, a3, bc(var[0:n, j, :], [n, J, D], 2), ALU.mult).then_inc(scaled, 1)
                dve.wait_ge(scaled, c + 1)
                nc.vector.tensor_tensor(a3, a3, bc(g.vec("g2")[0:n, :], [n, J, D], 1), ALU.mult).then_inc(gained, 1)

            def join(c, j, n, old):
                dve.wait_ge(shifted, c + 1)
                dve.wait_ge(residual, c + 1)
                nc.vector.scalar_tensor_tensor(a[0:n, j, :], a[0:n, j, :], 0.0, xin[0:n, j, :], ALU.max,
                                               ALU.add).then_inc(joined, 1)
                dve.wait_ge(joined, c + 1)
                a3 = wide(a[:, j, :], n)
                nc.vector.tensor_reduce(mean[0:n, j, :], a3, AX.X, ALU.add).then_inc(meaned, 1)
                dve.wait_ge(meaned, c + 1)
                nc.vector.tensor_scalar(mean[0:n, j, :], mean[0:n, j, :], 1.0 / D, None, ALU.mult).then_inc(mean_neg, 1)
                dve.wait_ge(mean_neg, c + 1)
                nc.vector.tensor_tensor(a3, a3, bc(mean[0:n, j, :], [n, J, D], 2), ALU.subtract).then_inc(centred, 1)

            def variance2(c, j, n, old):
                dve.wait_ge(squared2, c + 1)
                nc.vector.tensor_reduce(var2[0:n, j, :], wide(sq2[:, j % 2, :], n), AX.X,
                                        ALU.add).then_inc(reduced2, 1)

            def scale2(c, j, n, old):
                dve.wait_ge(rooted2, c + 1)
                nc.vector.reciprocal(var2[0:n, j, :], var2[0:n, j, :]).then_inc(rsigma2, 1)
                dve.wait_ge(rsigma2, c + 1)
                if old:
                    dve.wait_ge(stored[j], full(c, j, 16) - 16)
                nc.vector.tensor_tensor(wide(out[:, j, :], n), wide(a[:, j, :], n),
                                        bc(var2[0:n, j, :], [n, J, D], 2), ALU.mult).then_inc(out_ready, 1)

            over_chunks(dve, [(rec.stage(dve), 0), (variance2, 3), (variance, 1), (scale2, 3), (add_up, 0),
                              (scale, 1), (join, 2)])

        @block.scalar
        def _(act):
            def square(c, j, n, old):
                act.wait_ge(summed, c + 1)
                if old:
                    act.wait_ge(reduced, c - 1)
                nc.scalar.activation(sq[0:n, j % 2, :], a[0:n, j, :], ACT.Square).then_inc(squared, 1)

            def root(c, j, n, old):
                act.wait_ge(reduced, c + 1)
                nc.scalar.activation(var[0:n, j, :], var[0:n, j, :], ACT.Sqrt, bias=g.eps[0:n, :],
                                     scale=1.0 / D).then_inc(rooted, 1)

            def square2(c, j, n, old):
                act.wait_ge(centred, c + 1)
                if old:
                    act.wait_ge(reduced2, c - 1)
                nc.scalar.activation(sq2[0:n, j % 2, :], a[0:n, j, :], ACT.Square).then_inc(squared2, 1)

            def root2(c, j, n, old):
                act.wait_ge(reduced2, c + 1)
                nc.scalar.activation(var2[0:n, j, :], var2[0:n, j, :], ACT.Sqrt, bias=g.eps[0:n, :],
                                     scale=1.0 / D).then_inc(rooted2, 1)

            over_chunks(act, [(root2, 3), (root, 1), (square, 0), (square2, 2)])

        @block.gpsimd
        def _(pool):
            def add_residual(c, j, n, old):
                pool.wait_ge(hx_loaded[j], full(c, j, 32))
                nc.gpsimd.tensor_tensor(xin[0:n, j, :], xin[0:n, j, :], hin[0:n, j, :], ALU.add).then_inc(residual, 1)

            def shift(c, j, n, old):
                pool.wait_ge(gained, c + 1)
                a3 = wide(a[:, j, :], n)
                nc.gpsimd.tensor_tensor(a3, a3, bc(g.vec("be2")[0:n, :], [n, J, D], 1), ALU.add).then_inc(shifted, 1)

            over_chunks(pool, [(rec.scatter(pool), 0), (add_residual, 1), (shift, 1)])
            rec.wait_all(pool)


def reload_phase(nc, g, recs, dst2):
    s = Scope(nc, "re")
    with s:
        rec = s.sb("rec", [P, RTILES, 4])
        rows = s.sb("rows", [RTB, BLOCKS, P])
        ps_rows = s.ps("ps_rows", [RTB, BLOCKS, P])
        loaded, turned, copied, stored = s.sem("loaded"), s.sem("turned"), s.sem("copied"), s.sem("stored")
        steps = s.sem("steps")
        block = s.block()

        @block.sync
        def _(sp):
            sp.dma_start(rec[:, :, :].rearrange("p t f -> p (t f)"),
                         recs.rearrange("(p t) f -> p (t f)", p=P)).then_inc(loaded, 16)
            sp.wait_ge(copied, 1)
            sp.dma_start(dst2.rearrange("(b r p) -> r b p", b=BLOCKS, p=P), rows[:, :, :]).then_inc(stored, 16)
            sp.wait_ge(stored, 16)

        @block.vector
        def _(dve):
            dve.wait_ge(loaded, 16)
            nc.vector.tensor_copy(g.dcol2[:, :], rec[:, :, 1]).then_inc(steps, 1)
            nc.vector.tensor_copy(g.srcidx2[:, :], rec[:, :, 0])
            nc.vector.tensor_copy(g.wcol2[:, :], rec[:, :, 2])
            dve.wait_ge(steps, 1)
            nc.vector.tensor_tensor(g.ddump2[:, :].rearrange("p (g j) -> p g j", j=2),
                                    bc(g.dumpcol[:, :], [P, RTILES // 2, 2], 1),
                                    g.dcol2[:, :].rearrange("p (g j) -> p g j", j=2), ALU.subtract)

        @block.tensor
        def _(pe):
            pe.wait_ge(steps, 1)
            for b in range(BLOCKS):
                last = nc.tensor.transpose(ps_rows[:, b, :], g.dcol2[:, b * RTB:(b + 1) * RTB], g.ident[:, :])
            last.then_inc(turned, 1)

        @block.scalar
        def _(act):
            act.wait_ge(turned, 1)
            nc.scalar.copy(rows[:, :, :], ps_rows[:, :, :]).then_inc(copied, 1)


def stats_phase(nc, g, table, lin, y_out):
    s = Scope(nc, "st")
    with s:
        W = J * D
        tin = s.sb("tin", [P, DEEP, W])
        rin = s.sb("rin", [P, DEEP, W])
        y = s.sb("y", [P, DEEP, W])
        sq = s.sb("sq", [P, DEEP, W])
        acc = s.sb("acc", [P, W])
        acc2 = s.sb("acc2", [P, W])
        both = s.sb("both", [P, 2, D])
        mean = s.sb("mean", [P, D])
        var = s.sb("var", [P, D])
        m2 = s.sb("m2", [P, D])
        ps_sum = s.ps("ps_sum", [P, 2, D])
        t_loaded = [s.sem(f"t_loaded{j}") for j in range(DEEP)]
        r_loaded = [s.sem(f"r_loaded{j}") for j in range(DEEP)]
        stored = [s.sem(f"stored{j}") for j in range(DEEP)]
        cleared, clipped, y_ready, squared = s.sem("cleared"), s.sem("clipped"), s.sem("y_ready"), s.sem("squared")
        acc_added, acc2_added = s.sem("acc_added"), s.sem("acc2_added")
        folded, totalled, rooted, steps = s.sem("folded"), s.sem("totalled"), s.sem("rooted"), s.sem("steps")
        var_ready = s.sem("var_ready")
        block = s.block()

        @block.sync
        def _(sp):
            def load(c, j, n, old):
                if old:
                    sp.wait_ge(y_ready, c - DEEP + 1)
                sp.dma_start(tin[0:n, j, :], tile_rows(table, c * CH, n * J)).then_inc(t_loaded[j], 16)
                sp.dma_start(rin[0:n, j, :], tile_rows(lin, c * CH, n * J)).then_inc(r_loaded[j], 16)

            def store(c, j, n, old):
                sp.wait_ge(y_ready, c + 1)
                sp.dma_start(tile_rows(y_out, c * CH, n * J), y[0:n, j, :]).then_inc(stored[j], 16)

            over_chunks(sp, [(load, 0), (store, 2)])
            for j in range(DEEP):
                sp.wait_ge(stored[j], 16 * len(range(j, CHUNKS, DEEP)))

        @block.scalar
        def _(act):
            def clip(c, j, n, old):
                act.wait_ge(r_loaded[j], full(c, j, 16))
                nc.scalar.activation(rin[0:n, j, :], rin[0:n, j, :], ACT.Relu).then_inc(clipped, 1)

            def square(c, j, n, old):
                act.wait_ge(y_ready, c + 1)
                if old:
                    act.wait_ge(acc2_added, c - DEEP + 1)
                nc.scalar.activation(sq[0:n, j, :], y[0:n, j, :], ACT.Square).then_inc(squared, 1)

            over_chunks(act, [(clip, 0), (square, 1)])
            act.wait_ge(var_ready, 1)
            nc.scalar.activation(var[:, :], var[:, :], ACT.Sqrt, bias=g.eps[:, :], scale=1.0).then_inc(rooted, 1)

        @block.gpsimd
        def _(pool):
            nc.gpsimd.memset(acc[:, :], 0.0).then_inc(acc_added, 1)

            def add(c, j, n, old):
                pool.wait_ge(y_ready, c + 1)
                pool.wait_ge(acc_added, c + 1)
                nc.gpsimd.tensor_tensor(acc[0:n, :], acc[0:n, :], y[0:n, j, :], ALU.add).then_inc(acc_added, 1)

            over_chunks(pool, [(add, 1)])

        @block.vector
        def _(dve):
            nc.vector.memset(acc2[:, :], 0.0).then_inc(acc2_added, 1)

            def make_y(c, j, n, old):
                dve.wait_ge(t_loaded[j], full(c, j, 16))
                dve.wait_ge(clipped, c + 1)
                if old:
                    dve.wait_ge(stored[j], full(c, j, 16) - 16)
                    dve.wait_ge(acc_added, c - DEEP + 2)
                    dve.wait_ge(squared, c - DEEP + 1)
                nc.vector.scalar_tensor_tensor(y[0:n, j, :], tin[0:n, j, :], 0.0, rin[0:n, j, :], ALU.max,
                                               ALU.add).then_inc(y_ready, 1)

            def add_squares(c, j, n, old):
                dve.wait_ge(squared, c + 1)
                dve.wait_ge(acc2_added, c + 1)
                nc.vector.tensor_tensor(acc2[0:n, :], acc2[0:n, :], sq[0:n, j, :], ALU.add).then_inc(acc2_added, 1)

            over_chunks(dve, [(make_y, 0), (add_squares, 2)])
            step = Chain(dve, steps)
            dve.wait_ge(acc_added, CHUNKS + 1)
            dve.wait_ge(acc2_added, CHUNKS + 1)
            nc.vector.tensor_reduce(both[:, 0, :], acc[:, :].rearrange("p (j d) -> p d j", d=D), AX.X, ALU.add)
            nc.vector.tensor_reduce(both[:, 1, :], acc2[:, :].rearrange("p (j d) -> p d j", d=D), AX.X,
                                    ALU.add).then_inc(folded, 1)
            dve.wait_ge(totalled, 1)
            step(nc.vector.tensor_scalar(mean[:, :], ps_sum[:, 0, :], 1.0 / N, None, ALU.mult))
            step(nc.vector.tensor_tensor(m2[:, :], mean[:, :], mean[:, :], ALU.mult))
            nc.vector.scalar_tensor_tensor(var[:, :], ps_sum[:, 1, :], 1.0 / N, m2[:, :], ALU.mult,
                                           ALU.subtract).then_inc(var_ready, 1)
            dve.wait_ge(rooted, 1)
            step(nc.vector.reciprocal(m2[:, :], var[:, :]))
            step(nc.vector.tensor_tensor(g.bnab[:, 0, :], g.vec("gamma"), m2[:, :], ALU.mult))
            step(nc.vector.tensor_tensor(mean[:, :], mean[:, :], g.bnab[:, 0, :], ALU.mult))
            nc.vector.tensor_tensor(g.bnab[:, 1, :], g.vec("beta"), mean[:, :], ALU.subtract)

        @block.tensor
        def _(pe):
            pe.wait_ge(folded, 1)
            nc.tensor.matmul(ps_sum[:, :, :], g.onesf[:, :], both[:, :, :], start=True, stop=True).then_inc(totalled, 1)


def final_phase(nc, g, x1, y, out_dram):
    s = Scope(nc, "fi")
    with s:
        W = J * D
        xin = s.sb("xin", [P, DEEP, W])
        a = s.sb("a", [P, DEEP, W])
        sq = s.sb("sq", [P, DEEP, W])
        out = s.sb("out", [P, DEEP, W])
        mean = s.sb("mean", [P, DEEP, J])
        var = s.sb("var", [P, DEEP, J])
        y_loaded = [s.sem(f"y_loaded{j}") for j in range(DEEP)]
        x_loaded = [s.sem(f"x_loaded{j}") for j in range(DEEP)]
        stored = [s.sem(f"stored{j}") for j in range(DEEP)]
        gained, shifted, joined, meaned = s.sem("gained"), s.sem("shifted"), s.sem("joined"), s.sem("meaned")
        mean_made, centred, squared = s.sem("mean_made"), s.sem("centred"), s.sem("squared")
        reduced, rooted, rsigma, out_ready = s.sem("reduced"), s.sem("rooted"), s.sem("rsigma"), s.sem("out_ready")
        block = s.block()

        @block.sync
        def _(sp):
            def load(c, j, n, old):
                if old:
                    sp.wait_ge(out_ready, c - DEEP + 1)
                sp.dma_start(a[0:n, j, :], tile_rows(y, c * CH, n * J)).then_inc(y_loaded[j], 16)
                sp.dma_start(xin[0:n, j, :], tile_rows(x1, c * CH, n * J)).then_inc(x_loaded[j], 16)

            def store(c, j, n, old):
                sp.wait_ge(out_ready, c + 1)
                sp.dma_start(tile_rows(out_dram, c * CH, n * J), out[0:n, j, :]).then_inc(stored[j], 16)

            over_chunks(sp, [(store, 4), (load, 0)])
            for j in range(DEEP):
                sp.wait_ge(stored[j], 16 * len(range(j, CHUNKS, DEEP)))

        @block.gpsimd
        def _(pool):
            def affine(c, j, n, old):
                pool.wait_ge(y_loaded[j], full(c, j, 16))
                a3 = wide(a[:, j, :], n)
                nc.gpsimd.tensor_tensor(a3, a3, bc(g.bnab[0:n, 0, :], [n, J, D], 1), ALU.mult).then_inc(gained, 1)
                pool.wait_ge(gained, c + 1)
                nc.gpsimd.tensor_tensor(a3, a3, bc(g.bnab[0:n, 1, :], [n, J, D], 1), ALU.add).then_inc(shifted, 1)

            over_chunks(pool, [(affine, 0)])

        @block.vector
        def _(dve):
            def join(c, j, n, old):
                dve.wait_ge(x_loaded[j], full(c, j, 16))
                dve.wait_ge(shifted, c + 1)
                a3 = wide(a[:, j, :], n)
                nc.vector.tensor_tensor(a[0:n, j, :], a[0:n, j, :], xin[0:n, j, :], ALU.add).then_inc(joined, 1)
                dve.wait_ge(joined, c + 1)
                nc.vector.tensor_reduce(mean[0:n, j, :], a3, AX.X, ALU.add).then_inc(meaned, 1)
                dve.wait_ge(meaned, c + 1)
                nc.vector.tensor_scalar(mean[0:n, j, :], mean[0:n, j, :], 1.0 / D, None,
                                        ALU.mult).then_inc(mean_made, 1)
                dve.wait_ge(mean_made, c + 1)
                nc.vector.tensor_tensor(a3, a3, bc(mean[0:n, j, :], [n, J, D], 2), ALU.subtract).then_inc(centred, 1)

            def variance(c, j, n, old):
                dve.wait_ge(squared, c + 1)
                nc.vector.tensor_reduce(var[0:n, j, :], wide(sq[:, j, :], n), AX.X, ALU.add).then_inc(reduced, 1)

            def scale(c, j, n, old):
                dve.wait_ge(rooted, c + 1)
                nc.vector.reciprocal(var[0:n, j, :], var[0:n, j, :]).then_inc(rsigma, 1)
                dve.wait_ge(rsigma, c + 1)
                if old:
                    dve.wait_ge(stored[j], full(c, j, 16) - 16)
                nc.vector.tensor_tensor(wide(out[:, j, :], n), wide(a[:, j, :], n),
                                        bc(var[0:n, j, :], [n, J, D], 2), ALU.mult).then_inc(out_ready, 1)

            over_chunks(dve, [(variance, 1), (join, 0), (scale, 1)])

        @block.scalar
        def _(act):
            def square(c, j, n, old):
                act.wait_ge(centred, c + 1)
                if old:
                    act.wait_ge(reduced, c - DEEP + 1)
                nc.scalar.activation(sq[0:n, j, :], a[0:n, j, :], ACT.Square).then_inc(squared, 1)

            def root(c, j, n, old):
                act.wait_ge(reduced, c + 1)
                nc.scalar.activation(var[0:n, j, :], var[0:n, j, :], ACT.Sqrt, bias=g.eps[0:n, :],
                                     scale=1.0 / D).then_inc(rooted, 1)

            over_chunks(act, [(root, 1), (square, 0)])


def gnn_kernel(nc, io, out):
    def table(name, shape, dt=fp32):
        return nc.dram_tensor(name, shape, dt).ap()

    dr = {"t1": table("sums1", [TROWS, D + 1]), "t2": table("sums2", [TROWS, D]), "t3": table("sums3", [TROWS, D]),
          "lin1": table("lin1", [N, D]), "lin2": table("lin2", [N, D]), "lin3": table("lin3", [N, D]),
          "h1": table("h1", [N, D]), "x1": table("x1", [N, D]), "y": table("y", [N, D]),
          "recs": table("recs", [P * RTILES, 4]), "dst1": table("dst1", [TILES * P]),
          "dst2": table("dst2", [RTILES * P]), "wrel": table("wrel", [R * D, D]),
          "ttype": table("ttype", [BLOCKS * P], i32)}
    top = Scope(nc, "g")
    with top:
        g = Persistent(top)
        setup_phase(nc, g, io, dr)
        sort_phase(nc, g, dr)
        edge_phase(nc, g, "e1", io["x"], dr["dst1"], g.srcidx, g.dcol, g.ddump, dr["t1"], D + 1, g.wst1,
                   dr["lin1"], g.wblk[:, 0, :], g.vec("b1"), SUPERS)
        norm_phase1(nc, g, dr["t1"], dr["lin1"], dr["h1"], dr["recs"])
        edge_phase(nc, g, "e2", dr["h1"], dr["dst1"], g.srcidx, g.dcol, g.ddump, dr["t2"], D, g.wst2,
                   dr["lin2"], g.wblk[:, 1, :], g.vec("b2"), SUPERS)
        norm_phase2(nc, g, dr["t2"], dr["lin2"], dr["h1"], io["x"], dr["x1"], dr["recs"])
        reload_phase(nc, g, dr["recs"], dr["dst2"])
        edge_phase(nc, g, "e3", dr["x1"], dr["dst2"], g.srcidx2, g.dcol2, g.ddump2, dr["t3"], D, None,
                   dr["lin3"], g.wblk[:, 2, :], g.vec("res_b"), RSUPERS, wcol=g.wcol2, wrel=dr["wrel"],
                   ttype=dr["ttype"])
        stats_phase(nc, g, dr["t3"], dr["lin3"], dr["y"])
        final_phase(nc, g, dr["x1"], dr["y"], out)


_INS = ["x", "src", "dst", "edge_type_64", "edge_weight1", "L0_gnn_W1l", "L0_gnn_b1l", "L0_gnn_W1r", "L0_gnn_g1",
        "L0_gnn_beta1", "L0_gnn_W2l", "L0_gnn_b2l", "L0_gnn_W2r", "L0_gnn_g2", "L0_gnn_beta2", "L1_gnn_basis",
        "L1_gnn_comp", "L1_gnn_bias", "L1_gnn_res_w", "L1_gnn_res_b", "L1_gnn_gamma", "L1_gnn_beta"]


def kernel(**inputs):
    import numpy as _np
    import concourse.bacc as _bacc
    from concourse import mybir as _mybir
    from concourse.bass_utils import run_bass_kernel_spmd as _run

    nc = _bacc.Bacc("TRN2", target_bir_lowering=False, num_devices=1)
    arrays, io = {}, {}
    for name in _INS:
        a = _np.ascontiguousarray(inputs[name])
        arrays[f"in_{name}_dram"] = a
        io[name] = nc.dram_tensor(f"in_{name}_dram", a.shape, _mybir.dt.from_np(a.dtype), kind="ExternalInput").ap()
    out = nc.dram_tensor("out_0_dram", (N, D), _mybir.dt.float32, kind="ExternalOutput").ap()
    gnn_kernel(nc, io, out)
    r = _run(nc, [arrays], core_ids=[0])
    return r.results[0]["out_0_dram"]
```

```python
import concourse.bass as bass
from concourse import mybir
from contextlib import ExitStack

N = 100000
E = 50000
D = 64
R = 64
B = 64
EPS = 1e-5
P = 128

TILES = -(-E // (8 * P)) * 8
LAST_TILE = E // P
LAST_ROWS = E - LAST_TILE * P
BLOCKS = 4
TB = TILES // BLOCKS
SUPERS = TILES // 8
HALF = P // 2
RTILES = -(-((E - R) // HALF + R) // 16) * 8
HB = -(-2 * RTILES // P)
RSUPERS = RTILES // 8
RTB = RTILES // BLOCKS

J = 16
CH = P * J
CHUNKS = -(-N // CH)
PLAST = (N - (CHUNKS - 1) * CH) // J
assert PLAST * J == N - (CHUNKS - 1) * CH and CHUNKS == SUPERS and TILES % 8 == 0

TRASH = N
DUMP = N + 1
TROWS = CHUNKS * CH
assert TROWS >= DUMP + 2 * P

fp32 = mybir.dt.float32
bf16 = mybir.dt.bfloat16
i32 = mybir.dt.int32
ALU = mybir.AluOpType
ACT = mybir.ActivationFunctionType
AX = mybir.AxisListType
ds = bass.ds

VECS = ["b1", "g1", "be1", "b2", "g2", "be2", "bias", "res_b", "gamma", "beta"]


class Scope:

    def __init__(self, nc, tag):
        self.nc, self.tag, self.stack, self.sems = nc, tag, ExitStack(), []

    def sb(self, name, shape, dt=fp32):
        return self.stack.enter_context(self.nc.sbuf_tensor(f"{self.tag}_{name}", shape, dt))

    def ps(self, name, shape, dt=fp32):
        return self.stack.enter_context(self.nc.psum_tensor(f"{self.tag}_{name}", shape, dt))

    def sem(self, name):
        self.sems.append(self.nc.alloc_semaphore(f"{self.tag}_{name}"))
        return self.sems[-1]

    def block(self):
        return self.stack.enter_context(self.nc.Block())

    def __enter__(self):
        return self

    def __exit__(self, *error):
        self.stack.close()
        if self.sems:
            self.nc.clear_and_free_semaphores(self.sems)
            self.nc.all_engine_barrier()
        return False


def tile_rows(tensor, first, count, partitions=P, each=J):
    return tensor[ds(first, count), :].rearrange("(p j) d -> p (j d)", j=each)


def bc(ap, shape, axis):
    return ap.unsqueeze(axis).to_broadcast(shape)


class Chain:

    def __init__(self, eng, sem):
        self.eng, self.sem, self.n = eng, sem, 0

    def __call__(self, ins):
        self.n += 1
        ins.then_inc(self.sem, 1)
        self.eng.wait_ge(self.sem, self.n)


class Persistent:

    def __init__(self, s):
        self.ident = s.sb("ident", [P, P])
        self.onesf = s.sb("onesf", [P, P])
        self.onesb = s.sb("onesb", [P, P], bf16)
        self.before = s.sb("before", [P, 2, 2 * P])
        self.beforeb = s.sb("beforeb", [P, P], bf16)
        self.iota_rel = s.sb("iota_rel", [P, R])
        self.iota_half = s.sb("iota_half", [P, HB])
        self.dumpcol = s.sb("dumpcol", [P, 2])
        self.srcidx = s.sb("srcidx", [P, TILES], i32)
        self.dcol = s.sb("dcol", [P, TILES])
        self.ddump = s.sb("ddump", [P, TILES])
        self.rec = s.sb("rec", [P, TILES, 4])
        self.posidx = s.sb("posidx", [P, TILES], i32)
        self.wst1 = s.sb("wst1", [P, D])
        self.wst2 = s.sb("wst2", [P, D])
        self.wblk = s.sb("wblk", [P, 4, P])
        self.gcols = s.sb("gcols", [P, 4])
        self.vecs = s.sb("vecs", [P, len(VECS), D])
        self.eps = s.sb("eps", [P, 1])
        self.inv = s.sb("inv", [P, CHUNKS * J])
        self.bnab = s.sb("bnab", [P, 2, D])
        self.zero = s.sb("zero", [P, J * (D + 1)])
        self.biases = s.sb("biases", [P, J, D])
        self.srcidx2 = s.sb("srcidx2", [P, RTILES], i32)
        self.dcol2 = s.sb("dcol2", [P, RTILES])
        self.ddump2 = s.sb("ddump2", [P, RTILES])
        self.wcol2 = s.sb("wcol2", [P, RTILES])

    def vec(self, name):
        return self.vecs[:, VECS.index(name), :]


class Sort:

    def __init__(self, s):
        self.onehot = s.sb("onehot", [P, TILES, R], bf16)
        self.base = s.sb("base", [P, R])
        self.pos = s.sb("pos", [P, TILES])


def setup_phase(nc, g, sort, io, dr, t1_filled):
    s = Scope(nc, "su")
    with s:
        rows_i = s.sb("rows_i", [TB, 3, BLOCKS, P], i32)
        rows_f = s.sb("rows_f", [TB, 4, BLOCKS, P])
        wnat = s.sb("wnat", [D, 5, 2 * D])
        cent = s.sb("cent", [D, D])
        comp = s.sb("comp", [R, B])
        compT = s.sb("compT", [B, R])
        basis = s.sb("basis", [B, D * D])
        wrel = s.sb("wrel", [R, D * D])
        bsum = s.sb("bsum", [P, 2])
        recpad = s.sb("recpad", [P, RTILES, 4])
        ps_edge = [s.ps(f"ps_edge{a}", [P, TILES]) for a in range(4)]
        ps_w = s.ps("ps_w", [P, 5, D])
        ps_ct = s.ps("ps_ct", [B, R])
        ps_rel = s.ps("ps_rel", [R, 512])
        ps_count = s.ps("ps_count", [P, 8, R])
        tcol = s.sb("tcol", [P, TILES])
        count = s.sb("count", [P, R])
        count_i = s.sb("count_i", [P, R], i32)
        halves_i = s.sb("halves_i", [P, R], i32)
        halves_f = s.sb("halves_f", [P, R])
        hend = s.sb("hend", [P, R])
        cmp = s.sb("cmp", [P, HB, R])
        htype = s.sb("htype", [P, HB])
        htype_i = s.sb("htype_i", [P, HB], i32)

        rows_padded = s.sem("rows_padded")
        recpad_set = s.sem("recpad_set")
        edges_loaded = s.sem("edges_loaded")
        weights_loaded = s.sem("weights_loaded")
        vectors_loaded = s.sem("vectors_loaded")
        basis_loaded = s.sem("basis_loaded")
        pool_steps = s.sem("pool_steps")
        consts_made = s.sem("consts_made")
        centering_made = s.sem("centering_made")
        rows_converted = s.sem("rows_converted")
        columns_made = s.sem("columns_made")
        weights_turned = s.sem("weights_turned")
        comp_turned = s.sem("comp_turned")
        comp_copied = s.sem("comp_copied")
        rel_made = s.sem("rel_made")
        rel_copied = s.sem("rel_copied")
        dve_steps = s.sem("dve_steps")
        stored = s.sem("stored")
        zero_set = s.sem("zero_set")
        onehot_made = s.sem("onehot_made")
        counted = s.sem("counted")
        types_made = s.sem("types_made")
        block = s.block()

        @block.sync
        def _(sp):
            sp.wait_ge(rows_padded, 4)
            full = 3 * TB * P
            for k, name in enumerate(["src", "dst", "edge_type_64", "edge_weight1"]):
                flat = io[name] if k < 3 else io[name].rearrange("e o -> (e o)")
                rows = rows_i[:, k] if k < 3 else rows_f[:, 3]
                sp.dma_start(rows[:, 0:3, :],
                             flat[0:full].rearrange("(b r p) -> r b p", b=3, p=P)).then_inc(edges_loaded, 16)
                rest = LAST_TILE - 3 * TB
                sp.dma_start(rows[0:rest, 3, :],
                             flat[full:full + rest * P].rearrange("(r p) -> r p", p=P)).then_inc(edges_loaded, 16)
                sp.dma_start(rows[rest:rest + 1, 3, 0:LAST_ROWS],
                             flat[full + rest * P:E].rearrange("(r p) -> r p", p=LAST_ROWS)).then_inc(edges_loaded, 16)
            for k, name in enumerate(["L0_gnn_W1l", "L0_gnn_W2l", "L0_gnn_W1r", "L0_gnn_W2r", "L1_gnn_res_w"]):
                for h in range(2):
                    sp.dma_start(wnat[:, k, h * D:(h + 1) * D], io[name][:, :]).then_inc(weights_loaded, 16)
            sp.dma_start(comp[:, :], io["L1_gnn_comp"][:, :]).then_inc(basis_loaded, 16)
            sp.dma_start(basis[:, :], io["L1_gnn_basis"].rearrange("b i o -> b (i o)")).then_inc(basis_loaded, 16)
            for k, name in enumerate(["L0_gnn_b1l", "L0_gnn_g1", "L0_gnn_beta1", "L0_gnn_b2l", "L0_gnn_g2",
                                      "L0_gnn_beta2", "L1_gnn_bias", "L1_gnn_res_b", "L1_gnn_gamma",
                                      "L1_gnn_beta"]):
                sp.dma_start(g.vecs[:, k, :],
                             io[name].unsqueeze(0).to_broadcast([P, D])).then_inc(vectors_loaded, 16)
            for k, name in enumerate(["L0_gnn_g1", "L0_gnn_beta1", "L0_gnn_g2", "L0_gnn_beta2"]):
                for h in range(2):
                    sp.dma_start(g.gcols[h * D:(h + 1) * D, k:k + 1], io[name].unsqueeze(1)).then_inc(stored, 16)
            sp.wait_ge(recpad_set, 2)
            sp.dma_start(dr["recs"].rearrange("(p t) f -> p (t f)", p=P),
                         recpad[:, :, :].rearrange("p t f -> p (t f)")).then_inc(stored, 16)
            sp.wait_ge(rows_converted, 1)
            sp.dma_start(dr["dst1"].rearrange("(b r p) -> r b p", b=BLOCKS, p=P),
                         rows_f[:, 1]).then_inc(stored, 16)
            sp.wait_ge(rel_copied, 8)
            sp.dma_start(dr["wrel"].rearrange("(r i) o -> r (i o)", i=D), wrel[:, :]).then_inc(stored, 16)
            sp.wait_ge(types_made, 1)
            with nc.allow_non_contiguous_dma(reason="some small words, once"):
                sp.dma_start(dr["htype"].rearrange("(b p) -> p b", p=P), htype_i[:, :]).then_inc(stored, 16)
            sp.wait_ge(stored, 16 * 12)

        @block.gpsimd
        def _(pool):
            step = Chain(pool, pool_steps)
            step(nc.gpsimd.memset(g.ident[:, :], 0.0))
            step(nc.gpsimd.affine_select(out=g.ident[:, :], in_=g.ident[:, :], compare_op=ALU.not_equal, fill=1.0,
                                         base=0, pattern=[[-1, P]], channel_multiplier=1))
            step(nc.gpsimd.memset(g.before[:, :, :], 1.0))
            for i in range(2):
                nc.gpsimd.affine_select(out=g.before[:, i, :], in_=g.before[:, i, :], compare_op=ALU.is_gt, fill=0.0,
                                        base=-P * i, pattern=[[1, 2 * P]], channel_multiplier=-1)
            nc.gpsimd.iota(g.iota_rel[:, :], [[1, R]], base=0, channel_multiplier=0,
                           allow_small_or_imprecise_dtypes=True)
            nc.gpsimd.iota(g.iota_half[:, :], [[P, HB]], base=0, channel_multiplier=1,
                           allow_small_or_imprecise_dtypes=True)
            nc.gpsimd.iota(g.dumpcol[:, :], [[P, 2]], base=DUMP, channel_multiplier=1,
                           allow_small_or_imprecise_dtypes=True).then_inc(consts_made, 1)

        @block.tensor
        def _(pe):
            pe.wait_ge(consts_made, 1)
            pe.wait_ge(rows_converted, 1)
            for a in range(4):
                for b in range(BLOCKS):
                    last = nc.tensor.transpose(ps_edge[a][:, b * TB:(b + 1) * TB], rows_f[:, a, b, :],
                                               g.ident[0:TB, 0:TB])
            last.then_inc(columns_made, 1)
            pe.wait_ge(weights_loaded, 160)
            pe.wait_ge(centering_made, 1)
            for k in range(5):
                last = nc.tensor.matmul(ps_w[:, k, :], wnat[:, k, :], cent[:, :] if k < 4 else g.ident[0:D, 0:D],
                                        start=True, stop=True)
            last.then_inc(weights_turned, 1)
            pe.wait_ge(basis_loaded, 32)
            nc.tensor.transpose(ps_ct[:, :], comp[:, :], g.ident[0:R, 0:R]).then_inc(comp_turned, 1)
            pe.wait_ge(comp_copied, 1)
            for k in range(8):
                if k >= 1:
                    pe.wait_ge(rel_copied, k)
                nc.tensor.matmul(ps_rel[:, :], compT[:, :], basis[:, k * 512:(k + 1) * 512],
                                 start=True, stop=True).then_inc(rel_made, 1)
            for q in range(4):
                pe.wait_ge(onehot_made, q + 1)
            for b in range(SUPERS):
                last = nc.tensor.matmul(ps_count[:, :, :], g.onesb[:, :], sort.onehot[:, 8 * b:8 * b + 8, :],
                                        start=(b == 0), stop=(b == SUPERS - 1))
            last.then_inc(counted, 1)

        @block.scalar
        def _(act):
            act.wait_ge(zero_set, 1)
            with act.Fori(0, CHUNKS) as c:
                act.dma_start(tile_rows(dr["t1"], c * CH, CH), g.zero[:, :]).then_inc(t1_filled, 16)
            act.wait_ge(comp_turned, 1)
            nc.scalar.copy(compT[:, :], ps_ct[:, :]).then_inc(comp_copied, 1)
            for k in range(8):
                act.wait_ge(rel_made, k + 1)
                nc.scalar.copy(wrel[:, k * 512:(k + 1) * 512], ps_rel[:, :]).then_inc(rel_copied, 1)

        @block.vector
        def _(dve):
            step = Chain(dve, dve_steps)
            nc.vector.memset(g.zero[:, :], 0.0).then_inc(zero_set, 1)
            for k, pad in enumerate([0, TRASH, R]):
                nc.vector.memset(rows_i[:, k, 3, :], pad).then_inc(rows_padded, 1)
            nc.vector.memset(rows_f[:, 3, 3, :], 0.0).then_inc(rows_padded, 1)
            nc.vector.memset(recpad[:, :, :], 0.0).then_inc(recpad_set, 1)
            dve.wait_ge(recpad_set, 1)
            nc.vector.memset(recpad[:, :, 1:2], float(TRASH)).then_inc(recpad_set, 1)
            nc.vector.memset(g.onesf[:, :], 1.0)
            nc.vector.memset(g.onesb[:, :], 1.0)
            nc.vector.memset(g.eps[:, :], EPS)
            step(nc.vector.memset(g.wblk[:, :, :], 0.0))
            step(nc.vector.memset(g.rec[:, :, 3:4], 0.0))
            dve.wait_ge(edges_loaded, 12 * 16)
            nc.vector.tensor_copy(rows_f[:, 0:3], rows_i[:, :]).then_inc(rows_converted, 1)
            dve.wait_ge(consts_made, 1)
            nc.vector.tensor_scalar(cent[:, :], g.ident[0:D, 0:D], -1.0 / D, None, ALU.add).then_inc(centering_made, 1)
            for h in range(2):
                half = slice(h * D, (h + 1) * D)
                nc.vector.tensor_scalar(g.wblk[half, 3, half], g.ident[half, half], -1.0 / D, None, ALU.add)
            nc.vector.tensor_copy(g.beforeb[:, :], g.before[:, 0, 0:P])
            dve.wait_ge(vectors_loaded, 160)
            for j, name in enumerate(["b1", "b2"]):
                step(nc.vector.tensor_reduce(bsum[:, j:j + 1], g.vec(name), AX.X, ALU.add))
                step(nc.vector.tensor_scalar(bsum[:, j:j + 1], bsum[:, j:j + 1], -1.0 / D, None, ALU.mult))
                step(nc.vector.tensor_scalar(g.vec(name), g.vec(name), bsum[:, j:j + 1], None, ALU.add))
            dve.wait_ge(columns_made, 1)
            nc.vector.tensor_copy(g.srcidx[:, :], ps_edge[0][:, :])
            step(nc.vector.tensor_copy(g.dcol[:, :], ps_edge[1][:, :]))
            step(nc.vector.tensor_copy(tcol[:, :], ps_edge[2][:, :]))
            for q in range(4):
                t = slice(q * TB, (q + 1) * TB)
                nc.vector.tensor_tensor(sort.onehot[:, t, :], bc(g.iota_rel[:, :], [P, TB, R], 1),
                                        bc(tcol[:, t], [P, TB, R], 2), ALU.is_equal).then_inc(onehot_made, 1)
            for f, a in enumerate([0, 1, 3]):
                nc.vector.tensor_copy(g.rec[:, :, f], ps_edge[a][:, :])
            nc.vector.tensor_tensor(g.ddump[:, :].rearrange("p (g j) -> p g j", j=2),
                                    bc(g.dumpcol[:, :], [P, TILES // 2, 2], 1),
                                    g.dcol[:, :].rearrange("p (g j) -> p g j", j=2), ALU.subtract)
            dve.wait_ge(weights_turned, 1)
            nc.vector.tensor_copy(g.wst1[:, :], ps_w[:, 0, :])
            nc.vector.tensor_copy(g.wst2[:, :], ps_w[:, 1, :])
            for k in range(3):
                for h in range(2):
                    nc.vector.tensor_copy(g.wblk[h * D:(h + 1) * D, k, h * D:(h + 1) * D],
                                          ps_w[h * D:(h + 1) * D, 2 + k, :])
            nc.vector.tensor_copy(g.biases[:, :, :], bc(g.vec("bias"), [P, J, D], 1))
            dve.wait_ge(counted, 1)
            step(nc.vector.tensor_reduce(count[:, :], ps_count[:, :, :].rearrange("p k r -> p r k"), AX.X, ALU.add))
            step(nc.vector.tensor_scalar(count_i[:, :], count[:, :], float(HALF - 1), None, ALU.add))
            step(nc.vector.tensor_scalar(halves_i[:, :], count_i[:, :], 6, None, ALU.arith_shift_right))
            step(nc.vector.tensor_copy(halves_f[:, :], halves_i[:, :]))
            step(nc.vector.tensor_tensor_scan(hend[:, :], g.onesf[:, 0:R], halves_f[:, :], 0.0, ALU.mult, ALU.add))
            step(nc.vector.tensor_tensor(sort.base[:, :], hend[:, :], halves_f[:, :], ALU.subtract))
            step(nc.vector.tensor_scalar(sort.base[:, :], sort.base[:, :], float(HALF), None, ALU.mult))
            step(nc.vector.tensor_tensor(cmp[:, :, :], bc(g.iota_half[:, :], [P, HB, R], 2),
                                         bc(hend[:, :], [P, HB, R], 1), ALU.is_ge))
            step(nc.vector.tensor_reduce(htype[:, :], cmp[:, :, :], AX.X, ALU.add))
            nc.vector.tensor_scalar(htype_i[:, :], htype[:, :], float(R - 1), float(D), ALU.min,
                                    ALU.mult).then_inc(types_made, 1)


def edge_phase(nc, g, tag, x, dst_rows, srcidx, dcol, ddump, table, width, wst, lin_out, wblk, lin_bias, supers,
               wcol=None, wrel=None, htype=None, sort=None, table_filled=None, fill=None, x0=None, xc_out=None):
    s = Scope(nc, tag)
    relation = wrel is not None
    degree = width > D
    with s:
        XD = 0 if relation else D
        xg = s.sb("xg", [P, 4, 2, D + 2 * XD])
        xb = s.sb("xb", [P, 2, 2, P]) if relation else None
        gidx = s.sb("gidx", [P, 4, 2], i32)
        sidx = s.sb("sidx", [P, 4, 2], i32)
        first = s.sb("first", [P, 4, 2])
        drow = s.sb("drow", [P, 4, 2 * P])
        same = s.sb("same", [P, 4, 2, 2 * P])
        dup = s.sb("dup", [P, 4, 2, 2 * P], bf16)
        Z = 2 if relation else 1
        zs = s.sb("zs", [P, 2, Z, 2 * P])
        outs = s.sb("outs", [P, 4, 2, width])
        wslot = s.sb("wslot", [P, 4, 2, D]) if relation else None
        xf = s.sb("xf", [P, J // 2, P])
        xt = s.sb("xt", [P, 2, 512])
        lf = s.sb("lf", [P, J * D])
        xr = s.sb("xr", [P, J * D]) if xc_out is not None else None
        xmean = s.sb("xmean", [P, J]) if xc_out is not None else None
        if sort:
            work = s.sb("work", [P, 4, R])
            pos_i = s.sb("pos_i", [P, TILES], i32)
            tile_i = s.sb("tile_i", [P, TILES], i32)
            slot_i = s.sb("slot_i", [P, TILES], i32)
        ps_z = [s.ps(f"ps_z{a}", [P, Z, 2 * P]) for a in range(2)]
        ps_o = [s.ps(f"ps_o{a}", [P, 512]) for a in range(2)]
        ps_d = s.ps("ps_d", [P, 2])
        ps_r = s.ps("ps_r", [P, 5, R])
        ps_t = s.ps("ps_t", [P, 512])
        ps_l = s.ps("ps_l", [P, 512])

        drow_loaded = [s.sem(f"drow_loaded{q}") for q in range(4)]
        gathered = [s.sem(f"gathered{q}") for q in range(4)]
        w_loaded = [s.sem(f"w_loaded{q}") for q in range(4)] if relation else None
        scattered = s.sem("scattered")
        xg_zeroed = s.sem("xg_zeroed")
        gidx_ready = s.sem("gidx_ready")
        select_ready = s.sem("select_ready")
        dups_counted = s.sem("dups_counted")
        dups_read = s.sem("dups_read")
        sidx_ready = s.sem("sidx_ready")
        z_ready = s.sem("z_ready")
        spread = s.sem("spread") if relation else z_ready
        z_copied = s.sem("z_copied")
        out_ready = s.sem("out_ready")
        out_copied = s.sem("out_copied")
        pool_tick = s.sem("pool_tick")
        xf_loaded = s.sem("xf_loaded")
        turned = s.sem("turned")
        turned_copied = s.sem("turned_copied")
        lin_ready = s.sem("lin_ready")
        lin_done = s.sem("lin_done")
        lin_stored = s.sem("lin_stored")
        filled = s.sem("filled")
        ranked, rank_used, summed, masked = s.sem("ranked"), s.sem("rank_used"), s.sem("summed"), s.sem("masked")
        placed, last_steps = s.sem("placed"), s.sem("last_steps")
        xr_loaded, xc_summed, xc_meaned = s.sem("xr_loaded"), s.sem("xc_summed"), s.sem("xc_meaned")
        xc_scaled, xc_ready, xc_stored = s.sem("xc_scaled"), s.sem("xc_ready"), s.sem("xc_stored")
        block = s.block()
        last_super = supers - 1

        def over_supers(eng, body):
            cuts = sorted({0, 1, CHUNKS - 2, CHUNKS - 1, CHUNKS, CHUNKS + 1, last_super, supers})
            for a, b in zip(cuts, cuts[1:]):
                if b > supers:
                    break
                if b - a == 1:
                    body(a, a)
                else:
                    with eng.Fori(a, b) as c:
                        body(c, a)

        def parts(at):
            return 0 if not 0 <= at < CHUNKS else PLAST if at == CHUNKS - 1 else P

        def chunk(tensor, c, at):
            return tile_rows(tensor, c * CH, parts(at) * J)

        @block.sync
        def _(sp):
            sp.dma_start(xf[:, :, :].rearrange("p a b -> p (a b)"), chunk(x, 0, 0)).then_inc(xf_loaded, 16)
            if x0 is not None:
                sp.dma_start(xr[:, :], chunk(x0, 0, 0)).then_inc(xr_loaded, 16)

            def load_select(grp, q, old):
                if old:
                    sp.wait_ge(select_ready, grp - 3)
                src = dst_rows[ds(256 * grp, 256)].unsqueeze(0).to_broadcast([P, 256])
                sp.dma_start(drow[:, q, :], src).then_inc(drow_loaded[q], 16)

            def load_weights(grp, q, rels, old):
                if old:
                    sp.wait_ge(out_ready, grp - 3)
                for k in range(4):
                    rows = slice(k % 2 * D, (k % 2 + 1) * D)
                    sp.dma_start(wslot[rows, q, k // 2, :], wrel[ds(rels[k], D), :]).then_inc(w_loaded[q], 16)

            load_select(0, 0, False)
            load_select(1, 1, False)

            def body(c, at):
                if relation:
                    _, rels = nc.values_load_multi_w_load_instructions(
                        htype[ds(16 * c, 16)].unsqueeze(0), engines=(mybir.EngineType.SP,), min_val=0,
                        max_val=(R - 1) * D)
                for q in range(4):
                    if at < last_super or q < 2:
                        load_select(4 * c + q + 2, (q + 2) % 4, at > 0 or q >= 2)
                    if relation:
                        load_weights(4 * c + q, q, rels[4 * q:4 * q + 4], at > 0)
                    if q == 0 and x0 is not None and at > 0 and parts(at):
                        sp.wait_ge(xc_stored, 16 * c)
                        sp.dma_start(xr[0:parts(at), :], chunk(x0, c, at)).then_inc(xr_loaded, 16)
                    if q == 1 and fill is not None and parts(at):
                        sp.dma_start(tile_rows(fill[0], c * CH, CH), fill[1]).then_inc(filled, 16)
                    if q == 2 and parts(at + 1):
                        if x0 is not None:
                            sp.wait_ge(xc_summed, c + 1)
                        sp.wait_ge(turned, 2 * c + 2)
                        n = parts(at + 1)
                        sp.dma_start(xf[0:n, :, :].rearrange("p a b -> p (a b)"),
                                     chunk(x, c + 1, at + 1)).then_inc(xf_loaded, 16)

            over_supers(sp, body)
            if fill is not None:
                sp.wait_ge(filled, 16 * CHUNKS)
            if x0 is not None:
                sp.wait_ge(xc_stored, 16 * CHUNKS)
            sp.wait_ge(lin_stored, 16 * CHUNKS)

        @block.gpsimd
        def _(pool):
            def gather(c, q, used):
                grp = 4 * c + q
                pool.wait_ge(gidx_ready, grp + 1)
                if used:
                    pool.wait_ge(spread, grp - 3)
                else:
                    pool.wait_ge(xg_zeroed, 1)
                pool.sem_inc(pool_tick, 1)
                for i in range(2):
                    pool.indirect_dma_start(out=xg[:, q, i, XD:XD + D], out_offset=None, in_=x[:, :],
                                            in_offset=bass.IndirectOffsetOnAxis(ap=gidx[:, q, i:i + 1], axis=0)
                                            ).then_inc(gathered[q], 16)

            gather(0, 0, False)
            gather(0, 1, False)
            if table_filled is not None:
                pool.wait_ge(table_filled, 16 * CHUNKS)

            def body(c, at):
                for q in range(4):
                    if q < 2:
                        gather(c, q + 2, at > 0)
                    elif at < last_super:
                        gather(c + 1, q - 2, True)
                    grp = 4 * c + q
                    pool.wait_ge(sidx_ready, grp + 1)
                    pool.wait_ge(out_copied, grp + 1)
                    if at > 0 or q > 0:
                        pool.wait_ge(scattered, 32 * grp)
                    pool.sem_inc(pool_tick, 1)
                    for j in range(2):
                        pool.indirect_dma_start(out=table[:, :],
                                                out_offset=bass.IndirectOffsetOnAxis(ap=sidx[:, q, j:j + 1], axis=0),
                                                in_=outs[:, q, j, :], in_offset=None,
                                                compute_op=ALU.add).then_inc(scattered, 16)

            over_supers(pool, body)
            pool.wait_ge(scattered, 32 * 4 * supers)

        @block.vector
        def _(dve):
            nc.vector.memset((xb if relation else xg)[:, :, :, :], 0.0).then_inc(xg_zeroed, 1)

            def stage_gather(c, q, used):
                grp = 4 * c + q
                if used:
                    dve.wait_ge(gathered[q], 32 * c)
                nc.vector.tensor_copy(gidx[:, q, :], srcidx[:, ds(2 * grp, 2)]).then_inc(gidx_ready, 1)

            def select(c, q, used):
                grp = 4 * c + q
                dve.wait_ge(drow_loaded[q], 16 * (c + 1))
                if used:
                    dve.wait_ge(z_ready, grp - 3)
                for i in range(2):
                    col = ds(2 * grp + i, 1)
                    if wcol is None:
                        nc.vector.tensor_scalar(same[:, q, i, :], drow[:, q, :], dcol[:, col], None, ALU.is_equal)
                    else:
                        nc.vector.tensor_scalar(same[:, q, i, :], drow[:, q, :], dcol[:, col], wcol[:, col],
                                                ALU.is_equal, ALU.mult)
                for i in range(2):
                    col = ds(2 * grp + i, 1)
                    last = nc.vector.scalar_tensor_tensor(dup[:, q, i, :], drow[:, q, :], dcol[:, col],
                                                          g.before[:, i, :], ALU.is_equal, ALU.mult)
                last.then_inc(select_ready, 1)

            def place(c, h):
                b = 2 * c + h
                dve.wait_ge(ranked, b + 1)
                if not isinstance(b, int) or b > 0:
                    dve.wait_ge(rank_used, b)
                nc.vector.tensor_tensor(work[:, :, :], ps_r[:, 0:4, :], bc(sort.base[:, :], [P, 4, R], 1),
                                        ALU.add).then_inc(summed, 1)
                dve.wait_ge(summed, b + 1)
                nc.vector.tensor_tensor(sort.base[:, :], sort.base[:, :], ps_r[:, 4, :],
                                        ALU.add).then_inc(rank_used, 1)
                nc.vector.tensor_tensor(work[:, :, :], work[:, :, :], sort.onehot[:, ds(4 * b, 4), :],
                                        ALU.mult).then_inc(masked, 1)
                dve.wait_ge(masked, b + 1)
                nc.vector.tensor_reduce(sort.pos[:, ds(4 * b, 4)], work[:, :, :], AX.X, ALU.add).then_inc(placed, 1)

            def centre_sum(c, at):
                n = parts(at)
                x3 = xr[0:n, :].rearrange("p (j d) -> p j d", d=D)
                dve.wait_ge(xf_loaded, 16 * (c + 1))
                dve.wait_ge(xr_loaded, 16 * (c + 1))
                nc.vector.tensor_tensor(xr[0:n, :], xr[0:n, :], xf[0:n, :, :].rearrange("p a b -> p (a b)"),
                                        ALU.add).then_inc(xc_summed, 1)
                dve.wait_ge(xc_summed, c + 1)
                nc.vector.tensor_reduce(xmean[0:n, :], x3, AX.X, ALU.add).then_inc(xc_meaned, 1)
                dve.wait_ge(xc_meaned, c + 1)
                nc.vector.tensor_scalar(xmean[0:n, :], xmean[0:n, :], 1.0 / D, None, ALU.mult).then_inc(xc_scaled, 1)
                dve.wait_ge(xc_scaled, c + 1)
                nc.vector.tensor_tensor(x3, x3, bc(xmean[0:n, :], [n, J, D], 2), ALU.subtract).then_inc(xc_ready, 1)

            stage_gather(0, 0, False)
            stage_gather(0, 1, False)
            select(0, 0, False)

            def body(c, at):
                for q in range(4):
                    if q < 2:
                        stage_gather(c, q + 2, at > 0)
                    elif at < last_super:
                        stage_gather(c + 1, q - 2, True)
                    if q < 3:
                        select(c, q + 1, at > 0)
                    elif at < last_super:
                        select(c + 1, 0, True)
                    grp = 4 * c + q
                    cols = ds(2 * grp, 2)
                    dve.wait_ge(dups_counted, grp + 1)
                    nc.vector.scalar_tensor_tensor(first[:, q, :], ps_d[:, :], 1.0,
                                                   ddump[:, cols], ALU.min, ALU.mult).then_inc(dups_read, 1)
                    dve.wait_ge(dups_read, grp + 1)
                    if at > 0:
                        dve.wait_ge(scattered, 32 * (grp - 3))
                    nc.vector.tensor_tensor(sidx[:, q, :], first[:, q, :], dcol[:, cols],
                                            ALU.add).then_inc(sidx_ready, 1)
                    if sort and q in (1, 3):
                        place(c, q // 2)
                    if x0 is not None and q == 2 and parts(at):
                        centre_sum(c, at)
                    if parts(at) and q >= 2:
                        h, n = q - 2, parts(at)
                        dve.wait_ge(lin_ready, 2 * c + h + 1)
                        if at > 0:
                            dve.wait_ge(lin_stored, 16 * c)
                        nc.vector.tensor_tensor(
                            lf[0:n, h * 512:(h + 1) * 512].rearrange("p (j d) -> p j d", d=D),
                            ps_l[0:n, :].rearrange("p (j d) -> p j d", d=D),
                            bc(lin_bias[0:n, :], [n, 8, D], 1), ALU.add).then_inc(lin_done, 1)

            over_supers(dve, body)
            if sort:
                dve.wait_ge(placed, 2 * SUPERS)
                step = Chain(dve, last_steps)
                step(nc.vector.tensor_copy(pos_i[:, :], sort.pos[:, :]))
                step(nc.vector.tensor_scalar(tile_i[:, :], pos_i[:, :], 7, None, ALU.arith_shift_right))
                step(nc.vector.tensor_scalar(slot_i[:, :], pos_i[:, :], P - 1, None, ALU.bitwise_and))
                nc.vector.scalar_tensor_tensor(g.posidx[:, :], slot_i[:, :], float(RTILES), tile_i[:, :], ALU.mult,
                                               ALU.add)

        @block.tensor
        def _(pe):
            def rank(c, h):
                b = 2 * c + h
                if not isinstance(b, int) or b > 0:
                    pe.wait_ge(rank_used, b)
                nc.tensor.matmul(ps_r[:, 0:4, :], g.beforeb[:, :], sort.onehot[:, ds(4 * b, 4), :],
                                 start=True, stop=False)
                for k in range(1, 4):
                    nc.tensor.matmul(ps_r[:, k:4, :], g.onesb[:, :], sort.onehot[:, ds(4 * b, 4 - k), :],
                                     start=False, stop=(k == 3))
                for k in range(4):
                    last = nc.tensor.matmul(ps_r[:, 4, :], g.onesb[:, :], sort.onehot[:, ds(4 * b + k, 1), :],
                                            start=(k == 0), stop=(k == 3))
                last.then_inc(ranked, 1)

            def body(c, at):
                for q in range(4):
                    grp, a = 4 * c + q, q % 2
                    ready = at > 0 or q >= 2
                    if sort and q in (1, 3):
                        rank(c, q // 2)
                    pe.wait_ge(select_ready, grp + 1)
                    if at > 0 or q > 0:
                        pe.wait_ge(dups_read, grp)
                    for j in range(2):
                        for i in range(2):
                            last = nc.tensor.matmul(ps_d[:, j:j + 1],
                                                    dup[:, q, i, j * P:(j + 1) * P], g.onesb[:, 0:1],
                                                    start=(i == 0), stop=(i == 1))
                    last.then_inc(dups_counted, 1)
                    if ready:
                        pe.wait_ge(out_copied, grp - 1)
                    if degree:
                        for j in range(2):
                            for i in range(2):
                                nc.tensor.matmul(ps_o[a][:, j * width + D:j * width + D + 1],
                                                 same[:, q, i, j * P:(j + 1) * P], g.onesf[:, 0:1],
                                                 start=(i == 0), stop=(i == 1))
                    if relation:
                        pe.wait_ge(spread, grp + 1)
                    else:
                        pe.wait_ge(gathered[q], 32 * (c + 1))
                    if ready:
                        pe.wait_ge(z_copied, grp - 1)
                    for i in range(2):
                        last = nc.tensor.matmul(ps_z[a][:, i if relation else 0, :],
                                                xb[:, a, i, :] if relation else xg[:, q, i, (1 - i) * D:(3 - i) * D],
                                                same[:, q, i, :], start=(relation or i == 0),
                                                stop=(relation or i == 1))
                    last.then_inc(z_ready, 1)
                    n = parts(at)
                    if n and q < 2:
                        if q == 0:
                            pe.wait_ge(xf_loaded, 16 * (c + 1))
                        if at > 0 or q > 0:
                            pe.wait_ge(turned_copied, 2 * c + q)
                        for k in range(4):
                            last = nc.tensor.transpose(ps_t[:, k * n:(k + 1) * n], xf[0:n, 4 * q + k, :],
                                                       g.ident[0:n, 0:n])
                        last.then_inc(turned, 1)
                    if n and q >= 2:
                        h = q - 2
                        pe.wait_ge(turned_copied, 2 * c + h + 1)
                        if at > 0 or h > 0:
                            pe.wait_ge(lin_done, 2 * c + h)
                        for k in range(4):
                            last = nc.tensor.matmul(ps_l[0:n, k * P:(k + 1) * P], xt[:, h, k * n:(k + 1) * n],
                                                    wblk, start=True, stop=True)
                        last.then_inc(lin_ready, 1)
                    pe.wait_ge(z_copied, grp + 1)
                    if relation:
                        pe.wait_ge(w_loaded[q], 64 * (c + 1))
                    for j in range(2):
                        for i in range(Z):
                            last = nc.tensor.matmul(ps_o[a][:, j * width:j * width + D],
                                                    zs[:, a, i, j * P:(j + 1) * P],
                                                    wslot[:, q, i, :] if relation else wst[:, :],
                                                    start=(i == 0), stop=(i == Z - 1))
                    last.then_inc(out_ready, 1)

            over_supers(pe, body)

        @block.scalar
        def _(act):
            def spread_rows(c, q, old):
                grp, a = 4 * c + q, q % 2
                act.wait_ge(gathered[q], 32 * (c + 1))
                act.wait_ge(xg_zeroed, 1)
                if old:
                    act.wait_ge(z_ready, grp - 1)
                for h in range(2):
                    rows = slice(h * HALF, (h + 1) * HALF)
                    last = nc.scalar.copy(xb[rows, a, :, h * D:(h + 1) * D], xg[rows, q, :, :])
                last.then_inc(spread, 1)

            if relation:
                spread_rows(0, 0, False)

            def body(c, at):
                for q in range(4):
                    grp, a = 4 * c + q, q % 2
                    if relation and q < 3:
                        spread_rows(c, q + 1, at > 0 or q >= 1)
                    elif relation and at < last_super:
                        spread_rows(c + 1, 0, True)
                    act.wait_ge(z_ready, grp + 1)
                    if at > 0 or q >= 2:
                        act.wait_ge(out_ready, grp - 1)
                    nc.scalar.copy(zs[:, a, :, :], ps_z[a][:, :, :]).then_inc(z_copied, 1)
                    n = parts(at)
                    if n and q < 2:
                        act.wait_ge(turned, 2 * c + q + 1)
                        if at > 0:
                            act.wait_ge(lin_ready, 2 * c + q - 1)
                        nc.scalar.copy(xt[:, q, 0:4 * n], ps_t[:, 0:4 * n]).then_inc(turned_copied, 1)
                    act.wait_ge(out_ready, grp + 1)
                    if at > 0:
                        act.wait_ge(scattered, 32 * (grp - 3))
                    nc.scalar.copy(outs[:, q, :, :].rearrange("p j w -> p (j w)"),
                                   ps_o[a][:, 0:2 * width]).then_inc(out_copied, 1)
                    if q == 0 and parts(at - 1):
                        act.wait_ge(lin_done, 2 * c)
                        act.dma_start(chunk(lin_out, c - 1, at - 1), lf[0:parts(at - 1), :]).then_inc(lin_stored, 16)
                    if q == 3 and x0 is not None and n:
                        act.wait_ge(xc_ready, c + 1)
                        act.dma_start(chunk(xc_out, c, at), xr[0:n, :]).then_inc(xc_stored, 16)

            over_supers(act, body)
            if parts(last_super):
                act.wait_ge(lin_done, 2 * CHUNKS)
                act.dma_start(chunk(lin_out, CHUNKS - 1, CHUNKS - 1), lf[0:PLAST, :]).then_inc(lin_stored, 16)


DEEP = 4
PEEL = 3 * DEEP


def over_chunks(eng, stages):
    deepest = max(lag for _, lag in stages)

    def step(s, j, fixed):
        for stage, lag in stages:
            if fixed and not 0 <= s - lag < CHUNKS:
                continue
            n = PLAST if fixed and s - lag == CHUNKS - 1 else P
            stage(s - lag, (j - lag) % DEEP, n, s - lag if fixed else PEEL)

    for t in range(PEEL):
        step(t, t % DEEP, True)
    with eng.Fori(PEEL // DEEP, (CHUNKS - 1) // DEEP) as k:
        for j in range(DEEP):
            step(DEEP * k + j, j, False)
    for t in range(CHUNKS - 1, CHUNKS + deepest):
        step(t, t % DEEP, True)


def wide(ap, n, row=D):
    return ap[0:n, :].rearrange("p (j d) -> p j d", d=row)


class RecordScatter:

    def __init__(self, nc, g, s, table, first_tile):
        self.nc, self.g, self.table, self.first_tile = nc, g, table, first_tile
        self.idx = s.sb("rec_idx", [P, DEEP, 4], i32)
        self.val = s.sb("rec_val", [P, DEEP, 4, 4])
        self.staged = s.sem("rec_staged")
        self.landed = [s.sem(f"rec_landed{j}") for j in range(DEEP)]
        self.tick = s.sem("rec_tick")
        self.lots = [0] * DEEP

    def tiles(self, c):
        return [k for k in range(4) if not isinstance(c, int) or self.first_tile + 4 * c + k <= LAST_TILE]

    def stage(self, eng):
        def run(c, j, n, age):
            if age >= DEEP:
                eng.wait_ge(self.landed[j], self.done(c, j))
            cols = ds(4 * c + self.first_tile, 4)
            self.nc.vector.tensor_copy(self.idx[:, j, :], self.g.posidx[:, cols])
            self.nc.vector.tensor_copy(self.val[:, j, :, :], self.g.rec[:, cols, :]).then_inc(self.staged, 1)
        return run

    def done(self, c, j):
        return 64 * ((c - j) // DEEP) if isinstance(c, int) else 16 * (c - j)

    def scatter(self, pool):
        def run(c, j, n, age):
            pool.wait_ge(self.staged, c + 1)
            pool.sem_inc(self.tick, 1)
            for k in self.tiles(c):
                rows = P
                if isinstance(c, int) and self.first_tile + 4 * c + k == LAST_TILE:
                    rows = LAST_ROWS
                pool.indirect_dma_start(out=self.table[:, :],
                                        out_offset=bass.IndirectOffsetOnAxis(ap=self.idx[0:rows, j, k:k + 1], axis=0),
                                        in_=self.val[0:rows, j, k, :], in_offset=None).then_inc(self.landed[j], 16)
        return run

    def wait_all(self, pool):
        for j in range(DEEP):
            chunks = [c for c in range(CHUNKS) if c % DEEP == j]
            pool.wait_ge(self.landed[j], 16 * sum(len(self.tiles(c)) for c in chunks))


def norm_phase1(nc, g, table, lin, h_out, recs):
    s = Scope(nc, "n1")
    with s:
        W = J * (D + 1)
        tin = s.sb("tin", [P, DEEP, W])
        rin = s.sb("rin", [P, DEEP, J * D])
        a = s.sb("a", [P, DEEP, J * D])
        sq = s.sb("sq", [P, 2, J * D])
        ht = s.sb("ht", [P, 2, J // 2, P])
        out = s.sb("out", [P, DEEP, J * D])
        deg = s.sb("deg", [P, DEEP, J])
        var = s.sb("var", [P, DEEP, J])
        ps_t = [s.ps(f"ps_t{k}", [P, J // 2, P]) for k in range(2)]
        ps_h = [s.ps(f"ps_h{k}", [P, J // 2, P]) for k in range(2)]
        rec = RecordScatter(nc, g, s, recs, 0)
        loaded = [s.sem(f"loaded{j}") for j in range(DEEP)]
        stored = [s.sem(f"stored{j}") for j in range(DEEP)]
        d1, inverted, divided, summed = s.sem("deg_max"), s.sem("inverted"), s.sem("divided"), s.sem("summed")
        squared, reduced, rooted = s.sem("squared"), s.sem("reduced"), s.sem("rooted")
        rsigma, scaled = s.sem("rsigma"), s.sem("scaled")
        turned, clipped, back, h_ready = s.sem("turned"), s.sem("clipped"), s.sem("back"), s.sem("h_ready")
        block = s.block()

        @block.sync
        def _(sp):
            def load(c, j, n, age):
                if age >= DEEP:
                    sp.wait_ge(summed, c - DEEP + 1)
                sp.dma_start(tin[0:n, j, :], tile_rows(table, c * CH, n * J)).then_inc(loaded[j], 16)
                sp.dma_start(rin[0:n, j, :], tile_rows(lin, c * CH, n * J)).then_inc(loaded[j], 16)

            def store(c, j, n, age):
                sp.wait_ge(h_ready, c + 1)
                sp.dma_start(tile_rows(h_out, c * CH, n * J), out[0:n, j, :]).then_inc(stored[j], 16)

            over_chunks(sp, [(load, 0), (store, 6)])
            for j in range(DEEP):
                sp.wait_ge(stored[j], 16 * len(range(j, CHUNKS, DEEP)))

        @block.vector
        def _(dve):
            def degree(c, j, n, age):
                dve.wait_ge(loaded[j], full(c, j, 32))
                nc.vector.tensor_scalar(deg[0:n, j, :], wide(tin[:, j, :], n, D + 1)[:, :, D], 1.0, None,
                                        ALU.max).then_inc(d1, 1)

            def invert(c, j, n, age):
                dve.wait_ge(d1, c + 1)
                nc.vector.reciprocal(g.inv[0:n, ds(c * J, J)], deg[0:n, j, :]).then_inc(inverted, 1)

            def divide(c, j, n, age):
                dve.wait_ge(inverted, c + 1)
                if age >= DEEP:
                    dve.wait_ge(turned, c - DEEP + 1)
                nc.vector.tensor_tensor(wide(a[:, j, :], n), wide(tin[:, j, :], n, D + 1)[:, :, 0:D],
                                        bc(g.inv[0:n, ds(c * J, J)], [n, J, D], 2), ALU.mult).then_inc(divided, 1)

            def add_lin(c, j, n, age):
                dve.wait_ge(divided, c + 1)
                nc.vector.tensor_tensor(a[0:n, j, :], a[0:n, j, :], rin[0:n, j, :], ALU.add).then_inc(summed, 1)

            def variance(c, j, n, age):
                dve.wait_ge(squared, c + 1)
                nc.vector.tensor_reduce(var[0:n, j, :], wide(sq[:, j % 2, :], n), AX.X, ALU.add).then_inc(reduced, 1)

            def invert_root(c, j, n, age):
                dve.wait_ge(rooted, c + 1)
                nc.vector.reciprocal(var[0:n, j, :], var[0:n, j, :]).then_inc(rsigma, 1)

            def scale(c, j, n, age):
                dve.wait_ge(rsigma, c + 1)
                a3 = wide(a[:, j, :], n)
                nc.vector.tensor_tensor(a3, a3, bc(var[0:n, j, :], [n, J, D], 2), ALU.mult).then_inc(scaled, 1)

            over_chunks(dve, [(degree, 0), (variance, 1), (invert, 0), (rec.stage(dve), 0), (divide, 0),
                              (invert_root, 1), (add_lin, 0), (scale, 1)])

        @block.tensor
        def _(pe):
            def turn(c, j, n, age):
                pe.wait_ge(scaled, c + 1)
                if age >= 2:
                    pe.wait_ge(clipped, c - 1)
                for k in range(J // 2):
                    last = nc.tensor.transpose(ps_t[j % 2][:, k, 0:n], a[0:n, j, k * P:(k + 1) * P],
                                               g.ident[0:n, 0:n])
                last.then_inc(turned, 1)

            def turn_back(c, j, n, age):
                pe.wait_ge(clipped, c + 1)
                if age >= 2:
                    pe.wait_ge(h_ready, c - 1)
                for k in range(J // 2):
                    last = nc.tensor.transpose(ps_h[j % 2][0:n, k, :], ht[:, j % 2, k, 0:n], g.ident[:, :])
                last.then_inc(back, 1)

            over_chunks(pe, [(turn, 2), (turn_back, 3)])

        @block.scalar
        def _(act):
            def square(c, j, n, age):
                act.wait_ge(summed, c + 1)
                if age >= 2:
                    act.wait_ge(reduced, c - 1)
                nc.scalar.activation(sq[0:n, j % 2, :], a[0:n, j, :], ACT.Square).then_inc(squared, 1)

            def root(c, j, n, age):
                act.wait_ge(reduced, c + 1)
                nc.scalar.activation(var[0:n, j, :], var[0:n, j, :], ACT.Sqrt, bias=g.eps[0:n, :],
                                     scale=1.0 / D).then_inc(rooted, 1)

            def clip(c, j, n, age):
                act.wait_ge(turned, c + 1)
                if age >= 2:
                    act.wait_ge(back, c - 1)
                nc.scalar.activation(ht[:, j % 2, :, 0:n], ps_t[j % 2][:, :, 0:n], ACT.Relu, bias=g.gcols[:, 1:2],
                                     scale=g.gcols[:, 0:1]).then_inc(clipped, 1)

            def copy_out(c, j, n, age):
                act.wait_ge(back, c + 1)
                if age >= DEEP:
                    act.wait_ge(stored[j], full(c, j, 16) - 16)
                nc.scalar.copy(out[0:n, j, :].rearrange("p (k b) -> p k b", b=P),
                               ps_h[j % 2][0:n, :, :]).then_inc(h_ready, 1)

            over_chunks(act, [(root, 1), (square, 0), (clip, 2), (copy_out, 3)])

        @block.gpsimd
        def _(pool):
            over_chunks(pool, [(rec.scatter(pool), 0)])
            rec.wait_all(pool)


def full(c, j, each):
    return each * ((c - j) // DEEP + 1) if isinstance(c, int) else each // DEEP * (c - j) + each


def norm_phase2(nc, g, table, lin, xc, x1_out, recs):
    s = Scope(nc, "n2")
    with s:
        W = J * D
        tin = s.sb("tin", [P, DEEP, W])
        rin = s.sb("rin", [P, DEEP, W])
        xin = s.sb("xin", [P, DEEP, W])
        a = s.sb("a", [P, DEEP, W])
        sq = s.sb("sq", [P, 2, W])
        ht = s.sb("ht", [P, 2, J // 2, P])
        sq2 = s.sb("sq2", [P, 2, W])
        out = s.sb("out", [P, DEEP, W])
        var = s.sb("var", [P, DEEP, J])
        var2 = s.sb("var2", [P, DEEP, J])
        ps_t = [s.ps(f"ps_t{k}", [P, J // 2, P]) for k in range(2)]
        ps_h = [s.ps(f"ps_h{k}", [P, J // 2, P]) for k in range(2)]
        rec = RecordScatter(nc, g, s, recs, 4 * CHUNKS)
        loaded = [s.sem(f"loaded{j}") for j in range(DEEP)]
        x_loaded = [s.sem(f"x_loaded{j}") for j in range(DEEP)]
        stored = [s.sem(f"stored{j}") for j in range(DEEP)]
        divided, summed, squared, reduced = s.sem("divided"), s.sem("summed"), s.sem("squared"), s.sem("reduced")
        rooted, rsigma, scaled = s.sem("rooted"), s.sem("rsigma"), s.sem("scaled")
        turned, clipped, back, joined = s.sem("turned"), s.sem("clipped"), s.sem("back"), s.sem("joined")
        squared2, reduced2, rooted2 = s.sem("squared2"), s.sem("reduced2"), s.sem("rooted2")
        rsigma2, out_ready = s.sem("rsigma2"), s.sem("out_ready")
        block = s.block()

        @block.sync
        def _(sp):
            def load(c, j, n, age):
                if age >= DEEP:
                    sp.wait_ge(summed, c - DEEP + 1)
                sp.dma_start(tin[0:n, j, :], tile_rows(table, c * CH, n * J)).then_inc(loaded[j], 16)
                sp.dma_start(rin[0:n, j, :], tile_rows(lin, c * CH, n * J)).then_inc(loaded[j], 16)

            def load_x(c, j, n, age):
                if age >= DEEP:
                    sp.wait_ge(joined, c - DEEP + 1)
                sp.dma_start(xin[0:n, j, :], tile_rows(xc, c * CH, n * J)).then_inc(x_loaded[j], 16)

            def store(c, j, n, age):
                sp.wait_ge(out_ready, c + 1)
                sp.dma_start(tile_rows(x1_out, c * CH, n * J), out[0:n, j, :]).then_inc(stored[j], 16)

            over_chunks(sp, [(load, 0), (load_x, 1), (store, 8)])
            for j in range(DEEP):
                sp.wait_ge(stored[j], 16 * len(range(j, CHUNKS, DEEP)))

        @block.gpsimd
        def _(pool):
            def add_lin(c, j, n, age):
                pool.wait_ge(divided, c + 1)
                nc.gpsimd.tensor_tensor(a[0:n, j, :], a[0:n, j, :], rin[0:n, j, :], ALU.add).then_inc(summed, 1)

            over_chunks(pool, [(add_lin, 0), (rec.scatter(pool), 0)])
            rec.wait_all(pool)

        @block.vector
        def _(dve):
            def divide(c, j, n, age):
                dve.wait_ge(loaded[j], full(c, j, 32))
                if age >= DEEP:
                    dve.wait_ge(turned, c - DEEP + 1)
                nc.vector.tensor_tensor(wide(a[:, j, :], n), wide(tin[:, j, :], n),
                                        bc(g.inv[0:n, ds(c * J, J)], [n, J, D], 2), ALU.mult).then_inc(divided, 1)

            def variance(c, j, n, age):
                dve.wait_ge(squared, c + 1)
                nc.vector.tensor_reduce(var[0:n, j, :], wide(sq[:, j % 2, :], n), AX.X, ALU.add).then_inc(reduced, 1)

            def invert_root(c, j, n, age):
                dve.wait_ge(rooted, c + 1)
                nc.vector.reciprocal(var[0:n, j, :], var[0:n, j, :]).then_inc(rsigma, 1)

            def scale(c, j, n, age):
                dve.wait_ge(rsigma, c + 1)
                a3 = wide(a[:, j, :], n)
                nc.vector.tensor_tensor(a3, a3, bc(var[0:n, j, :], [n, J, D], 2), ALU.mult).then_inc(scaled, 1)

            def join(c, j, n, age):
                dve.wait_ge(back, c + 1)
                dve.wait_ge(x_loaded[j], full(c, j, 16))
                if age >= DEEP:
                    dve.wait_ge(stored[j], full(c, j, 16) - 16)
                nc.vector.tensor_tensor(out[0:n, j, :].rearrange("p (k b) -> p k b", b=P), ps_h[j % 2][0:n, :, :],
                                        xin[0:n, j, :].rearrange("p (k b) -> p k b", b=P),
                                        ALU.add).then_inc(joined, 1)

            def variance2(c, j, n, age):
                dve.wait_ge(squared2, c + 1)
                nc.vector.tensor_reduce(var2[0:n, j, :], wide(sq2[:, j % 2, :], n), AX.X,
                                        ALU.add).then_inc(reduced2, 1)

            def invert_root2(c, j, n, age):
                dve.wait_ge(rooted2, c + 1)
                nc.vector.reciprocal(var2[0:n, j, :], var2[0:n, j, :]).then_inc(rsigma2, 1)

            def scale2(c, j, n, age):
                dve.wait_ge(rsigma2, c + 1)
                o3 = wide(out[:, j, :], n)
                nc.vector.tensor_tensor(o3, o3, bc(var2[0:n, j, :], [n, J, D], 2), ALU.mult).then_inc(out_ready, 1)

            over_chunks(dve, [(divide, 0), (variance2, 5), (variance, 2), (rec.stage(dve), 0), (invert_root2, 5),
                              (join, 4), (invert_root, 2), (scale2, 5), (scale, 2)])

        @block.tensor
        def _(pe):
            def turn(c, j, n, age):
                pe.wait_ge(scaled, c + 1)
                if age >= 2:
                    pe.wait_ge(clipped, c - 1)
                for k in range(J // 2):
                    last = nc.tensor.transpose(ps_t[j % 2][:, k, 0:n], a[0:n, j, k * P:(k + 1) * P],
                                               g.ident[0:n, 0:n])
                last.then_inc(turned, 1)

            def turn_back(c, j, n, age):
                pe.wait_ge(clipped, c + 1)
                if age >= 2:
                    pe.wait_ge(joined, c - 1)
                for k in range(J // 2):
                    last = nc.tensor.matmul(ps_h[j % 2][0:n, k, :], ht[:, j % 2, k, 0:n], g.wblk[:, 3, :],
                                            start=True, stop=True)
                last.then_inc(back, 1)

            over_chunks(pe, [(turn, 3), (turn_back, 3)])

        @block.scalar
        def _(act):
            def square(c, j, n, age):
                act.wait_ge(summed, c + 1)
                if age >= 2:
                    act.wait_ge(reduced, c - 1)
                nc.scalar.activation(sq[0:n, j % 2, :], a[0:n, j, :], ACT.Square).then_inc(squared, 1)

            def root(c, j, n, age):
                act.wait_ge(reduced, c + 1)
                nc.scalar.activation(var[0:n, j, :], var[0:n, j, :], ACT.Sqrt, bias=g.eps[0:n, :],
                                     scale=1.0 / D).then_inc(rooted, 1)

            def clip(c, j, n, age):
                act.wait_ge(turned, c + 1)
                if age >= 2:
                    act.wait_ge(back, c - 1)
                nc.scalar.activation(ht[:, j % 2, :, 0:n], ps_t[j % 2][:, :, 0:n], ACT.Relu, bias=g.gcols[:, 3:4],
                                     scale=g.gcols[:, 2:3]).then_inc(clipped, 1)

            def square2(c, j, n, age):
                act.wait_ge(joined, c + 1)
                if age >= 2:
                    act.wait_ge(reduced2, c - 1)
                nc.scalar.activation(sq2[0:n, j % 2, :], out[0:n, j, :], ACT.Square).then_inc(squared2, 1)

            def root2(c, j, n, age):
                act.wait_ge(reduced2, c + 1)
                nc.scalar.activation(var2[0:n, j, :], var2[0:n, j, :], ACT.Sqrt, bias=g.eps[0:n, :],
                                     scale=1.0 / D).then_inc(rooted2, 1)

            over_chunks(act, [(root2, 5), (root, 2), (clip, 3), (square, 1), (square2, 4)])


def reload_phase(nc, g, recs, dst2):
    s = Scope(nc, "re")
    with s:
        rec = s.sb("rec", [P, RTILES, 4])
        rows = s.sb("rows", [RTB, BLOCKS, P])
        ps_rows = s.ps("ps_rows", [RTB, BLOCKS, P])
        loaded, turned, copied, stored = s.sem("loaded"), s.sem("turned"), s.sem("copied"), s.sem("stored")
        steps = s.sem("steps")
        block = s.block()

        @block.sync
        def _(sp):
            sp.dma_start(rec[:, :, :].rearrange("p t f -> p (t f)"),
                         recs.rearrange("(p t) f -> p (t f)", p=P)).then_inc(loaded, 16)
            sp.wait_ge(copied, 1)
            sp.dma_start(dst2.rearrange("(b r p) -> r b p", b=BLOCKS, p=P), rows[:, :, :]).then_inc(stored, 16)
            sp.wait_ge(stored, 16)

        @block.vector
        def _(dve):
            dve.wait_ge(loaded, 16)
            nc.vector.tensor_copy(g.dcol2[:, :], rec[:, :, 1]).then_inc(steps, 1)
            nc.vector.tensor_copy(g.srcidx2[:, :], rec[:, :, 0])
            nc.vector.tensor_copy(g.wcol2[:, :], rec[:, :, 2])
            dve.wait_ge(steps, 1)
            nc.vector.tensor_tensor(g.ddump2[:, :].rearrange("p (g j) -> p g j", j=2),
                                    bc(g.dumpcol[:, :], [P, RTILES // 2, 2], 1),
                                    g.dcol2[:, :].rearrange("p (g j) -> p g j", j=2), ALU.subtract)

        @block.tensor
        def _(pe):
            pe.wait_ge(steps, 1)
            for b in range(BLOCKS):
                last = nc.tensor.transpose(ps_rows[:, b, :], g.dcol2[:, b * RTB:(b + 1) * RTB], g.ident[:, :])
            last.then_inc(turned, 1)

        @block.scalar
        def _(act):
            act.wait_ge(turned, 1)
            nc.scalar.copy(rows[:, :, :], ps_rows[:, :, :]).then_inc(copied, 1)


def stats_phase(nc, g, table, lin, y_out):
    s = Scope(nc, "st")
    with s:
        W = J * D
        tin = s.sb("tin", [P, DEEP, W])
        rin = s.sb("rin", [P, DEEP, W])
        y = s.sb("y", [P, DEEP, W])
        sq = s.sb("sq", [P, DEEP, W])
        acc = s.sb("acc", [P, W])
        acc2 = s.sb("acc2", [P, W])
        both = s.sb("both", [P, 2, D])
        mean = s.sb("mean", [P, D])
        var = s.sb("var", [P, D])
        m2 = s.sb("m2", [P, D])
        ps_sum = s.ps("ps_sum", [P, 2, D])
        t_loaded = [s.sem(f"t_loaded{j}") for j in range(DEEP)]
        r_loaded = [s.sem(f"r_loaded{j}") for j in range(DEEP)]
        stored = [s.sem(f"stored{j}") for j in range(DEEP)]
        cleared, clipped, y_ready, squared = s.sem("cleared"), s.sem("clipped"), s.sem("y_ready"), s.sem("squared")
        acc_added, acc2_added = s.sem("acc_added"), s.sem("acc2_added")
        folded, totalled, rooted, steps = s.sem("folded"), s.sem("totalled"), s.sem("rooted"), s.sem("steps")
        var_ready = s.sem("var_ready")
        block = s.block()

        @block.sync
        def _(sp):
            def load(c, j, n, age):
                if age >= DEEP:
                    sp.wait_ge(y_ready, c - DEEP + 1)
                sp.dma_start(tin[0:n, j, :], tile_rows(table, c * CH, n * J)).then_inc(t_loaded[j], 16)
                sp.dma_start(rin[0:n, j, :], tile_rows(lin, c * CH, n * J)).then_inc(r_loaded[j], 16)

            def store(c, j, n, age):
                sp.wait_ge(y_ready, c + 1)
                sp.dma_start(tile_rows(y_out, c * CH, n * J), y[0:n, j, :]).then_inc(stored[j], 16)

            over_chunks(sp, [(load, 0), (store, 2)])
            for j in range(DEEP):
                sp.wait_ge(stored[j], 16 * len(range(j, CHUNKS, DEEP)))

        @block.scalar
        def _(act):
            def clip(c, j, n, age):
                act.wait_ge(r_loaded[j], full(c, j, 16))
                nc.scalar.activation(rin[0:n, j, :], rin[0:n, j, :], ACT.Relu).then_inc(clipped, 1)

            def square(c, j, n, age):
                act.wait_ge(y_ready, c + 1)
                if age >= DEEP:
                    act.wait_ge(acc2_added, c - DEEP + 1)
                nc.scalar.activation(sq[0:n, j, :], y[0:n, j, :], ACT.Square).then_inc(squared, 1)

            over_chunks(act, [(clip, 0), (square, 1)])
            act.wait_ge(var_ready, 1)
            nc.scalar.activation(var[:, :], var[:, :], ACT.Sqrt, bias=g.eps[:, :], scale=1.0).then_inc(rooted, 1)

        @block.gpsimd
        def _(pool):
            nc.gpsimd.memset(acc[:, :], 0.0).then_inc(acc_added, 1)

            def add(c, j, n, age):
                pool.wait_ge(y_ready, c + 1)
                pool.wait_ge(acc_added, c + 1)
                nc.gpsimd.tensor_tensor(acc[0:n, :], acc[0:n, :], y[0:n, j, :], ALU.add).then_inc(acc_added, 1)

            over_chunks(pool, [(add, 1)])

        @block.vector
        def _(dve):
            nc.vector.memset(acc2[:, :], 0.0).then_inc(acc2_added, 1)

            def make_y(c, j, n, age):
                dve.wait_ge(t_loaded[j], full(c, j, 16))
                dve.wait_ge(clipped, c + 1)
                if age >= DEEP:
                    dve.wait_ge(stored[j], full(c, j, 16) - 16)
                    dve.wait_ge(acc_added, c - DEEP + 2)
                    dve.wait_ge(squared, c - DEEP + 1)
                nc.vector.scalar_tensor_tensor(y[0:n, j, :], tin[0:n, j, :], 0.0, rin[0:n, j, :], ALU.max,
                                               ALU.add).then_inc(y_ready, 1)

            def add_squares(c, j, n, age):
                dve.wait_ge(squared, c + 1)
                dve.wait_ge(acc2_added, c + 1)
                nc.vector.tensor_tensor(acc2[0:n, :], acc2[0:n, :], sq[0:n, j, :], ALU.add).then_inc(acc2_added, 1)

            over_chunks(dve, [(make_y, 0), (add_squares, 2)])
            step = Chain(dve, steps)
            dve.wait_ge(acc_added, CHUNKS + 1)
            dve.wait_ge(acc2_added, CHUNKS + 1)
            nc.vector.tensor_reduce(both[:, 0, :], acc[:, :].rearrange("p (j d) -> p d j", d=D), AX.X, ALU.add)
            nc.vector.tensor_reduce(both[:, 1, :], acc2[:, :].rearrange("p (j d) -> p d j", d=D), AX.X,
                                    ALU.add).then_inc(folded, 1)
            dve.wait_ge(totalled, 1)
            step(nc.vector.tensor_scalar(mean[:, :], ps_sum[:, 0, :], 1.0 / N, None, ALU.mult))
            step(nc.vector.tensor_tensor(m2[:, :], mean[:, :], mean[:, :], ALU.mult))
            nc.vector.scalar_tensor_tensor(var[:, :], ps_sum[:, 1, :], 1.0 / N, m2[:, :], ALU.mult,
                                           ALU.subtract).then_inc(var_ready, 1)
            dve.wait_ge(rooted, 1)
            step(nc.vector.reciprocal(m2[:, :], var[:, :]))
            step(nc.vector.tensor_tensor(g.bnab[:, 0, :], g.vec("gamma"), m2[:, :], ALU.mult))
            step(nc.vector.tensor_tensor(mean[:, :], mean[:, :], g.bnab[:, 0, :], ALU.mult))
            nc.vector.tensor_tensor(g.bnab[:, 1, :], g.vec("beta"), mean[:, :], ALU.subtract)

        @block.tensor
        def _(pe):
            pe.wait_ge(folded, 1)
            nc.tensor.matmul(ps_sum[:, :, :], g.onesf[:, :], both[:, :, :], start=True, stop=True).then_inc(totalled, 1)


def final_phase(nc, g, x1, y, out_dram):
    s = Scope(nc, "fi")
    with s:
        W = J * D
        xin = s.sb("xin", [P, DEEP, W])
        a = s.sb("a", [P, DEEP, W])
        at = s.sb("at", [P, 2, J // 2, P])
        sq = s.sb("sq", [P, 2, W])
        out = s.sb("out", [P, DEEP, W])
        var = s.sb("var", [P, DEEP, J])
        ps_t = [s.ps(f"ps_t{k}", [P, J // 2, P]) for k in range(2)]
        ps_c = [s.ps(f"ps_c{k}", [P, J // 2, P]) for k in range(2)]
        y_loaded = [s.sem(f"y_loaded{j}") for j in range(DEEP)]
        x_loaded = [s.sem(f"x_loaded{j}") for j in range(DEEP)]
        stored = [s.sem(f"stored{j}") for j in range(DEEP)]
        gained, joined, turned, copied = s.sem("gained"), s.sem("joined"), s.sem("turned"), s.sem("copied")
        shifted = s.sem("shifted")
        centred, squared, reduced = s.sem("centred"), s.sem("squared"), s.sem("reduced")
        rooted, rsigma, out_ready = s.sem("rooted"), s.sem("rsigma"), s.sem("out_ready")
        block = s.block()

        @block.sync
        def _(sp):
            def load(c, j, n, age):
                if age >= DEEP:
                    sp.wait_ge(turned, c - DEEP + 1)
                sp.dma_start(a[0:n, j, :], tile_rows(y, c * CH, n * J)).then_inc(y_loaded[j], 16)
                sp.dma_start(xin[0:n, j, :], tile_rows(x1, c * CH, n * J)).then_inc(x_loaded[j], 16)

            def store(c, j, n, age):
                sp.wait_ge(out_ready, c + 1)
                sp.dma_start(tile_rows(out_dram, c * CH, n * J), out[0:n, j, :]).then_inc(stored[j], 16)

            over_chunks(sp, [(load, 0), (store, 5)])
            for j in range(DEEP):
                sp.wait_ge(stored[j], 16 * len(range(j, CHUNKS, DEEP)))

        @block.gpsimd
        def _(pool):
            def gain(c, j, n, age):
                pool.wait_ge(y_loaded[j], full(c, j, 16))
                a3 = wide(a[:, j, :], n)
                nc.gpsimd.tensor_tensor(a3, a3, bc(g.bnab[0:n, 0, :], [n, J, D], 1), ALU.mult).then_inc(gained, 1)
                pool.wait_ge(gained, c + 1)
                nc.gpsimd.tensor_tensor(a3, a3, bc(g.bnab[0:n, 1, :], [n, J, D], 1), ALU.add).then_inc(shifted, 1)

            over_chunks(pool, [(gain, 0)])

        @block.vector
        def _(dve):
            def join(c, j, n, age):
                dve.wait_ge(x_loaded[j], full(c, j, 16))
                dve.wait_ge(shifted, c + 1)
                nc.vector.tensor_tensor(a[0:n, j, :], a[0:n, j, :], xin[0:n, j, :], ALU.add).then_inc(joined, 1)

            def variance(c, j, n, age):
                dve.wait_ge(squared, c + 1)
                nc.vector.tensor_reduce(var[0:n, j, :], wide(sq[:, j % 2, :], n), AX.X, ALU.add).then_inc(reduced, 1)

            def invert_root(c, j, n, age):
                dve.wait_ge(rooted, c + 1)
                nc.vector.reciprocal(var[0:n, j, :], var[0:n, j, :]).then_inc(rsigma, 1)

            def scale(c, j, n, age):
                dve.wait_ge(rsigma, c + 1)
                if age >= DEEP:
                    dve.wait_ge(stored[j], full(c, j, 16) - 16)
                nc.vector.tensor_tensor(wide(out[:, j, :], n),
                                        ps_c[j % 2][0:n, :, :].rearrange("p k (i d) -> p (k i) d", d=D),
                                        bc(var[0:n, j, :], [n, J, D], 2), ALU.mult).then_inc(out_ready, 1)

            over_chunks(dve, [(variance, 3), (join, 1), (invert_root, 3), (scale, 3)])

        @block.tensor
        def _(pe):
            def turn(c, j, n, age):
                pe.wait_ge(joined, c + 1)
                if age >= 2:
                    pe.wait_ge(copied, c - 1)
                for k in range(J // 2):
                    last = nc.tensor.transpose(ps_t[j % 2][:, k, 0:n], a[0:n, j, k * P:(k + 1) * P],
                                               g.ident[0:n, 0:n])
                last.then_inc(turned, 1)

            def centre(c, j, n, age):
                pe.wait_ge(copied, c + 1)
                if age >= 2:
                    pe.wait_ge(out_ready, c - 1)
                for k in range(J // 2):
                    last = nc.tensor.matmul(ps_c[j % 2][0:n, k, :], at[:, j % 2, k, 0:n], g.wblk[:, 3, :],
                                            start=True, stop=True)
                last.then_inc(centred, 1)

            over_chunks(pe, [(centre, 2), (turn, 1)])

        @block.scalar
        def _(act):
            def copy_turned(c, j, n, age):
                act.wait_ge(turned, c + 1)
                if age >= 2:
                    act.wait_ge(centred, c - 1)
                nc.scalar.copy(at[:, j % 2, :, 0:n], ps_t[j % 2][:, :, 0:n]).then_inc(copied, 1)

            def square(c, j, n, age):
                act.wait_ge(centred, c + 1)
                if age >= 2:
                    act.wait_ge(reduced, c - 1)
                nc.scalar.activation(sq[0:n, j % 2, :].rearrange("p (k b) -> p k b", b=P), ps_c[j % 2][0:n, :, :],
                                     ACT.Square).then_inc(squared, 1)

            def root(c, j, n, age):
                act.wait_ge(reduced, c + 1)
                nc.scalar.activation(var[0:n, j, :], var[0:n, j, :], ACT.Sqrt, bias=g.eps[0:n, :],
                                     scale=1.0 / D).then_inc(rooted, 1)

            over_chunks(act, [(root, 3), (square, 2), (copy_turned, 1)])


def gnn_kernel(nc, io, out):
    def table(name, shape, dt=fp32):
        return nc.dram_tensor(name, shape, dt).ap()

    dr = {"t1": table("sums1", [TROWS, D + 1]), "t2": table("sums2", [TROWS, D]), "t3": table("sums3", [TROWS, D]),
          "lin1": table("lin1", [N, D]), "lin2": table("lin2", [N, D]), "lin3": table("lin3", [N, D]),
          "h1": table("h1", [N, D]), "xc": table("xc", [N, D]), "x1": table("x1", [N, D]), "y": table("y", [N, D]),
          "recs": table("recs", [P * RTILES, 4]), "dst1": table("dst1", [TILES * P]),
          "dst2": table("dst2", [RTILES * P]), "wrel": table("wrel", [R * D, D]),
          "htype": table("htype", [HB * P], i32)}
    top = Scope(nc, "g")
    with top:
        g = Persistent(top)
        t1_filled = top.sem("t1_filled")
        mid = Scope(nc, "m")
        with mid:
            sort = Sort(mid)
            setup_phase(nc, g, sort, io, dr, t1_filled)
            edge_phase(nc, g, "e1", io["x"], dr["dst1"], g.srcidx, g.dcol, g.ddump, dr["t1"], D + 1, g.wst1,
                       dr["lin1"], g.wblk[:, 0, :], g.vec("b1"), SUPERS, sort=sort, table_filled=t1_filled,
                       fill=(dr["t2"], g.zero[:, 0:J * D]))
        norm_phase1(nc, g, dr["t1"], dr["lin1"], dr["h1"], dr["recs"])
        edge_phase(nc, g, "e2", dr["h1"], dr["dst1"], g.srcidx, g.dcol, g.ddump, dr["t2"], D, g.wst2,
                   dr["lin2"], g.wblk[:, 1, :], g.vec("b2"), SUPERS,
                   fill=(dr["t3"], g.biases[:, :, :].rearrange("p j d -> p (j d)")), x0=io["x"], xc_out=dr["xc"])
        norm_phase2(nc, g, dr["t2"], dr["lin2"], dr["xc"], dr["x1"], dr["recs"])
        reload_phase(nc, g, dr["recs"], dr["dst2"])
        edge_phase(nc, g, "e3", dr["x1"], dr["dst2"], g.srcidx2, g.dcol2, g.ddump2, dr["t3"], D, None,
                   dr["lin3"], g.wblk[:, 2, :], g.vec("res_b"), RSUPERS, wcol=g.wcol2, wrel=dr["wrel"],
                   htype=dr["htype"])
        stats_phase(nc, g, dr["t3"], dr["lin3"], dr["y"])
        final_phase(nc, g, dr["x1"], dr["y"], out)


_INS = ["x", "src", "dst", "edge_type_64", "edge_weight1", "L0_gnn_W1l", "L0_gnn_b1l", "L0_gnn_W1r", "L0_gnn_g1",
        "L0_gnn_beta1", "L0_gnn_W2l", "L0_gnn_b2l", "L0_gnn_W2r", "L0_gnn_g2", "L0_gnn_beta2", "L1_gnn_basis",
        "L1_gnn_comp", "L1_gnn_bias", "L1_gnn_res_w", "L1_gnn_res_b", "L1_gnn_gamma", "L1_gnn_beta"]


def kernel(**inputs):
    import numpy as _np
    import concourse.bacc as _bacc
    from concourse import mybir as _mybir
    from concourse.bass_utils import run_bass_kernel_spmd as _run

    nc = _bacc.Bacc("TRN2", target_bir_lowering=False, num_devices=1)
    arrays, io = {}, {}
    for name in _INS:
        a = _np.ascontiguousarray(inputs[name])
        arrays[f"in_{name}_dram"] = a
        io[name] = nc.dram_tensor(f"in_{name}_dram", a.shape, _mybir.dt.from_np(a.dtype), kind="ExternalInput").ap()
    out = nc.dram_tensor("out_0_dram", (N, D), _mybir.dt.float32, kind="ExternalOutput").ap()
    gnn_kernel(nc, io, out)
    r = _run(nc, [arrays], core_ids=[0])
    return r.results[0]["out_0_dram"]
```

```python
import concourse.bass as bass
from concourse import mybir
from contextlib import ExitStack

N = 100000
E = 50000
D = 64
R = 64
B = 64
EPS = 1e-5
P = 128

TILES = -(-E // (8 * P)) * 8
LAST_TILE = E // P
LAST_ROWS = E - LAST_TILE * P
BLOCKS = 4
TB = TILES // BLOCKS
SUPERS = TILES // 8
HALF = P // 2
RTILES = -(-(E // HALF + R) // 16) * 8
HB = -(-2 * RTILES // P)
RSUPERS = RTILES // 8
RTB = RTILES // BLOCKS

J = 16
CH = P * J
CHUNKS = -(-N // CH)
PLAST = (N - (CHUNKS - 1) * CH) // J
assert PLAST * J == N - (CHUNKS - 1) * CH and CHUNKS == SUPERS and TILES % 8 == 0

KEEP = CHUNKS // 2
assert CHUNKS == 2 * KEEP + 1

TRASH = N
DUMP = N + 1
TROWS = CHUNKS * CH
assert TROWS >= DUMP + 2 * P

fp32 = mybir.dt.float32
bf16 = mybir.dt.bfloat16
i32 = mybir.dt.int32
ALU = mybir.AluOpType
ACT = mybir.ActivationFunctionType
AX = mybir.AxisListType
ds = bass.ds

VECS = ["b1", "g1", "be1", "b2", "g2", "be2", "bias", "res_b", "gamma", "beta"]


class Scope:

    def __init__(self, nc, tag):
        self.nc, self.tag, self.stack, self.sems = nc, tag, ExitStack(), []

    def sb(self, name, shape, dt=fp32):
        return self.stack.enter_context(self.nc.sbuf_tensor(f"{self.tag}_{name}", shape, dt))

    def ps(self, name, shape, dt=fp32):
        return self.stack.enter_context(self.nc.psum_tensor(f"{self.tag}_{name}", shape, dt))

    def sem(self, name):
        self.sems.append(self.nc.alloc_semaphore(f"{self.tag}_{name}"))
        return self.sems[-1]

    def block(self):
        return self.stack.enter_context(self.nc.Block())

    def __enter__(self):
        return self

    def __exit__(self, *error):
        self.stack.close()
        if self.sems:
            self.nc.clear_and_free_semaphores(self.sems)
            self.nc.all_engine_barrier()
        return False


def tile_rows(tensor, first, count, partitions=P, each=J):
    return tensor[ds(first, count), :].rearrange("(p j) d -> p (j d)", j=each)


def bc(ap, shape, axis):
    return ap.unsqueeze(axis).to_broadcast(shape)


class Chain:

    def __init__(self, eng, sem):
        self.eng, self.sem, self.n = eng, sem, 0

    def __call__(self, ins):
        self.n += 1
        ins.then_inc(self.sem, 1)
        self.eng.wait_ge(self.sem, self.n)


class Persistent:

    def __init__(self, s):
        self.ident = s.sb("ident", [P, P])
        self.onesf = s.sb("onesf", [P, P])
        self.onesb = s.sb("onesb", [P, P], bf16)
        self.before = s.sb("before", [P, 2, 2 * P])
        self.beforeb = s.sb("beforeb", [P, P], bf16)
        self.iota_rel = s.sb("iota_rel", [P, R])
        self.iota_half = s.sb("iota_half", [P, HB])
        self.dumpcol = s.sb("dumpcol", [P, 2])
        self.srcidx = s.sb("srcidx", [P, TILES], i32)
        self.dcol = s.sb("dcol", [P, TILES])
        self.ddump = s.sb("ddump", [P, TILES])
        self.rec = s.sb("rec", [P, TILES, 4])
        self.posidx = s.sb("posidx", [P, TILES], i32)
        self.wst1 = s.sb("wst1", [P, D])
        self.wst2 = s.sb("wst2", [P, D])
        self.wblk = s.sb("wblk", [P, 4, P])
        self.gcols = s.sb("gcols", [P, 4])
        self.vecs = s.sb("vecs", [P, len(VECS), D])
        self.eps = s.sb("eps", [P, 1])
        self.inv = s.sb("inv", [P, CHUNKS * J])
        self.bnab = s.sb("bnab", [P, 1, D])
        self.shiftcol = s.sb("shiftcol", [P, 1])
        self.zero = s.sb("zero", [P, J * (D + 1)])
        self.biases = s.sb("biases", [P, J, D])
        self.srcidx2 = s.sb("srcidx2", [P, RTILES], i32)
        self.dcol2 = s.sb("dcol2", [P, RTILES])
        self.ddump2 = s.sb("ddump2", [P, RTILES])
        self.wcol2 = s.sb("wcol2", [P, RTILES])
        self.wrow = s.sb("wrow", [1, RTILES], i32)

    def vec(self, name):
        return self.vecs[:, VECS.index(name), :]


class Sort:

    def __init__(self, s):
        self.onehot = s.sb("onehot", [P, TILES, R], bf16)
        self.base = s.sb("base", [P, R])
        self.pos = s.sb("pos", [P, TILES])


def setup_phase(nc, g, sort, io, dr, t1_filled):
    s = Scope(nc, "su")
    with s:
        rows_i = s.sb("rows_i", [TB, 3, BLOCKS, P], i32)
        rows_f = s.sb("rows_f", [TB, 4, BLOCKS, P])
        wnat = s.sb("wnat", [D, 5, 2 * D])
        cent = s.sb("cent", [D, D])
        comp = s.sb("comp", [R, B])
        compT = s.sb("compT", [B, R])
        basis = s.sb("basis", [B, D * D])
        wrel = s.sb("wrel", [R, D * D])
        bsum = s.sb("bsum", [P, 2])
        recpad = s.sb("recpad", [P, RTILES, 4])
        ps_edge = [s.ps(f"ps_edge{a}", [P, TILES]) for a in range(4)]
        ps_w = s.ps("ps_w", [P, 5, D])
        ps_ct = s.ps("ps_ct", [B, R])
        ps_rel = s.ps("ps_rel", [R, 512])
        ps_count = s.ps("ps_count", [P, 8, R])
        tcol = s.sb("tcol", [P, TILES])
        count = s.sb("count", [P, R])
        count_i = s.sb("count_i", [P, R], i32)
        halves_i = s.sb("halves_i", [P, R], i32)
        halves_f = s.sb("halves_f", [P, R])
        hend = s.sb("hend", [P, R])
        cmp = s.sb("cmp", [P, HB, R])
        htype = s.sb("htype", [P, HB])
        htype_i = s.sb("htype_i", [P, HB], i32)

        rows_padded = s.sem("rows_padded")
        recpad_set = s.sem("recpad_set")
        edges_loaded = s.sem("edges_loaded")
        weights_loaded = s.sem("weights_loaded")
        vectors_loaded = s.sem("vectors_loaded")
        basis_loaded = s.sem("basis_loaded")
        pool_steps = s.sem("pool_steps")
        consts_made = s.sem("consts_made")
        centering_made = s.sem("centering_made")
        rows_converted = s.sem("rows_converted")
        columns_made = s.sem("columns_made")
        weights_turned = s.sem("weights_turned")
        comp_turned = s.sem("comp_turned")
        comp_copied = s.sem("comp_copied")
        rel_made = s.sem("rel_made")
        rel_copied = s.sem("rel_copied")
        dve_steps = s.sem("dve_steps")
        stored = s.sem("stored")
        zero_set = s.sem("zero_set")
        onehot_made = s.sem("onehot_made")
        counted = s.sem("counted")
        types_made = s.sem("types_made")
        block = s.block()

        @block.sync
        def _(sp):
            sp.wait_ge(rows_padded, 4)
            full = 3 * TB * P
            for k, name in enumerate(["src", "dst", "edge_type_64", "edge_weight1"]):
                flat = io[name] if k < 3 else io[name].rearrange("e o -> (e o)")
                rows = rows_i[:, k] if k < 3 else rows_f[:, 3]
                sp.dma_start(rows[:, 0:3, :],
                             flat[0:full].rearrange("(b r p) -> r b p", b=3, p=P)).then_inc(edges_loaded, 16)
                rest = LAST_TILE - 3 * TB
                sp.dma_start(rows[0:rest, 3, :],
                             flat[full:full + rest * P].rearrange("(r p) -> r p", p=P)).then_inc(edges_loaded, 16)
                sp.dma_start(rows[rest:rest + 1, 3, 0:LAST_ROWS],
                             flat[full + rest * P:E].rearrange("(r p) -> r p", p=LAST_ROWS)).then_inc(edges_loaded, 16)
            for k, name in enumerate(["L0_gnn_W1l", "L0_gnn_W2l", "L0_gnn_W1r", "L0_gnn_W2r", "L1_gnn_res_w"]):
                for h in range(2):
                    sp.dma_start(wnat[:, k, h * D:(h + 1) * D], io[name][:, :]).then_inc(weights_loaded, 16)
            sp.dma_start(comp[:, :], io["L1_gnn_comp"][:, :]).then_inc(basis_loaded, 16)
            sp.dma_start(basis[:, :], io["L1_gnn_basis"].rearrange("b i o -> b (i o)")).then_inc(basis_loaded, 16)
            for k, name in enumerate(["L0_gnn_b1l", "L0_gnn_g1", "L0_gnn_beta1", "L0_gnn_b2l", "L0_gnn_g2",
                                      "L0_gnn_beta2", "L1_gnn_bias", "L1_gnn_res_b", "L1_gnn_gamma",
                                      "L1_gnn_beta"]):
                sp.dma_start(g.vecs[:, k, :],
                             io[name].unsqueeze(0).to_broadcast([P, D])).then_inc(vectors_loaded, 16)
            for k, name in enumerate(["L0_gnn_g1", "L0_gnn_beta1", "L0_gnn_g2", "L0_gnn_beta2"]):
                for h in range(2):
                    sp.dma_start(g.gcols[h * D:(h + 1) * D, k:k + 1], io[name].unsqueeze(1)).then_inc(stored, 16)
            sp.wait_ge(recpad_set, 2)
            sp.dma_start(dr["recs"].rearrange("(p t) f -> p (t f)", p=P),
                         recpad[:, :, :].rearrange("p t f -> p (t f)")).then_inc(stored, 16)
            sp.wait_ge(rows_converted, 1)
            sp.dma_start(dr["dst1"].rearrange("(b r p) -> r b p", b=BLOCKS, p=P),
                         rows_f[:, 1]).then_inc(stored, 16)
            sp.wait_ge(rel_copied, 8)
            for h in range(2):
                sp.dma_start(dr["wrel"].rearrange("(r h i) o -> h r (i o)", h=2, i=D)[h],
                             wrel[:, :]).then_inc(stored, 16)
            sp.wait_ge(types_made, 1)
            with nc.allow_non_contiguous_dma(reason="some small words, once"):
                sp.dma_start(dr["htype"].rearrange("(b p) -> p b", p=P), htype_i[:, :]).then_inc(stored, 16)
            sp.wait_ge(stored, 16 * 13)

        @block.gpsimd
        def _(pool):
            step = Chain(pool, pool_steps)
            step(nc.gpsimd.memset(g.ident[:, :], 0.0))
            step(nc.gpsimd.affine_select(out=g.ident[:, :], in_=g.ident[:, :], compare_op=ALU.not_equal, fill=1.0,
                                         base=0, pattern=[[-1, P]], channel_multiplier=1))
            step(nc.gpsimd.memset(g.before[:, :, :], 1.0))
            for i in range(2):
                nc.gpsimd.affine_select(out=g.before[:, i, :], in_=g.before[:, i, :], compare_op=ALU.is_gt, fill=0.0,
                                        base=-P * i, pattern=[[1, 2 * P]], channel_multiplier=-1)
            nc.gpsimd.iota(g.iota_rel[:, :], [[1, R]], base=0, channel_multiplier=0,
                           allow_small_or_imprecise_dtypes=True)
            nc.gpsimd.iota(g.iota_half[:, :], [[P, HB]], base=0, channel_multiplier=1,
                           allow_small_or_imprecise_dtypes=True)
            nc.gpsimd.iota(g.dumpcol[:, :], [[P, 2]], base=DUMP, channel_multiplier=1,
                           allow_small_or_imprecise_dtypes=True).then_inc(consts_made, 1)

        @block.tensor
        def _(pe):
            pe.wait_ge(consts_made, 1)
            pe.wait_ge(rows_converted, 1)
            for a in range(4):
                for b in range(BLOCKS):
                    last = nc.tensor.transpose(ps_edge[a][:, b * TB:(b + 1) * TB], rows_f[:, a, b, :],
                                               g.ident[0:TB, 0:TB])
            last.then_inc(columns_made, 1)
            pe.wait_ge(weights_loaded, 160)
            pe.wait_ge(centering_made, 1)
            for k in range(5):
                last = nc.tensor.matmul(ps_w[:, k, :], wnat[:, k, :], cent[:, :] if k < 4 else g.ident[0:D, 0:D],
                                        start=True, stop=True)
            last.then_inc(weights_turned, 1)
            pe.wait_ge(basis_loaded, 32)
            nc.tensor.transpose(ps_ct[:, :], comp[:, :], g.ident[0:R, 0:R]).then_inc(comp_turned, 1)
            pe.wait_ge(comp_copied, 1)
            for k in range(8):
                if k >= 1:
                    pe.wait_ge(rel_copied, k)
                nc.tensor.matmul(ps_rel[:, :], compT[:, :], basis[:, k * 512:(k + 1) * 512],
                                 start=True, stop=True).then_inc(rel_made, 1)
            for q in range(4):
                pe.wait_ge(onehot_made, q + 1)
            for b in range(SUPERS):
                last = nc.tensor.matmul(ps_count[:, :, :], g.onesb[:, :], sort.onehot[:, 8 * b:8 * b + 8, :],
                                        start=(b == 0), stop=(b == SUPERS - 1))
            last.then_inc(counted, 1)

        @block.scalar
        def _(act):
            act.wait_ge(zero_set, 1)
            with act.Fori(0, CHUNKS) as c:
                act.dma_start(tile_rows(dr["t1"], c * CH, CH), g.zero[:, :]).then_inc(t1_filled, 16)
            act.wait_ge(comp_turned, 1)
            nc.scalar.copy(compT[:, :], ps_ct[:, :]).then_inc(comp_copied, 1)
            for k in range(8):
                act.wait_ge(rel_made, k + 1)
                nc.scalar.copy(wrel[:, k * 512:(k + 1) * 512], ps_rel[:, :]).then_inc(rel_copied, 1)

        @block.vector
        def _(dve):
            step = Chain(dve, dve_steps)
            nc.vector.memset(g.zero[:, :], 0.0).then_inc(zero_set, 1)
            for k, pad in enumerate([0, TRASH, R]):
                nc.vector.memset(rows_i[:, k, 3, :], pad).then_inc(rows_padded, 1)
            nc.vector.memset(rows_f[:, 3, 3, :], 0.0).then_inc(rows_padded, 1)
            nc.vector.memset(recpad[:, :, :], 0.0).then_inc(recpad_set, 1)
            dve.wait_ge(recpad_set, 1)
            nc.vector.memset(recpad[:, :, 1:2], float(TRASH)).then_inc(recpad_set, 1)
            nc.vector.memset(g.onesf[:, :], 1.0)
            nc.vector.memset(g.onesb[:, :], 1.0)
            nc.vector.memset(g.eps[:, :], EPS)
            step(nc.vector.memset(g.wblk[:, :, :], 0.0))
            step(nc.vector.memset(g.rec[:, :, 3:4], 0.0))
            dve.wait_ge(edges_loaded, 12 * 16)
            nc.vector.tensor_copy(rows_f[:, 0:3], rows_i[:, :]).then_inc(rows_converted, 1)
            dve.wait_ge(consts_made, 1)
            nc.vector.tensor_scalar(cent[:, :], g.ident[0:D, 0:D], -1.0 / D, None, ALU.add).then_inc(centering_made, 1)
            for h in range(2):
                half = slice(h * D, (h + 1) * D)
                nc.vector.tensor_scalar(g.wblk[half, 3, half], g.ident[half, half], -1.0 / D, None, ALU.add)
            nc.vector.tensor_copy(g.beforeb[:, :], g.before[:, 0, 0:P])
            dve.wait_ge(vectors_loaded, 160)
            for j, name in enumerate(["b1", "b2"]):
                step(nc.vector.tensor_reduce(bsum[:, j:j + 1], g.vec(name), AX.X, ALU.add))
                step(nc.vector.tensor_scalar(bsum[:, j:j + 1], bsum[:, j:j + 1], -1.0 / D, None, ALU.mult))
                step(nc.vector.tensor_scalar(g.vec(name), g.vec(name), bsum[:, j:j + 1], None, ALU.add))
            dve.wait_ge(columns_made, 1)
            nc.vector.tensor_copy(g.srcidx[:, :], ps_edge[0][:, :])
            step(nc.vector.tensor_copy(g.dcol[:, :], ps_edge[1][:, :]))
            step(nc.vector.tensor_copy(tcol[:, :], ps_edge[2][:, :]))
            for q in range(4):
                t = slice(q * TB, (q + 1) * TB)
                nc.vector.tensor_tensor(sort.onehot[:, t, :], bc(g.iota_rel[:, :], [P, TB, R], 1),
                                        bc(tcol[:, t], [P, TB, R], 2), ALU.is_equal).then_inc(onehot_made, 1)
            for f, a in enumerate([0, 1, 3]):
                nc.vector.tensor_copy(g.rec[:, :, f], ps_edge[a][:, :])
            nc.vector.tensor_tensor(g.ddump[:, :].rearrange("p (g j) -> p g j", j=2),
                                    bc(g.dumpcol[:, :], [P, TILES // 2, 2], 1),
                                    g.dcol[:, :].rearrange("p (g j) -> p g j", j=2), ALU.subtract)
            dve.wait_ge(weights_turned, 1)
            nc.vector.tensor_copy(g.wst1[:, :], ps_w[:, 0, :])
            nc.vector.tensor_copy(g.wst2[:, :], ps_w[:, 1, :])
            for k in range(3):
                for h in range(2):
                    nc.vector.tensor_copy(g.wblk[h * D:(h + 1) * D, k, h * D:(h + 1) * D],
                                          ps_w[h * D:(h + 1) * D, 2 + k, :])
            nc.vector.tensor_copy(g.biases[:, :, :], bc(g.vec("bias"), [P, J, D], 1))
            dve.wait_ge(counted, 1)
            step(nc.vector.tensor_reduce(count[:, :], ps_count[:, :, :].rearrange("p k r -> p r k"), AX.X, ALU.add))
            step(nc.vector.tensor_scalar(count_i[:, :], count[:, :], float(HALF - 1), None, ALU.add))
            step(nc.vector.tensor_scalar(halves_i[:, :], count_i[:, :], 6, None, ALU.arith_shift_right))
            step(nc.vector.tensor_scalar(halves_f[:, :], halves_i[:, :], 1.0, None, ALU.max))
            step(nc.vector.tensor_tensor_scan(hend[:, :], g.onesf[:, 0:R], halves_f[:, :], 0.0, ALU.mult, ALU.add))
            step(nc.vector.tensor_tensor(sort.base[:, :], hend[:, :], halves_f[:, :], ALU.subtract))
            step(nc.vector.tensor_scalar(sort.base[:, :], sort.base[:, :], float(HALF), None, ALU.mult))
            step(nc.vector.tensor_tensor(cmp[:, :, :], bc(g.iota_half[:, :], [P, HB, R], 2),
                                         bc(hend[:, :], [P, HB, R], 1), ALU.is_ge))
            step(nc.vector.tensor_reduce(htype[:, :], cmp[:, :, :], AX.X, ALU.add))
            nc.vector.tensor_scalar(htype_i[:, :], htype[:, :], float(R - 1), float(D), ALU.min,
                                    ALU.mult).then_inc(types_made, 1)


def edge_phase(nc, g, tag, x, dst_rows, srcidx, dcol, ddump, table, width, wst, lin_out, wblk, lin_bias, supers,
               wcol=None, wrel=None, sort=None, table_filled=None, fill=None, x0=None, xc_out=None,
               keep=None):
    s = Scope(nc, tag)
    kept_chunks = 0 if keep is None else KEEP
    relation = wrel is not None
    degree = width > D
    with s:
        XD = 0 if relation else D
        xg = s.sb("xg", [P, 4, 2, D + 2 * XD])
        xb = s.sb("xb", [P, 2, 2, P]) if relation else None
        gidx = s.sb("gidx", [P, 4, 2], i32)
        sidx = s.sb("sidx", [P, 4, 2], i32)
        first = s.sb("first", [P, 4, 2])
        drow = s.sb("drow", [P, 4, 2 * P])
        same = s.sb("same", [P, 4, 2, 2 * P])
        dup = s.sb("dup", [P, 4, 2, 2 * P], bf16)
        Z = 2 if relation else 1
        zs = s.sb("zs", [P, 2, Z, 2 * P])
        outs = s.sb("outs", [P, 4, 2, width])
        wslot = s.sb("wslot", [P, 4, 2, D]) if relation else None
        xf = s.sb("xf", [P, J // 2, P])
        xt = s.sb("xt", [P, 2, 512])
        lf = s.sb("lf", [P, J * D])
        xr = s.sb("xr", [P, J * D]) if xc_out is not None else None
        xs = s.sb("xs", [P, J * D]) if xc_out is not None else None
        xmean = s.sb("xmean", [P, J]) if xc_out is not None else None
        if sort:
            work = s.sb("work", [P, 4, R])
            pos_i = s.sb("pos_i", [P, TILES], i32)
            tile_i = s.sb("tile_i", [P, TILES], i32)
            slot_i = s.sb("slot_i", [P, TILES], i32)
        ps_z = [s.ps(f"ps_z{a}", [P, Z, 2 * P]) for a in range(2)]
        ps_o = [s.ps(f"ps_o{a}", [P, 512]) for a in range(2)]
        ps_d = s.ps("ps_d", [P, 2])
        ps_r = s.ps("ps_r", [P, 5, R])
        ps_t = s.ps("ps_t", [P, 512])
        ps_l = s.ps("ps_l", [P, 512])

        drow_loaded = [s.sem(f"drow_loaded{q}") for q in range(4)]
        gathered = [s.sem(f"gathered{q}") for q in range(4)]
        w_loaded = [s.sem(f"w_loaded{q}") for q in range(4)] if relation else None
        scattered = s.sem("scattered")
        xg_zeroed = s.sem("xg_zeroed")
        gidx_ready = s.sem("gidx_ready")
        select_ready = s.sem("select_ready")
        dups_counted = s.sem("dups_counted")
        dups_read = s.sem("dups_read")
        sidx_ready = s.sem("sidx_ready")
        z_ready = s.sem("z_ready")
        spread = s.sem("spread") if relation else z_ready
        z_copied = s.sem("z_copied")
        out_ready = s.sem("out_ready")
        out_copied = s.sem("out_copied")
        pool_tick = s.sem("pool_tick")
        xf_loaded = s.sem("xf_loaded")
        turned = s.sem("turned")
        turned_copied = s.sem("turned_copied")
        lin_ready = s.sem("lin_ready")
        lin_done = s.sem("lin_done")
        lin_stored = s.sem("lin_stored")
        filled = s.sem("filled")
        ranked, rank_used, summed, masked = s.sem("ranked"), s.sem("rank_used"), s.sem("summed"), s.sem("masked")
        placed, last_steps = s.sem("placed"), s.sem("last_steps")
        xr_loaded, xc_summed, xc_meaned = s.sem("xr_loaded"), s.sem("xc_summed"), s.sem("xc_meaned")
        xc_scaled, xc_ready, xc_stored = s.sem("xc_scaled"), s.sem("xc_ready"), s.sem("xc_stored")
        block = s.block()
        last_super = supers - 1

        def over_supers(eng, body):
            cuts = sorted({0, 1, *([kept_chunks, kept_chunks + 1] if keep is not None else []), CHUNKS - 2, CHUNKS - 1, CHUNKS, CHUNKS + 1, last_super, supers})
            for a, b in zip(cuts, cuts[1:]):
                if b > supers:
                    break
                if b - a == 1:
                    body(a, a)
                else:
                    with eng.Fori(a, b) as c:
                        body(c, a)

        def parts(at):
            return 0 if not 0 <= at < CHUNKS else PLAST if at == CHUNKS - 1 else P

        def chunk(tensor, c, at):
            return tile_rows(tensor, c * CH, parts(at) * J)

        @block.sync
        def _(sp):
            def load_select(grp, q, old):
                if old:
                    sp.wait_ge(select_ready, grp - 3)
                src = dst_rows[ds(256 * grp, 256)].unsqueeze(0).to_broadcast([P, 256])
                sp.dma_start(drow[:, q, :], src).then_inc(drow_loaded[q], 16)

            def load_weights(grp, q, old):
                _, rows = nc.values_load_multi_w_load_instructions(
                    g.wrow[0:1, ds(2 * grp, 2)], engines=(mybir.EngineType.SP,), min_val=0,
                    max_val=2 * (R - 1) * D)
                if old:
                    sp.wait_ge(out_ready, grp - 3)
                for i in range(2):
                    sp.dma_start(wslot[:, q, i, :], wrel[ds(rows[i], 2 * D), :]).then_inc(w_loaded[q], 16)

            load_select(0, 0, False)
            load_select(1, 1, False)
            if relation:
                load_weights(0, 0, False)

            def body(c, at):
                for q in range(4):
                    if at < last_super or q < 2:
                        load_select(4 * c + q + 2, (q + 2) % 4, at > 0 or q >= 2)
                    if relation and (at < last_super or q < 3):
                        load_weights(4 * c + q + 1, (q + 1) % 4, at > 0 or q == 3)
                    if q == 1 and fill is not None and parts(at):
                        sp.dma_start(tile_rows(fill[0], c * CH, CH), fill[1]).then_inc(filled, 16)

            over_supers(sp, body)
            if fill is not None:
                sp.wait_ge(filled, 16 * CHUNKS)

        @block.gpsimd
        def _(pool):
            def gather(c, q, used):
                grp = 4 * c + q
                pool.wait_ge(gidx_ready, grp + 1)
                if used:
                    pool.wait_ge(spread, grp - 3)
                else:
                    pool.wait_ge(xg_zeroed, 1)
                pool.sem_inc(pool_tick, 1)
                for i in range(2):
                    pool.indirect_dma_start(out=xg[:, q, i, XD:XD + D], out_offset=None, in_=x[:, :],
                                            in_offset=bass.IndirectOffsetOnAxis(ap=gidx[:, q, i:i + 1], axis=0)
                                            ).then_inc(gathered[q], 16)

            for q in range(3):
                gather(0, q, False)
            if table_filled is not None:
                pool.wait_ge(table_filled, 16 * CHUNKS)

            def body(c, at):
                for q in range(4):
                    if q < 1:
                        gather(c, q + 3, at > 0)
                    elif at < last_super:
                        gather(c + 1, q - 1, True)
                    grp = 4 * c + q
                    pool.wait_ge(sidx_ready, grp + 1)
                    pool.wait_ge(out_copied, grp + 1)
                    if at > 0 or q > 0:
                        pool.wait_ge(scattered, 32 * grp)
                    pool.sem_inc(pool_tick, 1)
                    for j in range(2):
                        pool.indirect_dma_start(out=table[:, :],
                                                out_offset=bass.IndirectOffsetOnAxis(ap=sidx[:, q, j:j + 1], axis=0),
                                                in_=outs[:, q, j, :], in_offset=None,
                                                compute_op=ALU.add).then_inc(scattered, 16)

            over_supers(pool, body)
            pool.wait_ge(scattered, 32 * 4 * supers)

        @block.vector
        def _(dve):
            nc.vector.memset((xb if relation else xg)[:, :, :, :], 0.0).then_inc(xg_zeroed, 1)

            def stage_gather(c, q, used):
                grp = 4 * c + q
                if used:
                    dve.wait_ge(gathered[q], 32 * c)
                nc.vector.tensor_copy(gidx[:, q, :], srcidx[:, ds(2 * grp, 2)]).then_inc(gidx_ready, 1)

            def select(c, q, used):
                grp = 4 * c + q
                dve.wait_ge(drow_loaded[q], 16 * (c + 1))
                if used:
                    dve.wait_ge(z_ready, grp - 3)
                for i in range(2):
                    col = ds(2 * grp + i, 1)
                    if wcol is None:
                        nc.vector.tensor_scalar(same[:, q, i, :], drow[:, q, :], dcol[:, col], None, ALU.is_equal)
                    else:
                        nc.vector.tensor_scalar(same[:, q, i, :], drow[:, q, :], dcol[:, col], wcol[:, col],
                                                ALU.is_equal, ALU.mult)
                for i in range(2):
                    col = ds(2 * grp + i, 1)
                    last = nc.vector.scalar_tensor_tensor(dup[:, q, i, :], drow[:, q, :], dcol[:, col],
                                                          g.before[:, i, :], ALU.is_equal, ALU.mult)
                last.then_inc(select_ready, 1)

            def place(c, h):
                b = 2 * c + h
                dve.wait_ge(ranked, b + 1)
                if not isinstance(b, int) or b > 0:
                    dve.wait_ge(rank_used, b)
                nc.vector.tensor_tensor(work[:, :, :], ps_r[:, 0:4, :], bc(sort.base[:, :], [P, 4, R], 1),
                                        ALU.add).then_inc(summed, 1)
                dve.wait_ge(summed, b + 1)
                nc.vector.tensor_tensor(sort.base[:, :], sort.base[:, :], ps_r[:, 4, :],
                                        ALU.add).then_inc(rank_used, 1)
                nc.vector.tensor_tensor(work[:, :, :], work[:, :, :], sort.onehot[:, ds(4 * b, 4), :],
                                        ALU.mult).then_inc(masked, 1)
                dve.wait_ge(masked, b + 1)
                nc.vector.tensor_reduce(sort.pos[:, ds(4 * b, 4)], work[:, :, :], AX.X, ALU.add).then_inc(placed, 1)

            def add_other(c, at):
                n = parts(at)
                dve.wait_ge(xf_loaded, 16 * (c + 1))
                dve.wait_ge(xr_loaded, 16 * (c + 1))
                if at > 0:
                    dve.wait_ge(xc_stored, 16 * c)
                nc.vector.tensor_tensor(xs[0:n, :], xr[0:n, :], xf[0:n, :, :].rearrange("p a b -> p (a b)"),
                                        ALU.add).then_inc(xc_summed, 1)

            def means(c, at):
                n = parts(at)
                dve.wait_ge(xc_summed, c + 1)
                nc.vector.tensor_reduce(xmean[0:n, :], xs[0:n, :].rearrange("p (j d) -> p j d", d=D), AX.X,
                                        ALU.add).then_inc(xc_meaned, 1)
                dve.wait_ge(xc_meaned, c + 1)
                nc.vector.tensor_scalar(xmean[0:n, :], xmean[0:n, :], 1.0 / D, None, ALU.mult).then_inc(xc_scaled, 1)

            def subtract_means(c, at):
                n = parts(at)
                x3 = xs[0:n, :].rearrange("p (j d) -> p j d", d=D)
                dve.wait_ge(xc_scaled, c + 1)
                nc.vector.tensor_tensor(x3, x3, bc(xmean[0:n, :], [n, J, D], 2), ALU.subtract).then_inc(xc_ready, 1)

            for q in range(3):
                stage_gather(0, q, False)
            select(0, 0, False)

            def body(c, at):
                for q in range(4):
                    if q < 1:
                        stage_gather(c, q + 3, at > 0)
                    elif at < last_super:
                        stage_gather(c + 1, q - 1, True)
                    if q < 3:
                        select(c, q + 1, at > 0)
                    elif at < last_super:
                        select(c + 1, 0, True)
                    grp = 4 * c + q
                    cols = ds(2 * grp, 2)
                    dve.wait_ge(dups_counted, grp + 1)
                    nc.vector.scalar_tensor_tensor(first[:, q, :], ps_d[:, :], 1.0,
                                                   ddump[:, cols], ALU.min, ALU.mult).then_inc(dups_read, 1)
                    dve.wait_ge(dups_read, grp + 1)
                    if at > 0:
                        dve.wait_ge(scattered, 32 * (grp - 3))
                    nc.vector.tensor_tensor(sidx[:, q, :], first[:, q, :], dcol[:, cols],
                                            ALU.add).then_inc(sidx_ready, 1)
                    if sort and q in (1, 3):
                        place(c, q // 2)
                    if x0 is not None and parts(at):
                        if q == 1:
                            add_other(c, at)
                        elif q == 2:
                            means(c, at)
                        elif q == 3:
                            subtract_means(c, at)
                    if parts(at) and q >= 2:
                        h, n = q - 2, parts(at)
                        dve.wait_ge(lin_ready, 2 * c + h + 1)
                        if at > kept_chunks:
                            dve.wait_ge(lin_stored, 16 * (c - kept_chunks))
                        half = slice(h * 512, (h + 1) * 512)
                        nc.vector.tensor_tensor(
                            (lf[0:n, half] if at >= kept_chunks else keep[:, ds(c, 1), half].rearrange(
                                "p c x -> p (c x)")).rearrange("p (j d) -> p j d", d=D),
                            ps_l[0:n, :].rearrange("p (j d) -> p j d", d=D),
                            bc(lin_bias[0:n, :], [n, 8, D], 1), ALU.add).then_inc(lin_done, 1)

            over_supers(dve, body)
            if sort:
                dve.wait_ge(placed, 2 * SUPERS)
                step = Chain(dve, last_steps)
                step(nc.vector.tensor_copy(pos_i[:, :], sort.pos[:, :]))
                step(nc.vector.tensor_scalar(tile_i[:, :], pos_i[:, :], 7, None, ALU.arith_shift_right))
                step(nc.vector.tensor_scalar(slot_i[:, :], pos_i[:, :], P - 1, None, ALU.bitwise_and))
                nc.vector.scalar_tensor_tensor(g.posidx[:, :], slot_i[:, :], float(RTILES), tile_i[:, :], ALU.mult,
                                               ALU.add)

        @block.tensor
        def _(pe):
            def rank(c, h):
                b = 2 * c + h
                if not isinstance(b, int) or b > 0:
                    pe.wait_ge(rank_used, b)
                nc.tensor.matmul(ps_r[:, 0:4, :], g.beforeb[:, :], sort.onehot[:, ds(4 * b, 4), :],
                                 start=True, stop=False)
                for k in range(1, 4):
                    nc.tensor.matmul(ps_r[:, k:4, :], g.onesb[:, :], sort.onehot[:, ds(4 * b, 4 - k), :],
                                     start=False, stop=(k == 3))
                for k in range(4):
                    last = nc.tensor.matmul(ps_r[:, 4, :], g.onesb[:, :], sort.onehot[:, ds(4 * b + k, 1), :],
                                            start=(k == 0), stop=(k == 3))
                last.then_inc(ranked, 1)

            def body(c, at):
                for q in range(4):
                    grp, a = 4 * c + q, q % 2
                    ready = at > 0 or q >= 2
                    if sort and q in (1, 3):
                        rank(c, q // 2)
                    pe.wait_ge(select_ready, grp + 1)
                    if at > 0 or q > 0:
                        pe.wait_ge(dups_read, grp)
                    for j in range(2):
                        for i in range(2):
                            last = nc.tensor.matmul(ps_d[:, j:j + 1],
                                                    dup[:, q, i, j * P:(j + 1) * P], g.onesb[:, 0:1],
                                                    start=(i == 0), stop=(i == 1))
                    last.then_inc(dups_counted, 1)
                    if ready:
                        pe.wait_ge(out_copied, grp - 1)
                    if degree:
                        for j in range(2):
                            for i in range(2):
                                nc.tensor.matmul(ps_o[a][:, j * width + D:j * width + D + 1],
                                                 same[:, q, i, j * P:(j + 1) * P], g.onesf[:, 0:1],
                                                 start=(i == 0), stop=(i == 1))
                    if relation:
                        pe.wait_ge(spread, grp + 1)
                    else:
                        pe.wait_ge(gathered[q], 32 * (c + 1))
                    if ready:
                        pe.wait_ge(z_copied, grp - 1)
                    for i in range(2):
                        last = nc.tensor.matmul(ps_z[a][:, i if relation else 0, :],
                                                xb[:, a, i, :] if relation else xg[:, q, i, (1 - i) * D:(3 - i) * D],
                                                same[:, q, i, :], start=(relation or i == 0),
                                                stop=(relation or i == 1))
                    last.then_inc(z_ready, 1)
                    n = parts(at)
                    if n and q < 2:
                        if q == 0:
                            pe.wait_ge(xf_loaded, 16 * (c + 1))
                        if at > 0 or q > 0:
                            pe.wait_ge(turned_copied, 2 * c + q)
                        for k in range(4):
                            last = nc.tensor.transpose(ps_t[:, k * n:(k + 1) * n], xf[0:n, 4 * q + k, :],
                                                       g.ident[0:n, 0:n])
                        last.then_inc(turned, 1)
                    if n and q >= 2:
                        h = q - 2
                        pe.wait_ge(turned_copied, 2 * c + h + 1)
                        if at > 0 or h > 0:
                            pe.wait_ge(lin_done, 2 * c + h)
                        for k in range(4):
                            last = nc.tensor.matmul(ps_l[0:n, k * P:(k + 1) * P], xt[:, h, k * n:(k + 1) * n],
                                                    wblk, start=True, stop=True)
                        last.then_inc(lin_ready, 1)
                    pe.wait_ge(z_copied, grp + 1)
                    if relation:
                        pe.wait_ge(w_loaded[q], 32 * (c + 1))
                    for j in range(2):
                        for i in range(Z):
                            last = nc.tensor.matmul(ps_o[a][:, j * width:j * width + D],
                                                    zs[:, a, i, j * P:(j + 1) * P],
                                                    wslot[:, q, i, :] if relation else wst[:, :],
                                                    start=(i == 0), stop=(i == Z - 1))
                    last.then_inc(out_ready, 1)

            over_supers(pe, body)

        @block.scalar
        def _(act):
            def spread_rows(c, q, old):
                grp, a = 4 * c + q, q % 2
                act.wait_ge(gathered[q], 32 * (c + 1))
                act.wait_ge(xg_zeroed, 1)
                if old:
                    act.wait_ge(z_ready, grp - 1)
                for h in range(2):
                    rows = slice(h * HALF, (h + 1) * HALF)
                    last = nc.scalar.copy(xb[rows, a, :, h * D:(h + 1) * D], xg[rows, q, :, :])
                last.then_inc(spread, 1)

            def load_rows(c, at):
                n = parts(at)
                act.dma_start(xf[0:n, :, :].rearrange("p a b -> p (a b)"), chunk(x, c, at)).then_inc(xf_loaded, 16)

            def load_other(c, at):
                act.dma_start(xr[0:parts(at), :], chunk(x0, c, at)).then_inc(xr_loaded, 16)

            def store_sums(c, at):
                act.dma_start(chunk(xc_out, c, at), xs[0:parts(at), :]).then_inc(xc_stored, 16)

            load_rows(0, 0)
            if x0 is not None:
                load_other(0, 0)
            if relation:
                spread_rows(0, 0, False)

            def body(c, at):
                for q in range(4):
                    grp, a = 4 * c + q, q % 2
                    if relation and q < 3:
                        spread_rows(c, q + 1, at > 0 or q >= 1)
                    elif relation and at < last_super:
                        spread_rows(c + 1, 0, True)
                    act.wait_ge(z_ready, grp + 1)
                    if at > 0 or q >= 2:
                        act.wait_ge(out_ready, grp - 1)
                    nc.scalar.copy(zs[:, a, :, :], ps_z[a][:, :, :]).then_inc(z_copied, 1)
                    n = parts(at)
                    if n and q < 2:
                        act.wait_ge(turned, 2 * c + q + 1)
                        if at > 0:
                            act.wait_ge(lin_ready, 2 * c + q - 1)
                        nc.scalar.copy(xt[:, q, 0:4 * n], ps_t[:, 0:4 * n]).then_inc(turned_copied, 1)
                    act.wait_ge(out_ready, grp + 1)
                    if at > 0:
                        act.wait_ge(scattered, 32 * (grp - 3))
                    nc.scalar.copy(outs[:, q, :, :].rearrange("p j w -> p (j w)"),
                                   ps_o[a][:, 0:2 * width]).then_inc(out_copied, 1)
                    if q == 0 and parts(at - 1) and at > kept_chunks:
                        act.wait_ge(lin_done, 2 * c)
                        act.dma_start(chunk(lin_out, c - 1, at - 1), lf[0:parts(at - 1), :]).then_inc(lin_stored, 16)
                    if q == 1 and x0 is not None and parts(at + 1):
                        act.wait_ge(xc_summed, c + 1)
                        load_other(c + 1, at + 1)
                    if q == 2 and parts(at + 1):
                        if x0 is not None:
                            act.wait_ge(xc_summed, c + 1)
                        act.wait_ge(turned, 2 * c + 2)
                        load_rows(c + 1, at + 1)
                    if q == 3 and x0 is not None and n:
                        act.wait_ge(xc_ready, c + 1)
                        store_sums(c, at)

            over_supers(act, body)
            if parts(last_super):
                act.wait_ge(lin_done, 2 * CHUNKS)
                act.dma_start(chunk(lin_out, CHUNKS - 1, CHUNKS - 1), lf[0:PLAST, :]).then_inc(lin_stored, 16)
            act.wait_ge(lin_stored, 16 * (CHUNKS - kept_chunks))
            if x0 is not None:
                act.wait_ge(xc_stored, 16 * CHUNKS)


DEEP = 4
PEEL = 3 * DEEP


def over_chunks(eng, stages):
    deepest = max(lag for _, lag in stages)

    def step(s, j, fixed):
        for stage, lag in stages:
            if fixed and not 0 <= s - lag < CHUNKS:
                continue
            n = PLAST if fixed and s - lag == CHUNKS - 1 else P
            stage(s - lag, (j - lag) % DEEP, n, s - lag if fixed else PEEL)

    for t in range(PEEL):
        step(t, t % DEEP, True)
    with eng.Fori(PEEL // DEEP, (CHUNKS - 1) // DEEP) as k:
        for j in range(DEEP):
            step(DEEP * k + j, j, False)
    for t in range(CHUNKS - 1, CHUNKS + deepest):
        step(t, t % DEEP, True)


def wide(ap, n, row=D):
    return ap[0:n, :].rearrange("p (j d) -> p j d", d=row)


class RecordScatter:

    def __init__(self, nc, g, s, table, first_tile):
        self.nc, self.g, self.table, self.first_tile = nc, g, table, first_tile
        self.idx = s.sb("rec_idx", [P, DEEP, 4], i32)
        self.val = s.sb("rec_val", [P, DEEP, 4, 4])
        self.staged = s.sem("rec_staged")
        self.landed = [s.sem(f"rec_landed{j}") for j in range(DEEP)]
        self.tick = s.sem("rec_tick")
        self.lots = [0] * DEEP

    def tiles(self, c):
        return [k for k in range(4) if not isinstance(c, int) or self.first_tile + 4 * c + k <= LAST_TILE]

    def stage(self, eng):
        def run(c, j, n, age):
            if age >= DEEP:
                eng.wait_ge(self.landed[j], self.done(c, j))
            cols = ds(4 * c + self.first_tile, 4)
            self.nc.vector.tensor_copy(self.idx[:, j, :], self.g.posidx[:, cols])
            self.nc.vector.tensor_copy(self.val[:, j, :, :], self.g.rec[:, cols, :]).then_inc(self.staged, 1)
        return run

    def done(self, c, j):
        return 64 * ((c - j) // DEEP) if isinstance(c, int) else 16 * (c - j)

    def scatter(self, pool):
        def run(c, j, n, age):
            pool.wait_ge(self.staged, c + 1)
            pool.sem_inc(self.tick, 1)
            for k in self.tiles(c):
                rows = P
                if isinstance(c, int) and self.first_tile + 4 * c + k == LAST_TILE:
                    rows = LAST_ROWS
                pool.indirect_dma_start(out=self.table[:, :],
                                        out_offset=bass.IndirectOffsetOnAxis(ap=self.idx[0:rows, j, k:k + 1], axis=0),
                                        in_=self.val[0:rows, j, k, :], in_offset=None).then_inc(self.landed[j], 16)
        return run

    def wait_all(self, pool):
        for j in range(DEEP):
            chunks = [c for c in range(CHUNKS) if c % DEEP == j]
            pool.wait_ge(self.landed[j], 16 * sum(len(self.tiles(c)) for c in chunks))


def norm_phase1(nc, g, table, lin, h_out, recs):
    s = Scope(nc, "n1")
    with s:
        W = J * (D + 1)
        tin = s.sb("tin", [P, DEEP, W])
        rin = s.sb("rin", [P, DEEP, J * D])
        a = s.sb("a", [P, DEEP, J * D])
        sq = s.sb("sq", [P, 2, J * D])
        ht = s.sb("ht", [P, 2, J // 2, P])
        out = s.sb("out", [P, DEEP, J * D])
        deg = s.sb("deg", [P, DEEP, J])
        var = s.sb("var", [P, DEEP, J])
        ps_t = [s.ps(f"ps_t{k}", [P, J // 2, P]) for k in range(2)]
        ps_h = [s.ps(f"ps_h{k}", [P, J // 2, P]) for k in range(2)]
        rec = RecordScatter(nc, g, s, recs, 0)
        loaded = [s.sem(f"loaded{j}") for j in range(DEEP)]
        stored = [s.sem(f"stored{j}") for j in range(DEEP)]
        d1, inverted, divided, summed = s.sem("deg_max"), s.sem("inverted"), s.sem("divided"), s.sem("summed")
        squared, reduced, rooted = s.sem("squared"), s.sem("reduced"), s.sem("rooted")
        rsigma, scaled = s.sem("rsigma"), s.sem("scaled")
        turned, clipped, back, h_ready = s.sem("turned"), s.sem("clipped"), s.sem("back"), s.sem("h_ready")
        block = s.block()

        @block.sync
        def _(sp):
            def load(c, j, n, age):
                if age >= DEEP:
                    sp.wait_ge(summed, c - DEEP + 1)
                sp.dma_start(tin[0:n, j, :], tile_rows(table, c * CH, n * J)).then_inc(loaded[j], 16)
                sp.dma_start(rin[0:n, j, :], tile_rows(lin, c * CH, n * J)).then_inc(loaded[j], 16)

            def store(c, j, n, age):
                sp.wait_ge(h_ready, c + 1)
                sp.dma_start(tile_rows(h_out, c * CH, n * J), out[0:n, j, :]).then_inc(stored[j], 16)

            over_chunks(sp, [(load, 0), (store, 6)])
            for j in range(DEEP):
                sp.wait_ge(stored[j], 16 * len(range(j, CHUNKS, DEEP)))

        @block.vector
        def _(dve):
            def degree(c, j, n, age):
                dve.wait_ge(loaded[j], full(c, j, 32))
                nc.vector.tensor_scalar(deg[0:n, j, :], wide(tin[:, j, :], n, D + 1)[:, :, D], 1.0, None,
                                        ALU.max).then_inc(d1, 1)

            def invert(c, j, n, age):
                dve.wait_ge(d1, c + 1)
                nc.vector.reciprocal(g.inv[0:n, ds(c * J, J)], deg[0:n, j, :]).then_inc(inverted, 1)

            def divide(c, j, n, age):
                dve.wait_ge(inverted, c + 1)
                if age >= DEEP:
                    dve.wait_ge(turned, c - DEEP + 1)
                nc.vector.tensor_tensor(wide(a[:, j, :], n), wide(tin[:, j, :], n, D + 1)[:, :, 0:D],
                                        bc(g.inv[0:n, ds(c * J, J)], [n, J, D], 2), ALU.mult).then_inc(divided, 1)

            def add_lin(c, j, n, age):
                dve.wait_ge(divided, c + 1)
                nc.vector.tensor_tensor(a[0:n, j, :], a[0:n, j, :], rin[0:n, j, :], ALU.add).then_inc(summed, 1)

            def variance(c, j, n, age):
                dve.wait_ge(squared, c + 1)
                nc.vector.tensor_reduce(var[0:n, j, :], wide(sq[:, j % 2, :], n), AX.X, ALU.add).then_inc(reduced, 1)

            def invert_root(c, j, n, age):
                dve.wait_ge(rooted, c + 1)
                nc.vector.reciprocal(var[0:n, j, :], var[0:n, j, :]).then_inc(rsigma, 1)

            def scale(c, j, n, age):
                dve.wait_ge(rsigma, c + 1)
                a3 = wide(a[:, j, :], n)
                nc.vector.tensor_tensor(a3, a3, bc(var[0:n, j, :], [n, J, D], 2), ALU.mult).then_inc(scaled, 1)

            over_chunks(dve, [(degree, 0), (variance, 1), (invert, 0), (rec.stage(dve), 0), (divide, 0),
                              (invert_root, 1), (add_lin, 0), (scale, 1)])

        @block.tensor
        def _(pe):
            def turn(c, j, n, age):
                pe.wait_ge(scaled, c + 1)
                if age >= 2:
                    pe.wait_ge(clipped, c - 1)
                for k in range(J // 2):
                    last = nc.tensor.transpose(ps_t[j % 2][:, k, 0:n], a[0:n, j, k * P:(k + 1) * P],
                                               g.ident[0:n, 0:n])
                last.then_inc(turned, 1)

            def turn_back(c, j, n, age):
                pe.wait_ge(clipped, c + 1)
                if age >= 2:
                    pe.wait_ge(h_ready, c - 1)
                for k in range(J // 2):
                    last = nc.tensor.transpose(ps_h[j % 2][0:n, k, :], ht[:, j % 2, k, 0:n], g.ident[:, :])
                last.then_inc(back, 1)

            over_chunks(pe, [(turn, 2), (turn_back, 3)])

        @block.scalar
        def _(act):
            def square(c, j, n, age):
                act.wait_ge(summed, c + 1)
                if age >= 2:
                    act.wait_ge(reduced, c - 1)
                nc.scalar.activation(sq[0:n, j % 2, :], a[0:n, j, :], ACT.Square).then_inc(squared, 1)

            def root(c, j, n, age):
                act.wait_ge(reduced, c + 1)
                nc.scalar.activation(var[0:n, j, :], var[0:n, j, :], ACT.Sqrt, bias=g.eps[0:n, :],
                                     scale=1.0 / D).then_inc(rooted, 1)

            def clip(c, j, n, age):
                act.wait_ge(turned, c + 1)
                if age >= 2:
                    act.wait_ge(back, c - 1)
                nc.scalar.activation(ht[:, j % 2, :, 0:n], ps_t[j % 2][:, :, 0:n], ACT.Relu, bias=g.gcols[:, 1:2],
                                     scale=g.gcols[:, 0:1]).then_inc(clipped, 1)

            def copy_out(c, j, n, age):
                act.wait_ge(back, c + 1)
                if age >= DEEP:
                    act.wait_ge(stored[j], full(c, j, 16) - 16)
                nc.scalar.copy(out[0:n, j, :].rearrange("p (k b) -> p k b", b=P),
                               ps_h[j % 2][0:n, :, :]).then_inc(h_ready, 1)

            over_chunks(act, [(root, 1), (square, 0), (clip, 2), (copy_out, 3)])

        @block.gpsimd
        def _(pool):
            over_chunks(pool, [(rec.scatter(pool), 0)])
            rec.wait_all(pool)


def full(c, j, each):
    return each * ((c - j) // DEEP + 1) if isinstance(c, int) else each // DEEP * (c - j) + each


def norm_phase2(nc, g, table, lin, xc, x1_out, recs):
    s = Scope(nc, "n2")
    with s:
        W = J * D
        tin = s.sb("tin", [P, DEEP, W])
        rin = s.sb("rin", [P, DEEP, W])
        xin = s.sb("xin", [P, DEEP, W])
        a = s.sb("a", [P, DEEP, W])
        sq = s.sb("sq", [P, 2, W])
        ht = s.sb("ht", [P, 2, J // 2, P])
        sq2 = s.sb("sq2", [P, 2, W])
        out = s.sb("out", [P, DEEP, W])
        var = s.sb("var", [P, DEEP, J])
        var2 = s.sb("var2", [P, DEEP, J])
        ps_t = [s.ps(f"ps_t{k}", [P, J // 2, P]) for k in range(2)]
        ps_h = [s.ps(f"ps_h{k}", [P, J // 2, P]) for k in range(2)]
        rec = RecordScatter(nc, g, s, recs, 4 * CHUNKS)
        loaded = [s.sem(f"loaded{j}") for j in range(DEEP)]
        x_loaded = [s.sem(f"x_loaded{j}") for j in range(DEEP)]
        stored = [s.sem(f"stored{j}") for j in range(DEEP)]
        divided, summed, squared, reduced = s.sem("divided"), s.sem("summed"), s.sem("squared"), s.sem("reduced")
        rooted, rsigma, scaled = s.sem("rooted"), s.sem("rsigma"), s.sem("scaled")
        turned, clipped, back, joined = s.sem("turned"), s.sem("clipped"), s.sem("back"), s.sem("joined")
        squared2, reduced2, rooted2 = s.sem("squared2"), s.sem("reduced2"), s.sem("rooted2")
        rsigma2, out_ready = s.sem("rsigma2"), s.sem("out_ready")
        block = s.block()

        @block.sync
        def _(sp):
            def load(c, j, n, age):
                if age >= DEEP:
                    sp.wait_ge(summed, c - DEEP + 1)
                sp.dma_start(tin[0:n, j, :], tile_rows(table, c * CH, n * J)).then_inc(loaded[j], 16)
                sp.dma_start(rin[0:n, j, :], tile_rows(lin, c * CH, n * J)).then_inc(loaded[j], 16)

            def load_x(c, j, n, age):
                if age >= DEEP:
                    sp.wait_ge(joined, c - DEEP + 1)
                sp.dma_start(xin[0:n, j, :], tile_rows(xc, c * CH, n * J)).then_inc(x_loaded[j], 16)

            def store(c, j, n, age):
                sp.wait_ge(out_ready, c + 1)
                sp.dma_start(tile_rows(x1_out, c * CH, n * J), out[0:n, j, :]).then_inc(stored[j], 16)

            over_chunks(sp, [(load, 0), (load_x, 1), (store, 8)])
            for j in range(DEEP):
                sp.wait_ge(stored[j], 16 * len(range(j, CHUNKS, DEEP)))

        @block.gpsimd
        def _(pool):
            def add_lin(c, j, n, age):
                pool.wait_ge(divided, c + 1)
                nc.gpsimd.tensor_tensor(a[0:n, j, :], a[0:n, j, :], rin[0:n, j, :], ALU.add).then_inc(summed, 1)

            over_chunks(pool, [(add_lin, 0), (rec.scatter(pool), 0)])
            rec.wait_all(pool)

        @block.vector
        def _(dve):
            def divide(c, j, n, age):
                dve.wait_ge(loaded[j], full(c, j, 32))
                if age >= DEEP:
                    dve.wait_ge(turned, c - DEEP + 1)
                nc.vector.tensor_tensor(wide(a[:, j, :], n), wide(tin[:, j, :], n),
                                        bc(g.inv[0:n, ds(c * J, J)], [n, J, D], 2), ALU.mult).then_inc(divided, 1)

            def variance(c, j, n, age):
                dve.wait_ge(squared, c + 1)
                nc.vector.tensor_reduce(var[0:n, j, :], wide(sq[:, j % 2, :], n), AX.X, ALU.add).then_inc(reduced, 1)

            def invert_root(c, j, n, age):
                dve.wait_ge(rooted, c + 1)
                nc.vector.reciprocal(var[0:n, j, :], var[0:n, j, :]).then_inc(rsigma, 1)

            def scale(c, j, n, age):
                dve.wait_ge(rsigma, c + 1)
                a3 = wide(a[:, j, :], n)
                nc.vector.tensor_tensor(a3, a3, bc(var[0:n, j, :], [n, J, D], 2), ALU.mult).then_inc(scaled, 1)

            def join(c, j, n, age):
                dve.wait_ge(back, c + 1)
                dve.wait_ge(x_loaded[j], full(c, j, 16))
                if age >= DEEP:
                    dve.wait_ge(stored[j], full(c, j, 16) - 16)
                nc.vector.tensor_tensor(out[0:n, j, :].rearrange("p (k b) -> p k b", b=P), ps_h[j % 2][0:n, :, :],
                                        xin[0:n, j, :].rearrange("p (k b) -> p k b", b=P),
                                        ALU.add).then_inc(joined, 1)

            def variance2(c, j, n, age):
                dve.wait_ge(squared2, c + 1)
                nc.vector.tensor_reduce(var2[0:n, j, :], wide(sq2[:, j % 2, :], n), AX.X,
                                        ALU.add).then_inc(reduced2, 1)

            def invert_root2(c, j, n, age):
                dve.wait_ge(rooted2, c + 1)
                nc.vector.reciprocal(var2[0:n, j, :], var2[0:n, j, :]).then_inc(rsigma2, 1)

            def scale2(c, j, n, age):
                dve.wait_ge(rsigma2, c + 1)
                o3 = wide(out[:, j, :], n)
                nc.vector.tensor_tensor(o3, o3, bc(var2[0:n, j, :], [n, J, D], 2), ALU.mult).then_inc(out_ready, 1)

            over_chunks(dve, [(divide, 0), (variance2, 5), (variance, 2), (rec.stage(dve), 0), (invert_root2, 5),
                              (join, 4), (invert_root, 2), (scale2, 5), (scale, 2)])

        @block.tensor
        def _(pe):
            def turn(c, j, n, age):
                pe.wait_ge(scaled, c + 1)
                if age >= 2:
                    pe.wait_ge(clipped, c - 1)
                for k in range(J // 2):
                    last = nc.tensor.transpose(ps_t[j % 2][:, k, 0:n], a[0:n, j, k * P:(k + 1) * P],
                                               g.ident[0:n, 0:n])
                last.then_inc(turned, 1)

            def turn_back(c, j, n, age):
                pe.wait_ge(clipped, c + 1)
                if age >= 2:
                    pe.wait_ge(joined, c - 1)
                for k in range(J // 2):
                    last = nc.tensor.matmul(ps_h[j % 2][0:n, k, :], ht[:, j % 2, k, 0:n], g.wblk[:, 3, :],
                                            start=True, stop=True)
                last.then_inc(back, 1)

            over_chunks(pe, [(turn, 3), (turn_back, 3)])

        @block.scalar
        def _(act):
            def square(c, j, n, age):
                act.wait_ge(summed, c + 1)
                if age >= 2:
                    act.wait_ge(reduced, c - 1)
                nc.scalar.activation(sq[0:n, j % 2, :], a[0:n, j, :], ACT.Square).then_inc(squared, 1)

            def root(c, j, n, age):
                act.wait_ge(reduced, c + 1)
                nc.scalar.activation(var[0:n, j, :], var[0:n, j, :], ACT.Sqrt, bias=g.eps[0:n, :],
                                     scale=1.0 / D).then_inc(rooted, 1)

            def clip(c, j, n, age):
                act.wait_ge(turned, c + 1)
                if age >= 2:
                    act.wait_ge(back, c - 1)
                nc.scalar.activation(ht[:, j % 2, :, 0:n], ps_t[j % 2][:, :, 0:n], ACT.Relu, bias=g.gcols[:, 3:4],
                                     scale=g.gcols[:, 2:3]).then_inc(clipped, 1)

            def square2(c, j, n, age):
                act.wait_ge(joined, c + 1)
                if age >= 2:
                    act.wait_ge(reduced2, c - 1)
                nc.scalar.activation(sq2[0:n, j % 2, :], out[0:n, j, :], ACT.Square).then_inc(squared2, 1)

            def root2(c, j, n, age):
                act.wait_ge(reduced2, c + 1)
                nc.scalar.activation(var2[0:n, j, :], var2[0:n, j, :], ACT.Sqrt, bias=g.eps[0:n, :],
                                     scale=1.0 / D).then_inc(rooted2, 1)

            over_chunks(act, [(root2, 5), (root, 2), (clip, 3), (square, 1), (square2, 4)])


def reload_phase(nc, g, recs, dst2, type_rows):
    s = Scope(nc, "re")
    with s:
        rec = s.sb("rec", [P, RTILES, 4])
        htype = s.sb("htype", [1, RTILES, 2], i32)
        rows = s.sb("rows", [RTB, BLOCKS, P])
        ps_rows = s.ps("ps_rows", [RTB, BLOCKS, P])
        types_loaded = s.sem("types_loaded")
        loaded, turned, copied, stored = s.sem("loaded"), s.sem("turned"), s.sem("copied"), s.sem("stored")
        steps = s.sem("steps")
        block = s.block()

        @block.sync
        def _(sp):
            sp.dma_start(rec[:, :, :].rearrange("p t f -> p (t f)"),
                         recs.rearrange("(p t) f -> p (t f)", p=P)).then_inc(loaded, 16)
            sp.dma_start(htype[:, :, :].rearrange("p t h -> p (t h)"),
                         type_rows[0:2 * RTILES].unsqueeze(0)).then_inc(types_loaded, 16)
            sp.wait_ge(copied, 1)
            sp.dma_start(dst2.rearrange("(b r p) -> r b p", b=BLOCKS, p=P), rows[:, :, :]).then_inc(stored, 16)
            sp.wait_ge(stored, 16)

        @block.vector
        def _(dve):
            dve.wait_ge(loaded, 16)
            nc.vector.tensor_copy(g.dcol2[:, :], rec[:, :, 1]).then_inc(steps, 1)
            nc.vector.tensor_copy(g.srcidx2[:, :], rec[:, :, 0])
            nc.vector.tensor_copy(g.wcol2[:, :], rec[:, :, 2])
            dve.wait_ge(types_loaded, 16)
            nc.vector.tensor_copy(g.wrow[:, :], htype[:, :, 0]).then_inc(steps, 1)
            dve.wait_ge(steps, 2)
            nc.vector.tensor_tensor(g.wrow[:, :], g.wrow[:, :], htype[:, :, 1], ALU.add)
            dve.wait_ge(steps, 1)
            nc.vector.tensor_tensor(g.ddump2[:, :].rearrange("p (g j) -> p g j", j=2),
                                    bc(g.dumpcol[:, :], [P, RTILES // 2, 2], 1),
                                    g.dcol2[:, :].rearrange("p (g j) -> p g j", j=2), ALU.subtract)

        @block.tensor
        def _(pe):
            pe.wait_ge(steps, 1)
            for b in range(BLOCKS):
                last = nc.tensor.transpose(ps_rows[:, b, :], g.dcol2[:, b * RTB:(b + 1) * RTB], g.ident[:, :])
            last.then_inc(turned, 1)

        @block.scalar
        def _(act):
            act.wait_ge(turned, 1)
            nc.scalar.copy(rows[:, :, :], ps_rows[:, :, :]).then_inc(copied, 1)


def is_kept(j):
    return j % 2 == 1


def first_row(c, j):
    return c * (CH // 2) + (-(CH // 2) if is_kept(j) else KEEP * CH)


def kept_rows(keep, c):
    return keep[:, :, :].rearrange("p c x -> p (c x)")[:, ds(c * (J * D // 2) - J * D // 2, J * D)]


def stats_phase(nc, g, table, lin, y_out, keep):
    s = Scope(nc, "st")
    with s:
        W = J * D
        tin = s.sb("tin", [P, DEEP, W])
        rin = s.sb("rin", [P, DEEP // 2, W])
        y = s.sb("y", [P, DEEP // 2, W])
        sq = s.sb("sq", [P, DEEP, W])
        acc = s.sb("acc", [P, W])
        acc2 = s.sb("acc2", [P, W])
        both = s.sb("both", [P, 2, D])
        mean = s.sb("mean", [P, D])
        var = s.sb("var", [P, D])
        m2 = s.sb("m2", [P, D])
        shift2 = s.sb("shift2", [P, 2, D])
        ps_sum = s.ps("ps_sum", [P, 2, D])
        ps_shift = s.ps("ps_shift", [P, P])
        t_loaded = [s.sem(f"t_loaded{j}") for j in range(DEEP)]
        r_loaded = [s.sem(f"r_loaded{j}") for j in range(DEEP)]
        stored = [s.sem(f"stored{j}") for j in range(DEEP)]
        cleared, clipped, y_ready, squared = s.sem("cleared"), s.sem("clipped"), s.sem("y_ready"), s.sem("squared")
        acc_added, acc2_added = s.sem("acc_added"), s.sem("acc2_added")
        folded, totalled, rooted, steps = s.sem("folded"), s.sem("totalled"), s.sem("rooted"), s.sem("steps")
        act_tick = s.sem("act_tick")
        var_ready, shift_ready, shift_turned = s.sem("var_ready"), s.sem("shift_ready"), s.sem("shift_turned")
        block = s.block()

        @block.sync
        def _(sp):
            def load(c, j, n, age):
                if age >= DEEP:
                    sp.wait_ge(y_ready, c - DEEP + 1)
                sp.dma_start(tin[0:n, j, :], tile_rows(table, first_row(c, j), n * J)).then_inc(t_loaded[j], 16)
                if not is_kept(j):
                    sp.dma_start(rin[0:n, j // 2, :], tile_rows(lin, first_row(c, j), n * J)).then_inc(r_loaded[j], 16)

            def store(c, j, n, age):
                if is_kept(j):
                    return
                sp.wait_ge(y_ready, c + 1)
                sp.dma_start(tile_rows(y_out, first_row(c, j), n * J), y[0:n, j // 2, :]).then_inc(stored[j], 16)

            over_chunks(sp, [(load, 0), (store, 2)])
            for j in range(0, DEEP, 2):
                sp.wait_ge(stored[j], 16 * len(range(j, CHUNKS, DEEP)))

        @block.scalar
        def _(act):
            def clip(c, j, n, age):
                if not is_kept(j):
                    act.wait_ge(r_loaded[j], full(c, j, 16))
                lin_rows = kept_rows(keep, c) if is_kept(j) else rin[0:n, j // 2, :]
                nc.scalar.activation(lin_rows, lin_rows, ACT.Relu).then_inc(clipped, 1)

            def square(c, j, n, age):
                act.wait_ge(y_ready, c + 1)
                if age >= DEEP:
                    act.wait_ge(acc2_added, c - DEEP + 2)
                y_rows = kept_rows(keep, c) if is_kept(j) else y[0:n, j // 2, :]
                if is_kept(j):
                    act.sem_inc(act_tick, 1)
                nc.scalar.activation(sq[0:n, j, :], y_rows, ACT.Square).then_inc(squared, 1)

            over_chunks(act, [(clip, 0), (square, 1)])
            act.wait_ge(var_ready, 1)
            nc.scalar.activation(var[:, :], var[:, :], ACT.Sqrt, bias=g.eps[:, :], scale=1.0).then_inc(rooted, 1)

        @block.gpsimd
        def _(pool):
            nc.gpsimd.memset(acc2[:, :], 0.0).then_inc(acc2_added, 1)

            def add_squares(c, j, n, age):
                pool.wait_ge(squared, c + 1)
                pool.wait_ge(acc2_added, c + 1)
                nc.gpsimd.tensor_tensor(acc2[0:n, :], acc2[0:n, :], sq[0:n, j, :], ALU.add).then_inc(acc2_added, 1)

            over_chunks(pool, [(add_squares, 1)])

        @block.vector
        def _(dve):
            nc.vector.memset(acc[:, :], 0.0).then_inc(acc_added, 1)

            def make_y(c, j, n, age):
                dve.wait_ge(t_loaded[j], full(c, j, 16))
                dve.wait_ge(clipped, c + 1)
                if not is_kept(j) and age >= DEEP:
                    dve.wait_ge(stored[j], full(c, j, 16) - 16)
                    dve.wait_ge(acc_added, c - DEEP + 2)
                    dve.wait_ge(squared, c - DEEP + 1)
                lin_rows, y_rows = [kept_rows(keep, c)] * 2 if is_kept(j) else [rin[0:n, j // 2, :], y[0:n, j // 2, :]]
                nc.vector.scalar_tensor_tensor(y_rows, tin[0:n, j, :], 0.0, lin_rows, ALU.max,
                                               ALU.add).then_inc(y_ready, 1)

            def add(c, j, n, age):
                dve.wait_ge(y_ready, c + 1)
                dve.wait_ge(acc_added, c + 1)
                y_rows = kept_rows(keep, c) if is_kept(j) else y[0:n, j // 2, :]
                nc.vector.tensor_tensor(acc[0:n, :], acc[0:n, :], y_rows, ALU.add).then_inc(acc_added, 1)

            over_chunks(dve, [(make_y, 0), (add, 1)])
            step = Chain(dve, steps)
            dve.wait_ge(acc_added, CHUNKS + 1)
            dve.wait_ge(acc2_added, CHUNKS + 1)
            nc.vector.tensor_reduce(both[:, 0, :], acc[:, :].rearrange("p (j d) -> p d j", d=D), AX.X, ALU.add)
            nc.vector.tensor_reduce(both[:, 1, :], acc2[:, :].rearrange("p (j d) -> p d j", d=D), AX.X,
                                    ALU.add).then_inc(folded, 1)
            dve.wait_ge(totalled, 1)
            step(nc.vector.tensor_scalar(mean[:, :], ps_sum[:, 0, :], 1.0 / N, None, ALU.mult))
            step(nc.vector.tensor_tensor(m2[:, :], mean[:, :], mean[:, :], ALU.mult))
            nc.vector.scalar_tensor_tensor(var[:, :], ps_sum[:, 1, :], 1.0 / N, m2[:, :], ALU.mult,
                                           ALU.subtract).then_inc(var_ready, 1)
            dve.wait_ge(rooted, 1)
            step(nc.vector.reciprocal(m2[:, :], var[:, :]))
            step(nc.vector.tensor_tensor(g.bnab[:, 0, :], g.vec("gamma"), m2[:, :], ALU.mult))
            step(nc.vector.tensor_tensor(mean[:, :], mean[:, :], g.bnab[:, 0, :], ALU.mult))
            for h in range(2):
                last = nc.vector.tensor_tensor(shift2[:, h, :], g.vec("beta"), mean[:, :], ALU.subtract)
            last.then_inc(shift_ready, 1)
            dve.wait_ge(shift_turned, 1)
            nc.vector.tensor_copy(g.shiftcol[:, :], ps_shift[:, 0:1])

        @block.tensor
        def _(pe):
            pe.wait_ge(folded, 1)
            nc.tensor.matmul(ps_sum[:, :, :], g.onesf[:, :], both[:, :, :], start=True, stop=True).then_inc(totalled, 1)
            pe.wait_ge(shift_ready, 1)
            nc.tensor.transpose(ps_shift[:, :], shift2[:, :, :].rearrange("p h d -> p (h d)"),
                                g.ident[:, :]).then_inc(shift_turned, 1)


def final_phase(nc, g, x1, y, out_dram, keep):
    s = Scope(nc, "fi")
    with s:
        W = J * D
        xin = s.sb("xin", [P, DEEP, W])
        a = s.sb("a", [P, DEEP, W])
        at = s.sb("at", [P, 2, J // 2, P])
        sq = s.sb("sq", [P, 2, W])
        out = s.sb("out", [P, DEEP, W])
        var = s.sb("var", [P, DEEP, J])
        ps_t = [s.ps(f"ps_t{k}", [P, J // 2, P]) for k in range(2)]
        ps_c = [s.ps(f"ps_c{k}", [P, J // 2, P]) for k in range(2)]
        y_loaded = [s.sem(f"y_loaded{j}") for j in range(DEEP)]
        x_loaded = [s.sem(f"x_loaded{j}") for j in range(DEEP)]
        stored = [s.sem(f"stored{j}") for j in range(DEEP)]
        gained, joined, turned, copied = s.sem("gained"), s.sem("joined"), s.sem("turned"), s.sem("copied")
        centred, squared, reduced = s.sem("centred"), s.sem("squared"), s.sem("reduced")
        rooted, rsigma, out_ready = s.sem("rooted"), s.sem("rsigma"), s.sem("out_ready")
        block = s.block()

        @block.sync
        def _(sp):
            def load(c, j, n, age):
                if age >= DEEP:
                    sp.wait_ge(turned, c - DEEP + 1)
                if not is_kept(j):
                    sp.dma_start(a[0:n, j, :], tile_rows(y, first_row(c, j), n * J)).then_inc(y_loaded[j], 16)
                sp.dma_start(xin[0:n, j, :], tile_rows(x1, first_row(c, j), n * J)).then_inc(x_loaded[j], 16)

            def store(c, j, n, age):
                sp.wait_ge(out_ready, c + 1)
                sp.dma_start(tile_rows(out_dram, first_row(c, j), n * J), out[0:n, j, :]).then_inc(stored[j], 16)

            over_chunks(sp, [(load, 0), (store, 6)])
            for j in range(DEEP):
                sp.wait_ge(stored[j], 16 * len(range(j, CHUNKS, DEEP)))

        @block.gpsimd
        def _(pool):
            def join(c, j, n, age):
                pool.wait_ge(x_loaded[j], full(c, j, 16))
                pool.wait_ge(gained, c + 1)
                nc.gpsimd.tensor_tensor(a[0:n, j, :], a[0:n, j, :], xin[0:n, j, :], ALU.add).then_inc(joined, 1)

            over_chunks(pool, [(join, 1)])

        @block.vector
        def _(dve):
            def gain(c, j, n, age):
                if is_kept(j) and age >= DEEP:
                    dve.wait_ge(turned, c - DEEP + 1)
                if not is_kept(j):
                    dve.wait_ge(y_loaded[j], full(c, j, 16))
                y_rows = kept_rows(keep, c).rearrange("p (j d) -> p j d", d=D) if is_kept(j) else wide(a[:, j, :], n)
                nc.vector.tensor_tensor(wide(a[:, j, :], n), y_rows, bc(g.bnab[0:n, 0, :], [n, J, D], 1),
                                        ALU.mult).then_inc(gained, 1)

            def variance(c, j, n, age):
                dve.wait_ge(squared, c + 1)
                nc.vector.tensor_reduce(var[0:n, j, :], wide(sq[:, j % 2, :], n), AX.X, ALU.add).then_inc(reduced, 1)

            def invert_root(c, j, n, age):
                dve.wait_ge(rooted, c + 1)
                nc.vector.reciprocal(var[0:n, j, :], var[0:n, j, :]).then_inc(rsigma, 1)

            def scale(c, j, n, age):
                dve.wait_ge(rsigma, c + 1)
                if age >= DEEP:
                    dve.wait_ge(stored[j], full(c, j, 16) - 16)
                nc.vector.tensor_tensor(wide(out[:, j, :], n),
                                        ps_c[j % 2][0:n, :, :].rearrange("p k (i d) -> p (k i) d", d=D),
                                        bc(var[0:n, j, :], [n, J, D], 2), ALU.mult).then_inc(out_ready, 1)

            over_chunks(dve, [(variance, 4), (gain, 0), (invert_root, 4), (scale, 4)])

        @block.tensor
        def _(pe):
            def turn(c, j, n, age):
                pe.wait_ge(joined, c + 1)
                if age >= 2:
                    pe.wait_ge(copied, c - 1)
                for k in range(J // 2):
                    last = nc.tensor.transpose(ps_t[j % 2][:, k, 0:n], a[0:n, j, k * P:(k + 1) * P],
                                               g.ident[0:n, 0:n])
                last.then_inc(turned, 1)

            def centre(c, j, n, age):
                pe.wait_ge(copied, c + 1)
                if age >= 2:
                    pe.wait_ge(out_ready, c - 1)
                for k in range(J // 2):
                    last = nc.tensor.matmul(ps_c[j % 2][0:n, k, :], at[:, j % 2, k, 0:n], g.wblk[:, 3, :],
                                            start=True, stop=True)
                last.then_inc(centred, 1)

            over_chunks(pe, [(turn, 2), (centre, 3)])

        @block.scalar
        def _(act):
            def add_shift(c, j, n, age):
                act.wait_ge(turned, c + 1)
                if age >= 2:
                    act.wait_ge(centred, c - 1)
                nc.scalar.activation(at[:, j % 2, :, 0:n], ps_t[j % 2][:, :, 0:n], ACT.Identity,
                                     bias=g.shiftcol[:, :]).then_inc(copied, 1)

            def square(c, j, n, age):
                act.wait_ge(centred, c + 1)
                if age >= 2:
                    act.wait_ge(reduced, c - 1)
                nc.scalar.activation(sq[0:n, j % 2, :].rearrange("p (k b) -> p k b", b=P), ps_c[j % 2][0:n, :, :],
                                     ACT.Square).then_inc(squared, 1)

            def root(c, j, n, age):
                act.wait_ge(reduced, c + 1)
                nc.scalar.activation(var[0:n, j, :], var[0:n, j, :], ACT.Sqrt, bias=g.eps[0:n, :],
                                     scale=1.0 / D).then_inc(rooted, 1)

            over_chunks(act, [(root, 4), (add_shift, 2), (square, 3)])


def gnn_kernel(nc, io, out):
    def table(name, shape, dt=fp32):
        return nc.dram_tensor(name, shape, dt).ap()

    dr = {"t1": table("sums1", [TROWS, D + 1]), "t2": table("sums2", [TROWS, D]), "t3": table("sums3", [TROWS, D]),
          "lin1": table("lin1", [N, D]), "lin2": table("lin2", [N, D]), "lin3": table("lin3", [N, D]),
          "h1": table("h1", [N, D]), "xc": table("xc", [N, D]), "x1": table("x1", [N, D]), "y": table("y", [N, D]),
          "recs": table("recs", [P * RTILES, 4]), "dst1": table("dst1", [TILES * P]),
          "dst2": table("dst2", [RTILES * P]), "wrel": table("wrel", [2 * R * D, D]),
          "htype": table("htype", [HB * P], i32)}
    top = Scope(nc, "g")
    with top:
        g = Persistent(top)
        t1_filled = top.sem("t1_filled")
        mid = Scope(nc, "m")
        with mid:
            sort = Sort(mid)
            setup_phase(nc, g, sort, io, dr, t1_filled)
            edge_phase(nc, g, "e1", io["x"], dr["dst1"], g.srcidx, g.dcol, g.ddump, dr["t1"], D + 1, g.wst1,
                       dr["lin1"], g.wblk[:, 0, :], g.vec("b1"), SUPERS, sort=sort, table_filled=t1_filled,
                       fill=(dr["t2"], g.zero[:, 0:J * D]))
        norm_phase1(nc, g, dr["t1"], dr["lin1"], dr["h1"], dr["recs"])
        edge_phase(nc, g, "e2", dr["h1"], dr["dst1"], g.srcidx, g.dcol, g.ddump, dr["t2"], D, g.wst2,
                   dr["lin2"], g.wblk[:, 1, :], g.vec("b2"), SUPERS,
                   fill=(dr["t3"], g.biases[:, :, :].rearrange("p j d -> p (j d)")), x0=io["x"], xc_out=dr["xc"])
        norm_phase2(nc, g, dr["t2"], dr["lin2"], dr["xc"], dr["x1"], dr["recs"])
        late = Scope(nc, "late")
        with late:
            keep = late.sb("keep", [P, KEEP, J * D])
            reload_phase(nc, g, dr["recs"], dr["dst2"], dr["htype"])
            edge_phase(nc, g, "e3", dr["x1"], dr["dst2"], g.srcidx2, g.dcol2, g.ddump2, dr["t3"], D, None,
                       dr["lin3"], g.wblk[:, 2, :], g.vec("res_b"), RSUPERS, wcol=g.wcol2, wrel=dr["wrel"],
                       keep=keep)
            stats_phase(nc, g, dr["t3"], dr["lin3"], dr["y"], keep)
            final_phase(nc, g, dr["x1"], dr["y"], out, keep)


_INS = ["x", "src", "dst", "edge_type_64", "edge_weight1", "L0_gnn_W1l", "L0_gnn_b1l", "L0_gnn_W1r", "L0_gnn_g1",
        "L0_gnn_beta1", "L0_gnn_W2l", "L0_gnn_b2l", "L0_gnn_W2r", "L0_gnn_g2", "L0_gnn_beta2", "L1_gnn_basis",
        "L1_gnn_comp", "L1_gnn_bias", "L1_gnn_res_w", "L1_gnn_res_b", "L1_gnn_gamma", "L1_gnn_beta"]


def kernel(**inputs):
    import numpy as _np
    import concourse.bacc as _bacc
    from concourse import mybir as _mybir
    from concourse.bass_utils import run_bass_kernel_spmd as _run

    nc = _bacc.Bacc("TRN2", target_bir_lowering=False, num_devices=1)
    arrays, io = {}, {}
    for name in _INS:
        a = _np.ascontiguousarray(inputs[name])
        arrays[f"in_{name}_dram"] = a
        io[name] = nc.dram_tensor(f"in_{name}_dram", a.shape, _mybir.dt.from_np(a.dtype), kind="ExternalInput").ap()
    out = nc.dram_tensor("out_0_dram", (N, D), _mybir.dt.float32, kind="ExternalOutput").ap()
    gnn_kernel(nc, io, out)
    r = _run(nc, [arrays], core_ids=[0])
    return r.results[0]["out_0_dram"]
```
